# Optimizing a Trainium2 kernel written in Bass

```python
import numpy as np
import jax
import jax.numpy as jnp

def _softmax(x, axis=-1):
    return jax.nn.softmax(x, axis=axis)

def _gelu(x):
    return jax.nn.gelu(x, approximate=True)

def _silu(x):
    return jax.nn.silu(x)

def _sigmoid(x):
    return jax.nn.sigmoid(x)

def _layernorm(x, axis=-1, eps=1e-05):
    m = jnp.mean(x, axis=axis, keepdims=True)
    v = jnp.var(x, axis=axis, keepdims=True)
    return (x - m) / jnp.sqrt(v + eps)

def _scatter_add(tgt, idx, src, axis=0):
    return tgt.at[idx].add(src)

def _segment_sum(src, seg, n):
    return jax.ops.segment_sum(src, seg, n)
kernel_name = 'mk_flamingo_gated_d4_seqx_r8_8bc4fb'

def setup_inputs(seed: int=0):
    np.random.seed(seed)
    _w = jnp.asarray

    def _rec_inputs():
        import jax
        import jax.numpy as jnp
        _rk = jax.random.key(seed)
        x = 0.0003765 + 1 * jax.random.normal(jax.random.fold_in(_rk, 1), (16, 128, 256), jnp.float32)
        _lenS = 128 - jax.random.randint(jax.random.fold_in(_rk, 7), (16,), 0, max(1, 128 // 4) + 1, jnp.int32)
        _lenS2 = 128 - jax.random.randint(jax.random.fold_in(_rk, 8), (16,), 0, max(1, 128 // 4) + 1, jnp.int32)
        _ctx_2048P = jax.random.normal(jax.random.fold_in(_rk, 11), (16, 16, 256), jnp.float32)
        _ctx_2048c = jax.random.dirichlet(jax.random.fold_in(_rk, 511), 0.3 * jnp.ones((16,), jnp.float32), (16, 128))
        _ctx_2048t = jnp.einsum('bsk,bkd->bsd', _ctx_2048c, _ctx_2048P)
        _ctx_2048t = _ctx_2048t * jax.lax.rsqrt(jnp.mean(jnp.square(_ctx_2048t)) + 1e-12) * 0.953939
        ctx_2048 = -0.000292821 + 1.00034 * (_ctx_2048t + 0.3 * jax.random.normal(jax.random.fold_in(_rk, 611), (16, 128, 256), jnp.float32))
        _g = jax.random.normal(jax.random.fold_in(_rk, 9001), (2, 4), jnp.float32)
        _g = jnp.sign(_g) * jnp.maximum(jnp.abs(_g), 1.0) + (_g == 0) * 1.0
        g_xattn = _g[0]
        g_ffn = _g[1]
        return (x, ctx_2048, g_xattn, g_ffn)
    x, ctx_2048, g_xattn, g_ffn = _rec_inputs()

    def _L0_xattn_setup():
        import jax, jax.numpy as jnp
        import numpy as np
        key = jax.random.key(seed)
        k1, k2, k3, k4, k5 = jax.random.split(key, 5)
        B, D_MODEL, L = (2, 128, 256)
        HEAD_DIM = 8
        H = D_MODEL // HEAD_DIM
        return {'k': jax.random.normal(k1, (B, D_MODEL, L), dtype=jnp.float32), 'v': jax.random.normal(k2, (B, D_MODEL, L), dtype=jnp.float32), 'q': jax.random.normal(k3, (B, D_MODEL, L), dtype=jnp.float32), 'ssm_kernel': jax.random.normal(k4, (H, L), dtype=jnp.float32), 'D': jax.random.normal(k5, (H,), dtype=jnp.float32), 'head_dim': HEAD_DIM}
    _L0_xattn_all = _L0_xattn_setup()
    _L0_xattn_in = {k: v for k, v in _L0_xattn_all.items() if k in ('ssm_kernel', 'D')}
    del _L0_xattn_all

    def _L0_ffn_setup():
        import jax, jax.numpy as jnp
        import numpy as np
        from jax import lax
        B, S, H = (1, 256, 256)
        E, I, TOP_K = (64, 64, 8)
        SHARED_I = 64
        key = jax.random.key(seed)
        ks = jax.random.split(key, 8)
        sc = 0.02
        return {'hidden_states': jax.random.normal(ks[0], (B, S, H), jnp.float32), 'router_w': jax.random.normal(ks[1], (E, H), jnp.float32) * sc, 'gate_up_proj': jax.random.normal(ks[2], (E, 2 * I, H), jnp.float32) * sc, 'down_proj': jax.random.normal(ks[3], (E, H, I), jnp.float32) * sc, 'shared_gate_w': jax.random.normal(ks[4], (SHARED_I, H), jnp.float32) * sc, 'shared_up_w': jax.random.normal(ks[5], (SHARED_I, H), jnp.float32) * sc, 'shared_down_w': jax.random.normal(ks[6], (H, SHARED_I), jnp.float32) * sc, 'shared_expert_gate_w': jax.random.normal(ks[7], (1, H), jnp.float32) * sc}
    _L0_ffn_all = _L0_ffn_setup()
    _L0_ffn_in = {k: v for k, v in _L0_ffn_all.items() if k in ('router_w', 'gate_up_proj', 'down_proj', 'shared_gate_w', 'shared_up_w', 'shared_down_w', 'shared_expert_gate_w')}
    del _L0_ffn_all

    def _L1_xattn_setup():
        import jax, jax.numpy as jnp
        import numpy as np
        DIM = 256
        NHEADS = 32
        HEAD_DIM = DIM // NHEADS
        EPS = 1e-06

        def _rmsnorm(t):
            return t * jax.lax.rsqrt(jnp.mean(t * t, axis=-1, keepdims=True) + EPS)
        key = jax.random.key(seed)
        kx, kc, kq, kk, kv = jax.random.split(key, 5)
        x = jax.random.normal(kx, (2, 512, DIM), dtype=jnp.float32)
        context = jax.random.normal(kc, (2, 64, DIM), dtype=jnp.float32)
        std = 0.02
        Wq = jax.random.normal(kq, (DIM, DIM), dtype=jnp.float32) * std
        Wk = jax.random.normal(kk, (DIM, DIM), dtype=jnp.float32) * std
        Wv = jax.random.normal(kv, (DIM, DIM), dtype=jnp.float32) * std
        return {'x': x, 'context': context, 'Wq': Wq, 'Wk': Wk, 'Wv': Wv}
    _L1_xattn_all = _L1_xattn_setup()
    _L1_xattn_in = {k: v for k, v in _L1_xattn_all.items() if k in ('Wq', 'Wk', 'Wv')}
    del _L1_xattn_all

    def _L1_ffn_setup():
        import jax, jax.numpy as jnp
        import numpy as np
        B, S, H = (4, 256, 256)
        INTER = 512
        E = 8
        TOPK = 2
        SHARED_I = INTER * 2

        def moe_forward(hidden_states, router_w, w1, w2, w_gate, w_up, w_down):
            b, s, h = hidden_states.shape
            x = hidden_states.reshape(-1, h)
            T = x.shape[0]
            logits = x @ router_w
            top_logits, top_indices = jax.lax.top_k(logits, TOPK)
            scores = jax.nn.softmax(top_logits, axis=-1)
            flat_idx = top_indices.reshape(-1)
            sorted_pos = jnp.argsort(flat_idx, stable=True)
            permuted = x[sorted_pos // TOPK]
            expert_ids = flat_idx[sorted_pos]
            out = jnp.zeros((T * TOPK, h), x.dtype)
            for e in range(E):
                mask = (expert_ids == e)[:, None]
                f1 = permuted * mask @ w1[e]
                g, u = jnp.split(f1, 2, axis=-1)
                act = jax.nn.silu(g) * u
                out = out + jnp.where(mask, act @ w2[e], 0.0)
            unperm = jnp.zeros_like(out).at[sorted_pos].set(out)
            combined = (unperm.reshape(T, TOPK, h) * scores[..., None]).sum(axis=1)
            shared = jax.nn.silu(x @ w_gate) * (x @ w_up) @ w_down
            return (combined + shared).reshape(b, s, h)
        key = jax.random.key(seed)
        ks = jax.random.split(key, 7)
        s = 0.02
        return {'hidden_states': jax.random.normal(ks[0], (B, S, H), jnp.float32), 'router_w': jax.random.normal(ks[1], (H, E), jnp.float32) * s, 'w1': jax.random.normal(ks[2], (E, H, 2 * INTER), jnp.float32) * s, 'w2': jax.random.normal(ks[3], (E, INTER, H), jnp.float32) * s, 'w_gate': jax.random.normal(ks[4], (H, SHARED_I), jnp.float32) * s, 'w_up': jax.random.normal(ks[5], (H, SHARED_I), jnp.float32) * s, 'w_down': jax.random.normal(ks[6], (SHARED_I, H), jnp.float32) * s}
    _L1_ffn_all = _L1_ffn_setup()
    _L1_ffn_in = {k: v for k, v in _L1_ffn_all.items() if k in ('router_w', 'w1', 'w2', 'w_gate', 'w_up', 'w_down')}
    del _L1_ffn_all

    def _L2_xattn_setup():
        import jax, jax.numpy as jnp
        import numpy as np
        D_MODEL = 256
        NUM_HEADS = 16
        HEAD_DIM = D_MODEL // NUM_HEADS

        def _fq_sym(x, axis):
            s = jnp.max(jnp.abs(x), axis=axis, keepdims=True) / 127.0
            s = jnp.maximum(s, 1e-08)
            q = jnp.clip(jnp.round(x / s), -127.0, 127.0) * s
            return x + jax.lax.stop_gradient(q - x)

        def _fq_unsigned(x, axis):
            s = jnp.max(x, axis=axis, keepdims=True) / 255.0
            s = jnp.maximum(s, 1e-08)
            q = jnp.clip(jnp.round(x / s), 0.0, 255.0) * s
            return x + jax.lax.stop_gradient(q - x)
        key = jax.random.key(seed)
        ks = jax.random.split(key, 8)
        B, N, M, C = (2, 256, 64, D_MODEL)
        return {'x': jax.random.normal(ks[0], (B, N, C), jnp.float32), 'cond': jax.random.normal(ks[1], (B, M, C), jnp.float32), 'Wq': jax.random.normal(ks[2], (C, C), jnp.float32) * 0.02, 'bq': jnp.zeros((C,), jnp.float32), 'Wkv': jax.random.normal(ks[3], (C, 2 * C), jnp.float32) * 0.02, 'bkv': jnp.zeros((2 * C,), jnp.float32), 'Wp': jax.random.normal(ks[4], (C, C), jnp.float32) * 0.02, 'bp': jnp.zeros((C,), jnp.float32)}
    _L2_xattn_all = _L2_xattn_setup()
    _L2_xattn_in = {k: v for k, v in _L2_xattn_all.items() if k in ('Wq', 'bq', 'Wkv', 'bkv', 'Wp', 'bp')}
    del _L2_xattn_all

    def _L2_ffn_setup():
        import jax, jax.numpy as jnp
        import numpy as np
        BITS = 4
        SIGNED_MIN, SIGNED_MAX = (-2 ** (BITS - 1), 2 ** (BITS - 1) - 1)
        UNSIGNED_MIN, UNSIGNED_MAX = (0, 2 ** BITS - 1)
        INT32_MIN, INT32_MAX = (-2.0 ** 31, 2.0 ** 31 - 1)

        def fake_quant(x, scale, qmin, qmax):
            q = jnp.clip(jnp.round(x / scale), qmin, qmax) * scale
            return x + jax.lax.stop_gradient(q - x)

        def weight_scale(W):
            return jax.lax.stop_gradient(jnp.max(jnp.abs(W))) / SIGNED_MAX
        key = jax.random.key(seed)
        ks = jax.random.split(key, 5)
        B, S, D, F = (4, 256, 256, 1024)
        return {'x': jax.random.normal(ks[0], (B, S, D), dtype=jnp.float32), 'W1': jax.random.normal(ks[1], (F, D), dtype=jnp.float32) * 0.02, 'b1': jax.random.normal(ks[2], (F,), dtype=jnp.float32) * 0.02, 'W2': jax.random.normal(ks[3], (D, F), dtype=jnp.float32) * 0.02, 'b2': jax.random.normal(ks[4], (D,), dtype=jnp.float32) * 0.02, 's_act1': jnp.full((1,), 0.1, dtype=jnp.float32), 's_act2': jnp.full((1,), 0.1, dtype=jnp.float32)}
    _L2_ffn_all = _L2_ffn_setup()
    _L2_ffn_in = {k: v for k, v in _L2_ffn_all.items() if k in ('W1', 'b1', 'W2', 'b2', 's_act1', 's_act2')}
    del _L2_ffn_all

    def _L3_xattn_setup():
        import jax, jax.numpy as jnp
        import numpy as np
        HIDDEN = 256
        NUM_HEADS = 16
        HEAD_DIM = HIDDEN // NUM_HEADS
        CHUNK = 128
        SCALE = HEAD_DIM ** (-0.5)

        def _chunked_causal_attention(q, k, v):
            B, H, S, D = q.shape
            n_chunks = S // CHUNK
            kc = k.reshape(B, H, n_chunks, CHUNK, D).transpose(2, 0, 1, 3, 4)
            vc = v.reshape(B, H, n_chunks, CHUNK, D).transpose(2, 0, 1, 3, 4)
            j0s = jnp.arange(n_chunks) * CHUNK
            q_idx = jnp.arange(S)[:, None]
            k_off = jnp.arange(CHUNK)[None, :]
            out0 = jnp.zeros_like(q)
            m0 = jnp.full((B, H, S, 1), -jnp.inf, dtype=q.dtype)
            s0 = jnp.zeros((B, H, S, 1), dtype=q.dtype)

            def step(carry, inputs):
                out, m, s = carry
                kj, vj, j0 = inputs
                scores = jnp.einsum('bhqd,bhkd->bhqk', q, kj) * SCALE
                causal = j0 + k_off > q_idx
                scores = jnp.where(causal[None, None], -jnp.inf, scores)
                chunk_max = scores.max(axis=-1, keepdims=True)
                new_m = jnp.maximum(m, chunk_max)
                exp_old = jnp.exp(m - new_m)
                exp_c = jnp.exp(scores - new_m)
                new_s = s * exp_old + exp_c.sum(axis=-1, keepdims=True)
                out = out * (s / new_s) * exp_old + jnp.einsum('bhqk,bhkd->bhqd', exp_c / new_s, vj)
                return ((out, new_m, new_s), None)
            (out, _, _), _ = jax.lax.scan(step, (out0, m0, s0), (kc, vc, j0s))
            return out
        key = jax.random.key(seed)
        kq, kk, kv = jax.random.split(key, 3)
        B, S = (2, 512)
        return {'query': jax.random.normal(kq, (B, S, HIDDEN), dtype=jnp.float32), 'key': jax.random.normal(kk, (B, S, HIDDEN), dtype=jnp.float32), 'value': jax.random.normal(kv, (B, S, HIDDEN), dtype=jnp.float32)}
    _L3_xattn_all = _L3_xattn_setup()
    _L3_xattn_in = {k: v for k, v in _L3_xattn_all.items() if k in ()}
    del _L3_xattn_all

    def _L3_ffn_setup():
        import jax, jax.numpy as jnp
        import numpy as np
        import math
        GELU_C = math.sqrt(2.0 / math.pi)

        def activation_quant(x):
            scale = 127.0 / jnp.clip(jnp.max(jnp.abs(x), axis=-1, keepdims=True), 1e-05, None)
            y = jnp.clip(jnp.round(x * scale), -128, 127) / scale
            return x + jax.lax.stop_gradient(y - x)

        def weight_quant(w):
            scale = jnp.clip(jnp.mean(jnp.abs(w), axis=-1, keepdims=True), 1e-05, None)
            quant = jnp.clip(jnp.round(w / scale), -1, 1) * scale
            w_q = w + jax.lax.stop_gradient(quant - w)
            return (w_q / scale, scale.T)

        def new_gelu(x):
            return 0.5 * x * (1.0 + jnp.tanh(GELU_C * (x + 0.044715 * x * x * x)))

        def bitlinear(x, w):
            x_q = activation_quant(x)
            w_q, scale = weight_quant(w)
            out = jnp.einsum('bsd,hd->bsh', x_q, w_q)
            return out * scale
        key = jax.random.key(seed)
        k1, k2, k3 = jax.random.split(key, 3)
        dim, hidden = (256, 1024)
        B, S = (4, 256)
        x = jax.random.normal(k1, (B, S, dim), dtype=jnp.float32)
        lim1 = 1.0 / math.sqrt(dim)
        lim2 = 1.0 / math.sqrt(hidden)
        w1 = jax.random.uniform(k2, (hidden, dim), dtype=jnp.float32, minval=-lim1, maxval=lim1)
        w2 = jax.random.uniform(k3, (dim, hidden), dtype=jnp.float32, minval=-lim2, maxval=lim2)
        return {'x': x, 'w1': w1, 'w2': w2}
    _L3_ffn_all = _L3_ffn_setup()
    _L3_ffn_in = {k: v for k, v in _L3_ffn_all.items() if k in ('w1', 'w2')}
    del _L3_ffn_all
    return {'x': x, 'ctx_2048': ctx_2048, 'g_xattn': g_xattn, 'g_ffn': g_ffn, 'L0_xattn_ssm_kernel': _L0_xattn_in['ssm_kernel'], 'L0_xattn_D': _L0_xattn_in['D'], 'L0_ffn_router_w': _L0_ffn_in['router_w'], 'L0_ffn_gate_up_proj': _L0_ffn_in['gate_up_proj'], 'L0_ffn_down_proj': _L0_ffn_in['down_proj'], 'L0_ffn_shared_gate_w': _L0_ffn_in['shared_gate_w'], 'L0_ffn_shared_up_w': _L0_ffn_in['shared_up_w'], 'L0_ffn_shared_down_w': _L0_ffn_in['shared_down_w'], 'L0_ffn_shared_expert_gate_w': _L0_ffn_in['shared_expert_gate_w'], 'L1_xattn_Wq': _L1_xattn_in['Wq'], 'L1_xattn_Wk': _L1_xattn_in['Wk'], 'L1_xattn_Wv': _L1_xattn_in['Wv'], 'L1_ffn_router_w': _L1_ffn_in['router_w'], 'L1_ffn_w1': _L1_ffn_in['w1'], 'L1_ffn_w2': _L1_ffn_in['w2'], 'L1_ffn_w_gate': _L1_ffn_in['w_gate'], 'L1_ffn_w_up': _L1_ffn_in['w_up'], 'L1_ffn_w_down': _L1_ffn_in['w_down'], 'L2_xattn_Wq': _L2_xattn_in['Wq'], 'L2_xattn_bq': _L2_xattn_in['bq'], 'L2_xattn_Wkv': _L2_xattn_in['Wkv'], 'L2_xattn_bkv': _L2_xattn_in['bkv'], 'L2_xattn_Wp': _L2_xattn_in['Wp'], 'L2_xattn_bp': _L2_xattn_in['bp'], 'L2_ffn_W1': _L2_ffn_in['W1'], 'L2_ffn_b1': _L2_ffn_in['b1'], 'L2_ffn_W2': _L2_ffn_in['W2'], 'L2_ffn_b2': _L2_ffn_in['b2'], 'L2_ffn_s_act1': _L2_ffn_in['s_act1'], 'L2_ffn_s_act2': _L2_ffn_in['s_act2'], 'L3_ffn_w1': _L3_ffn_in['w1'], 'L3_ffn_w2': _L3_ffn_in['w2']}

def reference(x, ctx_2048, g_xattn, g_ffn, L0_xattn_ssm_kernel, L0_xattn_D, L0_ffn_router_w, L0_ffn_gate_up_proj, L0_ffn_down_proj, L0_ffn_shared_gate_w, L0_ffn_shared_up_w, L0_ffn_shared_down_w, L0_ffn_shared_expert_gate_w, L1_xattn_Wq, L1_xattn_Wk, L1_xattn_Wv, L1_ffn_router_w, L1_ffn_w1, L1_ffn_w2, L1_ffn_w_gate, L1_ffn_w_up, L1_ffn_w_down, L2_xattn_Wq, L2_xattn_bq, L2_xattn_Wkv, L2_xattn_bkv, L2_xattn_Wp, L2_xattn_bp, L2_ffn_W1, L2_ffn_b1, L2_ffn_W2, L2_ffn_b2, L2_ffn_s_act1, L2_ffn_s_act2, L3_ffn_w1, L3_ffn_w2):
    import jax
    import jax.numpy as jnp

    def _L0_xattn_ref(k, v, q, ssm_kernel, D, head_dim):
        import jax, jax.numpy as jnp
        import numpy as np
        B, HD, L = k.shape
        H = HD // head_dim
        fft_size = 2 * L
        k_ = k.reshape(B, H, head_dim, L)
        v_ = v.reshape(B, H, head_dim, L)
        q_ = q.reshape(B, H, head_dim, L)
        kv = jnp.einsum('bhil,bhjl->bijhl', k_, v_)
        kv_f = jnp.fft.rfft(kv, n=fft_size)
        kernel_f = jnp.fft.rfft(ssm_kernel, n=fft_size)
        y = jnp.fft.irfft(kv_f * kernel_f, n=fft_size)[..., :L]
        out = y + kv * D[None, None, None, :, None]
        out = jnp.einsum('bijhl,bhil->bjhl', out, q_)
        out = jnp.transpose(out, (0, 2, 1, 3)).reshape(B, H * head_dim, L)
        return out.astype(k.dtype)

    def _L0_ffn_ref(hidden_states, router_w, gate_up_proj, down_proj, shared_gate_w, shared_up_w, shared_down_w, shared_expert_gate_w):
        import jax, jax.numpy as jnp
        import numpy as np
        from jax import lax
        B, S, H = (1, 256, 256)
        E, I, TOP_K = (64, 64, 8)
        SHARED_I = 64
        b, s, h_dim = hidden_states.shape
        h = hidden_states.reshape(-1, h_dim)
        T = h.shape[0]
        shared = jnp.dot(jax.nn.silu(jnp.dot(h, shared_gate_w.T)) * jnp.dot(h, shared_up_w.T), shared_down_w.T)
        shared = jax.nn.sigmoid(jnp.dot(h, shared_expert_gate_w.T)) * shared
        logits = jnp.dot(h, router_w.T)
        probs = jax.nn.softmax(logits.astype(jnp.float32), axis=-1)
        top_vals, top_idx = lax.top_k(probs, TOP_K)
        top_vals = top_vals / jnp.sum(top_vals, axis=-1, keepdims=True)
        top_vals = top_vals.astype(h.dtype)
        comb = jnp.zeros((T, E), h.dtype).at[jnp.arange(T)[:, None], top_idx].add(top_vals)

        def body(acc, xs):
            wgu, wd, w_e = xs
            g, u = jnp.split(jnp.dot(h, wgu.T), 2, axis=-1)
            eo = jnp.dot(jax.nn.silu(g) * u, wd.T)
            return (acc + eo * w_e[:, None], None)
        expert_out, _ = lax.scan(body, jnp.zeros_like(h), (gate_up_proj, down_proj, comb.T))
        return (expert_out + shared).reshape(b, s, h_dim)

    def _L1_xattn_ref(x, context, Wq, Wk, Wv):
        import jax, jax.numpy as jnp
        import numpy as np
        DIM = 256
        NHEADS = 32
        HEAD_DIM = DIM // NHEADS
        EPS = 1e-06

        def _rmsnorm(t):
            return t * jax.lax.rsqrt(jnp.mean(t * t, axis=-1, keepdims=True) + EPS)
        b, n, _ = x.shape
        m = context.shape[1]
        q = x @ Wq.T
        k_raw = context @ Wk.T
        v_raw = context @ Wv.T
        q = q.reshape(b, n, NHEADS, HEAD_DIM).transpose(0, 2, 1, 3)
        kv = jnp.concatenate([k_raw, v_raw], axis=-1)
        kv = kv.reshape(b, m, NHEADS, HEAD_DIM, 2)
        k = kv[..., 0].transpose(0, 2, 1, 3)
        v = kv[..., 1].transpose(0, 2, 1, 3)
        q = _rmsnorm(q)
        k = _rmsnorm(k)
        scale = HEAD_DIM ** (-0.5)
        scores = jnp.einsum('bhnd,bhmd->bhnm', q, k) * scale
        attn = jax.nn.softmax(scores, axis=-1)
        out = jnp.einsum('bhnm,bhmd->bhnd', attn, v)
        return out.transpose(0, 2, 1, 3).reshape(b, n, NHEADS * HEAD_DIM)

    def _L1_ffn_ref(hidden_states, router_w, w1, w2, w_gate, w_up, w_down):
        import jax, jax.numpy as jnp
        import numpy as np
        B, S, H = (4, 256, 256)
        INTER = 512
        E = 8
        TOPK = 2
        SHARED_I = INTER * 2

        def moe_forward(hidden_states, router_w, w1, w2, w_gate, w_up, w_down):
            b, s, h = hidden_states.shape
            x = hidden_states.reshape(-1, h)
            T = x.shape[0]
            logits = x @ router_w
            top_logits, top_indices = jax.lax.top_k(logits, TOPK)
            scores = jax.nn.softmax(top_logits, axis=-1)
            flat_idx = top_indices.reshape(-1)
            sorted_pos = jnp.argsort(flat_idx, stable=True)
            permuted = x[sorted_pos // TOPK]
            expert_ids = flat_idx[sorted_pos]
            out = jnp.zeros((T * TOPK, h), x.dtype)
            for e in range(E):
                mask = (expert_ids == e)[:, None]
                f1 = permuted * mask @ w1[e]
                g, u = jnp.split(f1, 2, axis=-1)
                act = jax.nn.silu(g) * u
                out = out + jnp.where(mask, act @ w2[e], 0.0)
            unperm = jnp.zeros_like(out).at[sorted_pos].set(out)
            combined = (unperm.reshape(T, TOPK, h) * scores[..., None]).sum(axis=1)
            shared = jax.nn.silu(x @ w_gate) * (x @ w_up) @ w_down
            return (combined + shared).reshape(b, s, h)
        return moe_forward(hidden_states, router_w, w1, w2, w_gate, w_up, w_down)

    def _L2_xattn_ref(x, cond, Wq, bq, Wkv, bkv, Wp, bp):
        import jax, jax.numpy as jnp
        import numpy as np
        D_MODEL = 256
        NUM_HEADS = 16
        HEAD_DIM = D_MODEL // NUM_HEADS

        def _fq_sym(x, axis):
            s = jnp.max(jnp.abs(x), axis=axis, keepdims=True) / 127.0
            s = jnp.maximum(s, 1e-08)
            q = jnp.clip(jnp.round(x / s), -127.0, 127.0) * s
            return x + jax.lax.stop_gradient(q - x)

        def _fq_unsigned(x, axis):
            s = jnp.max(x, axis=axis, keepdims=True) / 255.0
            s = jnp.maximum(s, 1e-08)
            q = jnp.clip(jnp.round(x / s), 0.0, 255.0) * s
            return x + jax.lax.stop_gradient(q - x)
        B, N, C = x.shape
        H, hd = (NUM_HEADS, HEAD_DIM)
        q = (x @ Wq + bq).reshape(1, B * N, H, hd)
        kv = (cond @ Wkv + bkv).reshape(1, -1, 2, H, hd)
        k, v = (kv[:, :, 0], kv[:, :, 1])
        scale = 1.0 / np.sqrt(hd).astype(np.float32)
        q = jnp.transpose(q * scale, (0, 2, 1, 3))
        k = jnp.transpose(k, (0, 2, 1, 3))
        v = jnp.transpose(v, (0, 2, 1, 3))
        q = _fq_sym(q, axis=-1)
        k = _fq_sym(k, axis=-1)
        v = _fq_sym(v, axis=2)
        attn = jnp.einsum('bhqd,bhkd->bhqk', q, k)
        attn = jax.nn.softmax(attn.astype(jnp.float32), axis=-1)
        attn = _fq_unsigned(attn, axis=-1)
        out = jnp.einsum('bhqk,bhkd->bhqd', attn, v)
        out = jnp.transpose(out, (0, 2, 1, 3)).reshape(B, N, C)
        return out @ Wp + bp

    def _L2_ffn_ref(x, W1, b1, W2, b2, s_act1, s_act2):
        import jax, jax.numpy as jnp
        import numpy as np
        BITS = 4
        SIGNED_MIN, SIGNED_MAX = (-2 ** (BITS - 1), 2 ** (BITS - 1) - 1)
        UNSIGNED_MIN, UNSIGNED_MAX = (0, 2 ** BITS - 1)
        INT32_MIN, INT32_MAX = (-2.0 ** 31, 2.0 ** 31 - 1)

        def fake_quant(x, scale, qmin, qmax):
            q = jnp.clip(jnp.round(x / scale), qmin, qmax) * scale
            return x + jax.lax.stop_gradient(q - x)

        def weight_scale(W):
            return jax.lax.stop_gradient(jnp.max(jnp.abs(W))) / SIGNED_MAX
        s1 = s_act1[0]
        s2 = s_act2[0]
        x_q = fake_quant(x, s1, SIGNED_MIN, SIGNED_MAX)
        sw1 = weight_scale(W1)
        W1_q = fake_quant(W1, sw1, SIGNED_MIN, SIGNED_MAX)
        b1_q = fake_quant(b1, s1 * sw1, INT32_MIN, INT32_MAX)
        h = jnp.einsum('bsd,fd->bsf', x_q, W1_q) + b1_q
        h_q = fake_quant(jax.nn.relu(h), s2, UNSIGNED_MIN, UNSIGNED_MAX)
        sw2 = weight_scale(W2)
        W2_q = fake_quant(W2, sw2, SIGNED_MIN, SIGNED_MAX)
        b2_q = fake_quant(b2, s2 * sw2, INT32_MIN, INT32_MAX)
        out = jnp.einsum('bsf,df->bsd', h_q, W2_q) + b2_q
        return out

    def _L3_xattn_ref(query, key, value):
        import jax, jax.numpy as jnp
        import numpy as np
        HIDDEN = 256
        NUM_HEADS = 16
        HEAD_DIM = HIDDEN // NUM_HEADS
        CHUNK = 128
        SCALE = HEAD_DIM ** (-0.5)

        def _chunked_causal_attention(q, k, v):
            B, H, S, D = q.shape
            n_chunks = S // CHUNK
            kc = k.reshape(B, H, n_chunks, CHUNK, D).transpose(2, 0, 1, 3, 4)
            vc = v.reshape(B, H, n_chunks, CHUNK, D).transpose(2, 0, 1, 3, 4)
            j0s = jnp.arange(n_chunks) * CHUNK
            q_idx = jnp.arange(S)[:, None]
            k_off = jnp.arange(CHUNK)[None, :]
            out0 = jnp.zeros_like(q)
            m0 = jnp.full((B, H, S, 1), -jnp.inf, dtype=q.dtype)
            s0 = jnp.zeros((B, H, S, 1), dtype=q.dtype)

            def step(carry, inputs):
                out, m, s = carry
                kj, vj, j0 = inputs
                scores = jnp.einsum('bhqd,bhkd->bhqk', q, kj) * SCALE
                causal = j0 + k_off > q_idx
                scores = jnp.where(causal[None, None], -jnp.inf, scores)
                chunk_max = scores.max(axis=-1, keepdims=True)
                new_m = jnp.maximum(m, chunk_max)
                exp_old = jnp.exp(m - new_m)
                exp_c = jnp.exp(scores - new_m)
                new_s = s * exp_old + exp_c.sum(axis=-1, keepdims=True)
                out = out * (s / new_s) * exp_old + jnp.einsum('bhqk,bhkd->bhqd', exp_c / new_s, vj)
                return ((out, new_m, new_s), None)
            (out, _, _), _ = jax.lax.scan(step, (out0, m0, s0), (kc, vc, j0s))
            return out
        B, S, _ = query.shape
        q = query.reshape(B, S, NUM_HEADS, HEAD_DIM).transpose(0, 2, 1, 3)
        k = key.reshape(B, S, NUM_HEADS, HEAD_DIM).transpose(0, 2, 1, 3)
        v = value.reshape(B, S, NUM_HEADS, HEAD_DIM).transpose(0, 2, 1, 3)
        out = _chunked_causal_attention(q, k, v)
        return out.transpose(0, 2, 1, 3).reshape(B, S, HIDDEN)

    def _L3_ffn_ref(x, w1, w2):
        import jax, jax.numpy as jnp
        import numpy as np
        import math
        GELU_C = math.sqrt(2.0 / math.pi)

        def activation_quant(x):
            scale = 127.0 / jnp.clip(jnp.max(jnp.abs(x), axis=-1, keepdims=True), 1e-05, None)
            y = jnp.clip(jnp.round(x * scale), -128, 127) / scale
            return x + jax.lax.stop_gradient(y - x)

        def weight_quant(w):
            scale = jnp.clip(jnp.mean(jnp.abs(w), axis=-1, keepdims=True), 1e-05, None)
            quant = jnp.clip(jnp.round(w / scale), -1, 1) * scale
            w_q = w + jax.lax.stop_gradient(quant - w)
            return (w_q / scale, scale.T)

        def new_gelu(x):
            return 0.5 * x * (1.0 + jnp.tanh(GELU_C * (x + 0.044715 * x * x * x)))

        def bitlinear(x, w):
            x_q = activation_quant(x)
            w_q, scale = weight_quant(w)
            out = jnp.einsum('bsd,hd->bsh', x_q, w_q)
            return out * scale
        h = bitlinear(x, w1)
        h = new_gelu(h)
        return bitlinear(h, w2)
    x = x + jnp.tanh(g_xattn[0]) * _L0_xattn_ref(ctx_2048, ctx_2048, _layernorm(x, axis=-1), L0_xattn_ssm_kernel, L0_xattn_D, 8)
    x = x + jnp.tanh(g_ffn[0]) * _L0_ffn_ref(_layernorm(x, axis=-1), L0_ffn_router_w, L0_ffn_gate_up_proj, L0_ffn_down_proj, L0_ffn_shared_gate_w, L0_ffn_shared_up_w, L0_ffn_shared_down_w, L0_ffn_shared_expert_gate_w)
    x = x + jnp.tanh(g_xattn[1]) * _L1_xattn_ref(_layernorm(x, axis=-1), ctx_2048, L1_xattn_Wq, L1_xattn_Wk, L1_xattn_Wv)
    x = x + jnp.tanh(g_ffn[1]) * _L1_ffn_ref(_layernorm(x, axis=-1), L1_ffn_router_w, L1_ffn_w1, L1_ffn_w2, L1_ffn_w_gate, L1_ffn_w_up, L1_ffn_w_down)
    x = x + jnp.tanh(g_xattn[2]) * _L2_xattn_ref(_layernorm(x, axis=-1), ctx_2048, L2_xattn_Wq, L2_xattn_bq, L2_xattn_Wkv, L2_xattn_bkv, L2_xattn_Wp, L2_xattn_bp)
    x = x + jnp.tanh(g_ffn[2]) * _L2_ffn_ref(_layernorm(x, axis=-1), L2_ffn_W1, L2_ffn_b1, L2_ffn_W2, L2_ffn_b2, L2_ffn_s_act1, L2_ffn_s_act2)
    x = x + jnp.tanh(g_xattn[3]) * _L3_xattn_ref(_layernorm(x, axis=-1), ctx_2048, ctx_2048)
    x = x + jnp.tanh(g_ffn[3]) * _L3_ffn_ref(_layernorm(x, axis=-1), L3_ffn_w1, L3_ffn_w2)
    return x

_drawn_inputs = setup_inputs


def setup_inputs(seed=0):
    import zlib

    import numpy as np

    out = dict(_drawn_inputs(seed))
    spreads = {'L2_xattn_bq': (0.0, 0.8), 'L2_xattn_bkv': (0.0, 0.8), 'L2_xattn_bp': (0.0, 2.0)}
    factors = {'g_ffn': 8.0,
     'L0_ffn_router_w': 8.0,
     'L0_ffn_gate_up_proj': 8.0,
     'L0_ffn_down_proj': 8.0,
     'L0_ffn_shared_gate_w': 8.0,
     'L0_ffn_shared_up_w': 8.0,
     'L0_ffn_shared_down_w': 8.0,
     'L0_ffn_shared_expert_gate_w': 8.0,
     'L1_xattn_Wq': 8.0,
     'L1_xattn_Wk': 8.0,
     'L1_xattn_Wv': 8.0,
     'L1_ffn_router_w': 8.0,
     'L1_ffn_w1': 8.0,
     'L1_ffn_w2': 8.0,
     'L1_ffn_w_gate': 8.0,
     'L1_ffn_w_up': 8.0,
     'L1_ffn_w_down': 8.0,
     'L2_xattn_Wq': 8.0,
     'L2_xattn_Wkv': 8.0,
     'L2_xattn_Wp': 8.0,
     'L2_ffn_W1': 8.0,
     'L2_ffn_b1': 36.537,
     'L2_ffn_W2': 8.0,
     'L2_ffn_b2': 64.0,
     'L3_ffn_w1': 8.0,
     'L3_ffn_w2': 8.0}
    for name, (base, spread) in spreads.items():
        noise = np.random.default_rng([zlib.crc32(name.encode()), seed]).standard_normal(out[name].shape)
        drawn = base * np.exp(spread * noise) if base else spread * noise
        out[name] = jnp.asarray(drawn.astype(out[name].dtype))
    for name, factor in factors.items():
        out[name] = (out[name] * factor).astype(out[name].dtype)
    return out
```

```python
from contextlib import ExitStack, contextmanager
import numpy as np
import concourse.bass as bass
from concourse import mybir


F32 = mybir.dt.float32
F16 = mybir.dt.float16
BF16 = mybir.dt.bfloat16
ALU = mybir.AluOpType
ACT = mybir.ActivationFunctionType
AXX = mybir.AxisListType.X

P = 128
NB = 16
D = 256
KT = D // P
T = NB * P
EPS = 1e-5


class Shared:
    pass


def make_shared(nc, ctx, x, g_xattn, g_ffn):
    sh = Shared()

    def sb(n, shape, dt=F32):
        return ctx.enter_context(nc.sbuf_tensor(n, shape, dt))

    sh.X = sb("X", [P, NB, D])
    sh.H = sb("H", [P, NB, D])
    sh.gates = sb("gates", [P, 8])
    graw = sb("graw", [P, 8])
    sh.eps = sb("eps", [P, 1])
    sh.ident = sb("ident", [P, P])
    sh.ident16 = sb("ident16", [P, P], BF16)
    sh.identh = sb("identh", [P, P], F16)
    sh.ln_stats = sb("ln_stats", [P, NB, 6])
    sh.ln_mv = sb("ln_mv", [P, NB, 2])
    sh.ln_std = sb("ln_std", [P, NB])
    sh.ln_rstd = sb("ln_rstd", [P, NB])
    s_load = nc.alloc_semaphore(name="setup_load")
    s_ident = nc.alloc_semaphore(name="setup_ident")
    s_set = nc.alloc_semaphore(name="setup_set")
    with nc.Block() as block:
        @block.sync
        def _(sp):
            sp.dma_start(sh.X[:, :, :], x.rearrange("b p d -> p b d")).then_inc(s_load, 16)
            sp.dma_start(graw[:, 0:4], g_xattn.partition_broadcast(P)).then_inc(s_load, 16)
            sp.dma_start(graw[:, 4:8], g_ffn.partition_broadcast(P)).then_inc(s_load, 16)
            sp.wait_ge(s_load, 48)

        @block.gpsimd
        def _(pool):
            nc.gpsimd.memset(sh.eps[:, :], EPS).then_inc(s_set, 1)
            nc.gpsimd.memset(sh.ident[:, :], 0.0).then_inc(s_set, 1)
            pool.wait_ge(s_set, 2)
            nc.gpsimd.affine_select(out=sh.ident[:, :], in_=sh.ident[:, :], compare_op=ALU.not_equal, fill=1.0,
                                    base=0, pattern=[[-1, P]], channel_multiplier=1).then_inc(s_ident, 1)

        @block.vector
        def _(dve):
            dve.wait_ge(s_ident, 1)
            nc.vector.tensor_copy(sh.ident16[:, :], sh.ident[:, :])
            nc.vector.tensor_copy(sh.identh[:, :], sh.ident[:, :])

        @block.scalar
        def _(act):
            act.wait_ge(s_load, 48)
            nc.scalar.activation(sh.gates[:, 0::2], graw[:, 0:4], ACT.Tanh)
            nc.scalar.activation(sh.gates[:, 1::2], graw[:, 4:8], ACT.Tanh)
    return sh


def layernorm(nc, ctx, sh, name):
    s_stats = nc.alloc_semaphore(name=f"{name}_stats")
    s_mv = nc.alloc_semaphore(name=f"{name}_mv")
    s_std = nc.alloc_semaphore(name=f"{name}_std")
    s_rstd = nc.alloc_semaphore(name=f"{name}_rstd")
    with nc.Block() as block:
        @block.vector
        def _(dve):
            with dve.Fori(0, NB) as t:
                nc.vector.bn_stats(sh.ln_stats[:, bass.ds(t, 1), :], sh.X[:, bass.ds(t, 1), :]).then_inc(s_stats, 1)
            dve.wait_ge(s_stats, NB)
            for t in range(NB):
                nc.vector.bn_aggr(sh.ln_mv[:, t, :], sh.ln_stats[:, t, :]).then_inc(s_mv, 1)
            dve.wait_ge(s_std, 1)
            nc.vector.reciprocal(sh.ln_rstd[:, :], sh.ln_std[:, :]).then_inc(s_rstd, 1)
            dve.wait_ge(s_rstd, 1)
            with dve.Fori(0, NB) as t:
                nc.vector.tensor_scalar(sh.H[:, bass.ds(t, 1), :], sh.X[:, bass.ds(t, 1), :],
                                        sh.ln_mv[:, bass.ds(t, 1), 0], sh.ln_rstd[:, bass.ds(t, 1)],
                                        ALU.subtract, ALU.mult)

        @block.scalar
        def _(act):
            act.wait_ge(s_mv, NB)
            nc.scalar.activation(sh.ln_std[:, :], sh.ln_mv[:, :, 1], ACT.Sqrt, bias=sh.eps[:, 0:1]).then_inc(s_std, 1)


def long_convolution(nc, sh, sems, ctx_flip, ctxT_flip, ssm_pad, ssm_D):
    NH, HD = 16, 8
    W = D + P
    HG = 2
    NG = NH // HG
    R = 3 * HD
    with ExitStack() as ctx:
        def sb(n, shape, dt=F32):
            return ctx.enter_context(nc.sbuf_tensor("conv_" + n, shape, dt))

        def sem(n):
            return nc.alloc_semaphore(name="conv_" + n)

        toep = sb("toep", [P, NH, W])
        anti = sb("anti", [P, P])
        dvals = sb("dvals", [P, NH])
        kf = sb("kf", [P, NB, D])
        vt = sb("vt", [P, NB, KT, P])
        parts = sb("parts", [P, 4, NB, D], F16)
        qst = sb("qst", [R, 2, NH, D], F16)
        kst = sb("kst", [R, 2, NH, D], F16)
        vpad = sb("vpad", [P, 2, KT, NH, P])
        A = sb("A", [P, 2, HG, W])
        rows = nc.dram_tensor("conv_rows", [4, NB, P, D], F16, kind="Internal").ap()
        s_rows = sem("rows")
        gate = sh.gates[:, 0:1]
        S = ctx.enter_context(nc.psum_tensor("conv_S", [P, 2, HG, 512], F32))
        Y = ctx.enter_context(nc.psum_tensor("conv_Y", [P, 2, 512], F32))
        s_load, s_zero, s_anti, s_toep = sem("load"), sem("zero"), sem("anti"), sem("toep")
        s_hi, s_lo = sem("hi"), sem("lo")
        s_stack = [sem("stack0"), sem("stack1")]
        s_vpad = sem("vpad")
        s_S, s_A, s_Y, s_res = sem("S"), sem("A"), sem("Y"), sem("res")
        with nc.Block() as block:
            @block.sync
            def _(sp):
                sp.dma_start(kf[:, :, :], ctx_flip.rearrange("b p d -> p b d")).then_inc(s_load, 16)
                sp.dma_start(vt[:, :, :, :], ctxT_flip).then_inc(s_load, 16)
                for h in range(NH):
                    sp.dma_start(toep[:, h, 0:D], bass.AP(ssm_pad.tensor, h * (P - 1 + D), [[1, P], [1, D]])).then_inc(s_load, 16)
                sp.dma_start(dvals[:, :], ssm_D.partition_broadcast(P)).then_inc(s_load, 16)
                sp.wait_ge(s_hi, 2)
                sp.wait_ge(s_lo, 2)
                for part in range(4):
                    sp.dma_start(rows[part, :, :, :].rearrange("b p l -> p b l"), parts[:, part, :, :]).then_inc(s_rows, 16)
                sp.wait_ge(s_rows, 64)
                with sp.Fori(0, NB // 2) as pair:
                    for par in range(2):
                        b = pair * 2 + par
                        sp.wait_ge(s_S, b * NG + NG)
                        for stack, order in ((qst, (0, 0, 1)), (kst, (2, 3, 2))):
                            for r, part in enumerate(order):
                                sp.dma_start(stack[r * HD:(r + 1) * HD, par, :, :],
                                             rows[part, b, :, :].rearrange("(h i) l -> i h l", i=HD)).then_inc(s_stack[par], 16)

            @block.scalar
            def _(act):
                nc.scalar.activation(parts[:, 0, :, :], sh.H[:, :, :], ACT.Copy).then_inc(s_hi, 1)
                act.wait_ge(s_load, 16 * (NH + 3))
                nc.scalar.activation(parts[:, 2, :, :], kf[:, :, :], ACT.Copy).then_inc(s_hi, 1)

            @block.gpsimd
            def _(pool):
                nc.gpsimd.memset(vpad[:, :, :, :, :], 0.0).then_inc(s_zero, 1)
                nc.gpsimd.memset(anti[:, :], 0.0).then_inc(s_zero, 1)
                pool.wait_ge(s_zero, 2)
                nc.gpsimd.affine_select(out=anti[:, :], in_=anti[:, :], compare_op=ALU.not_equal, fill=1.0,
                                        base=-(P - 1), pattern=[[1, P]], channel_multiplier=1).then_inc(s_anti, 1)
                pool.wait_ge(s_load, 16 * (NH + 3))
                with pool.Fori(0, NB // 2) as pair:
                    for par in range(2):
                        b = pair * 2 + par
                        pool.wait_ge(s_Y, b * NG + NG)
                        for mt in range(KT):
                            flat = vpad[:, par, mt, :, :].rearrange("p h c -> p (h c)")
                            dst = bass.AP(flat.tensor, flat.offset, [flat.ap[0], [P + HD, NH], [1, HD]])
                            nc.gpsimd.tensor_copy(dst, vt[:, b, mt, :].rearrange("p (h j) -> p h j", j=HD)).then_inc(s_vpad, 1)

            @block.vector
            def _(dve):
                dve.sem_inc(s_A, 2)
                dve.sem_inc(s_res, 2)
                dve.wait_ge(s_hi, 1)
                nc.vector.tensor_tensor(parts[:, 1, :, :], sh.H[:, :, :], parts[:, 0, :, :], ALU.subtract).then_inc(s_lo, 1)
                dve.wait_ge(s_hi, 2)
                nc.vector.tensor_tensor(parts[:, 3, :, :], kf[:, :, :], parts[:, 2, :, :], ALU.subtract).then_inc(s_lo, 1)
                dve.wait_ge(s_load, 16 * (NH + 3))
                dve.wait_ge(s_anti, 1)
                for h in range(NH):
                    nc.vector.scalar_tensor_tensor(out=toep[:, h, 0:P], in0=anti[:, :], scalar=dvals[:, h:h + 1],
                                                   in1=toep[:, h, 0:P], op0=ALU.mult, op1=ALU.add).then_inc(s_toep, 1)
                dve.wait_ge(s_toep, NH)
                nc.vector.tensor_copy(toep[:, :, D:W], toep[:, :, 0:P]).then_inc(s_toep, 1)
                dve.wait_ge(s_toep, NH + 1)
                with dve.Fori(0, NB // 2) as pair:
                    for par in range(2):
                        b = pair * 2 + par
                        for g in range(NG):
                            k = b * NG + g
                            dve.wait_ge(s_S, k + 2 * NG + 1)
                            dve.wait_ge(s_Y, k + 2 * NG - 1)
                            nc.vector.tensor_tensor(A[:, g % 2, :, :], S[:, g % 2, :, 0:W],
                                                    toep[:, g * HG:(g + 1) * HG, :], ALU.mult).then_inc(s_A, 1)
                        dve.wait_ge(s_Y, b * NG + 3 * NG)
                        nc.vector.scalar_tensor_tensor(out=sh.X[:, b, :], in0=Y[:, par, 0:D], scalar=gate,
                                                       in1=sh.X[:, b, :], op0=ALU.mult, op1=ALU.add).then_inc(s_res, 1)

            @block.tensor
            def _(pe):
                pe.sem_inc(s_S, 2 * NG)
                pe.sem_inc(s_Y, 2 * NG)

                def scores(b, par, g):
                    k = b * NG + g
                    pe.wait_ge(s_A, k + 1)
                    for i in range(HG):
                        h = g * HG + i
                        nc.tensor.matmul(S[:, g % 2, i, 0:D], kst[:, par, h, 0:P], qst[:, par, h, :], start=True, stop=True)
                        last = nc.tensor.matmul(S[:, g % 2, i, D:W], kst[:, par, h, P:D], qst[:, par, h, P:D], start=True, stop=True)
                    last.then_inc(s_S, 1)

                def values(b, par, g):
                    pe.wait_ge(s_A, b * NG + g + 3)
                    for i in range(HG):
                        h = g * HG + i
                        nc.tensor.matmul(Y[:, par, 0:D], vpad[:, par, 0, h, :], A[:, g % 2, i, 0:D], start=h == 0, stop=False)
                        last = nc.tensor.matmul(Y[:, par, P:D], vpad[:, par, 1, h, :], A[:, g % 2, i, D:W], start=False, stop=h == NH - 1)
                    last.then_inc(s_Y, 1)

                with pe.Fori(0, NB // 2) as pair:
                    for par in range(2):
                        b = pair * 2 + par
                        pe.wait_ge(s_stack[par], pair * 96 + 96)
                        scores(b, par, 0)
                        pe.wait_ge(s_vpad, b * 2 + 2)
                        pe.wait_ge(s_res, b + 1)
                        for g in range(NG):
                            if g + 1 < NG:
                                scores(b, par, g + 1)
                            values(b, par, g)


def copy_indexed(nc, out, in_):
    return nc.vector.tensor_scalar(out, in_, 1.0, None, ALU.mult)


def split_transpose(nc, sems, sh, name):
    s_hi, s_lo, s_T, s_even, s_odd = (nc.alloc_semaphore(name=f"{name}_{n}") for n in ("hi", "lo", "T", "even", "odd"))
    with ExitStack() as ctx:
        parts = ctx.enter_context(nc.sbuf_tensor(name + "_parts", [P, 2, NB, D], F16))
        TP = ctx.enter_context(nc.psum_tensor(name + "_TP", [P, 2, 2, KT, P], F32))
        with nc.Block() as block:
            @block.scalar
            def _(act):
                act.sem_inc(s_even, 1)
                nc.scalar.activation(parts[:, 0, :, :], sh.H[:, :, :], ACT.Copy).then_inc(s_hi, 1)
                with act.Fori(0, NB // 2) as pair:
                    act.wait_ge(s_T, pair * 2 + 1)
                    nc.scalar.activation(sh.hT[:, :, :, bass.ds(pair * 2 * P, P)], TP[:, 0, :, :, :], ACT.Copy).then_inc(s_even, 1)

            @block.vector
            def _(dve):
                dve.sem_inc(s_odd, 1)
                dve.wait_ge(s_hi, 1)
                nc.vector.tensor_tensor(parts[:, 1, :, :], sh.H[:, :, :], parts[:, 0, :, :], ALU.subtract).then_inc(s_lo, 1)
                with dve.Fori(0, NB // 2) as pair:
                    dve.wait_ge(s_T, pair * 2 + 2)
                    copy_indexed(nc, sh.hT[:, :, :, bass.ds((pair * 2 + 1) * P, P)], TP[:, 1, :, :, :]).then_inc(s_odd, 1)

            @block.tensor
            def _(pe):
                pe.wait_ge(s_lo, 1)
                with pe.Fori(0, NB // 2) as pair:
                    for par in range(2):
                        t = pair * 2 + par
                        pe.wait_ge((s_even, s_odd)[par], pair + 1)
                        for part in range(2):
                            for k in range(KT):
                                last = nc.tensor.matmul(TP[:, par, part, k, :], parts[:, part, t, k * P:(k + 1) * P],
                                                        sh.identh[:, :], start=True, stop=True)
                        last.then_inc(s_T, 1)


PRODUCTS = ((0, 0), (0, 1), (1, 0))


class MoE:

    def __init__(self, experts, top, tiles, rows, chunk):
        self.experts, self.top, self.tiles, self.rows, self.chunk = experts, top, tiles, rows, chunk


MOE0 = MoE(64, 8, 33, 66, 3)
MOE1 = MoE(8, 2, 40, 80, 4)
TW = 6 * P


def load_expert_weights(nc, sems, sh, m, w, name):
    C = m.chunk * TW
    n = m.tiles // m.chunk
    s_load = [nc.alloc_semaphore(name=f"{name}_load{i}") for i in range(2)]
    s_hi, s_lo = (nc.alloc_semaphore(name=f"{name}_{x}") for x in ("hi", "lo"))
    with ExitStack() as ctx:
        stage = ctx.enter_context(nc.sbuf_tensor(name + "_stage", [P, 2, C], F32))
        with nc.Block() as block:
            @block.sync
            def _(sp):
                for i in range(n):
                    if i >= 2:
                        sp.wait_ge(s_lo, i - 1)
                    sp.dma_start(stage[:, i % 2, :], w[:, i * C:(i + 1) * C]).then_inc(s_load[i % 2], 16)

            @block.scalar
            def _(act):
                for i in range(n):
                    act.wait_ge(s_load[i % 2], 16 * (i // 2 + 1))
                    nc.scalar.activation(sh.W[:, 0, i * C:(i + 1) * C], stage[:, i % 2, :], ACT.Copy).then_inc(s_hi, 1)

            @block.vector
            def _(dve):
                for i in range(n):
                    dve.wait_ge(s_hi, i + 1)
                    nc.vector.tensor_tensor(sh.W[:, 1, i * C:(i + 1) * C], stage[:, i % 2, :],
                                            sh.W[:, 0, i * C:(i + 1) * C], ALU.subtract).then_inc(s_lo, 1)


LOW = -1.0e30
TAKEN = -3.0e38


def route(nc, sems, sh, m, router, weights_T, name):
    NE = m.experts
    NR = 65 if m is MOE0 else NE
    NL = NE + 8
    with ExitStack() as ctx:
        def sb(n, shape, dt=F32):
            return ctx.enter_context(nc.sbuf_tensor(f"{name}_{n}", shape, dt))

        def sem(n):
            return nc.alloc_semaphore(name=f"{name}_{n}")

        rw = sb("rw", [P, KT, NR])
        rwp = sb("rwp", [P, 2, KT, NR], F16)
        L = sb("L", [P, NB, NL])
        rest = sb("rest", [P, NB, NL])
        top8 = sb("top8", [P, NB, 8])
        chosen = sb("chosen", [P, NB, 8])
        shifted = sb("shifted", [P, NB, NE])
        e = sb("e", [P, NB, NE])
        em = sb("em", [P, NB, NE])
        total = sb("total", [P, NB])
        inv = sb("inv", [P, NB])
        sig = sb("sig", [P, NB])
        sig1 = sb("sig1", [P, NB])
        comb = sb("comb", [P, NB, m.rows])
        combT = sb("combT", [m.rows, T])
        LP = ctx.enter_context(nc.psum_tensor(name + "_LP", [P, NB, P], F32))
        CP = ctx.enter_context(nc.psum_tensor(name + "_CP", [P, NB, P], F32))
        s_load, s_hi, s_lo, s_L, s_d, s_e, s_comb, s_CT, s_ct, s_out, s_pad, s_Lc = map(sem, (
            "load", "hi", "lo", "L", "chain", "exp", "comb", "CT", "ct", "out", "pad", "Lc"))
        with nc.Block() as block:
            @block.sync
            def _(sp):
                sp.dma_start(rw[:, :, :], router).then_inc(s_load, 16)
                sp.wait_ge(s_ct, 1)
                sp.dma_start(weights_T, combT[:, :]).then_inc(s_out, 16)
                sp.wait_ge(s_out, 16)

            @block.scalar
            def _(act):
                act.wait_ge(s_load, 16)
                nc.scalar.activation(rwp[:, 0, :, :], rw[:, :, :], ACT.Copy).then_inc(s_hi, 1)
                act.wait_ge(s_Lc, 2)
                nc.scalar.activation(e[:, :, :], shifted[:, :, :], ACT.Exp).then_inc(s_e, 1)
                if m is MOE0:
                    nc.scalar.activation(sig[:, :], LP[:, :, NE], ACT.Exp, scale=-1.0).then_inc(s_e, 1)
                act.wait_ge(s_CT, 1)
                nc.scalar.activation(combT[:, :], CP[0:m.rows, :, :].rearrange("p t c -> p (t c)"), ACT.Copy).then_inc(s_ct, 1)

            @block.tensor
            def _(pe):
                pe.wait_ge(s_lo, 1)
                with pe.Fori(0, NB) as t:
                    i = 0
                    for a, b in PRODUCTS:
                        for k in range(KT):
                            last = nc.tensor.matmul(LP[:, bass.ds(t, 1), 0:NR], sh.hT[:, a, k, bass.ds(t * P, P)], rwp[:, b, k, :],
                                                    start=i == 0, stop=i == 5)
                            i += 1
                    last.then_inc(s_L, 1)
                pe.wait_ge(s_comb, 1)
                for t in range(NB):
                    last = nc.tensor.transpose(CP[0:m.rows, t, :], comb[:, t, :], sh.ident[:, :])
                last.then_inc(s_CT, 1)

            @block.vector
            def _(dve):
                done = [0]

                def chained(ins):
                    done[0] += 1
                    ins.then_inc(s_d, 1)
                    dve.wait_ge(s_d, done[0])

                dve.wait_ge(s_hi, 1)
                nc.vector.tensor_tensor(rwp[:, 1, :, :], rw[:, :, :], rwp[:, 0, :, :], ALU.subtract).then_inc(s_lo, 1)
                nc.vector.memset(L[:, :, NE:NL], LOW)
                nc.vector.memset(chosen[:, :, :], LOW)
                nc.vector.memset(comb[:, :, :], 1.0 if m is MOE1 else 0.0)
                dve.wait_ge(s_L, NB)
                chained(nc.vector.tensor_copy(L[:, :, 0:NE], LP[:, :, 0:NE]))
                for t in range(NB):
                    last = nc.vector.max(top8[:, t, :], L[:, t, :])
                chained(last)
                nc.vector.tensor_copy(chosen[:, :, 0:m.top], top8[:, :, 0:m.top]).then_inc(s_Lc, 1)
                nc.vector.tensor_tensor(shifted[:, :, :], L[:, :, 0:NE], top8[:, :, 0:1].to_broadcast([P, NB, NE]),
                                        ALU.subtract).then_inc(s_Lc, 1)
                dve.wait_ge(s_Lc, 2)
                for t in range(NB):
                    last = nc.vector.match_replace(rest[:, t, :], chosen[:, t, :], L[:, t, :], TAKEN)
                chained(last)
                dve.wait_ge(s_e, 2 if m is MOE0 else 1)
                chained(nc.vector.scalar_tensor_tensor(out=em[:, :, :], in0=rest[:, :, 0:NE], scalar=-2.0e38, in1=e[:, :, :],
                                                       op0=ALU.is_le, op1=ALU.mult))
                chained(nc.vector.reduce_sum(total[:, :], em[:, :, :], axis=AXX))
                chained(nc.vector.reciprocal(inv[:, :], total[:, :]))
                rep = 64 // NE
                dst = comb[:, :, 0:64].rearrange("p t (e r) -> p t e r", r=rep)
                if rep == 1:
                    chained(nc.vector.tensor_tensor(comb[:, :, 0:64], em[:, :, :], inv[:, :].unsqueeze(2).to_broadcast([P, NB, NE]), ALU.mult))
                    chained(nc.vector.tensor_scalar_add(sig1[:, :], sig[:, :], 1.0))
                    nc.vector.reciprocal(comb[:, :, 64], sig1[:, :]).then_inc(s_comb, 1)
                else:
                    chained(nc.vector.tensor_tensor(shifted[:, :, :], em[:, :, :], inv[:, :].unsqueeze(2).to_broadcast([P, NB, NE]), ALU.mult))
                    nc.vector.tensor_copy(dst, shifted[:, :, :].unsqueeze(3).to_broadcast([P, NB, NE, rep])).then_inc(s_comb, 1)


def experts(nc, sems, sh, m, weights_T, gate, name):
    CT = 512
    NC = T // CT
    NF = m.tiles
    uses = ((NF + 1) // 2, NF // 2)
    with ExitStack() as ctx:
        def sb(n, shape, dt=F32):
            return ctx.enter_context(nc.sbuf_tensor(f"{name}_{n}", shape, dt))

        def sems2(n):
            return [nc.alloc_semaphore(name=f"{name}_{n}{u}") for u in range(2)]

        wb = sb("wb", [P, 2, CT])
        sg = sb("sg", [P, 2, CT])
        t1 = sb("t1", [P, 2, CT])
        a = sb("a", [P, 2, CT])
        ap = sb("ap", [P, 2, 2, CT], F16)
        zero = sb("zero", [P, CT], F16)
        G = ctx.enter_context(nc.psum_tensor(name + "_G", [P, 2, CT], F32))
        U = ctx.enter_context(nc.psum_tensor(name + "_U", [P, 2, CT], F32))
        O = ctx.enter_context(nc.psum_tensor(name + "_O", [P, CT // P, D], F32))
        s_wb, s_G, s_U, s_sg, s_t1, s_a, s_hi, s_lo, s_O = map(sems2, ("wb", "G", "U", "sg", "t1", "a", "hi", "lo", "O"))
        s_res = nc.alloc_semaphore(name=name + "_res")
        s_zero = nc.alloc_semaphore(name=name + "_zero")

        def steps(eng, c, step):
            with eng.Fori(0, NF // 2) as i:
                for u in range(2):
                    step(i * 2 + u, u, c * uses[u] + i)
            if NF % 2:
                step(NF - 1, 0, c * uses[0] + NF // 2)

        with nc.Block() as block:
            @block.sync
            def _(sp):
                def step(c, f, u, n):
                    sp.wait_ge(s_t1[u], n + 1)
                    for half in range(2):
                        src = weights_T[bass.ds(f * 2 + half, 1), bass.ds(c * CT, CT)].to_broadcast([P // 2, CT])
                        sp.dma_start(wb[half * 64:half * 64 + 64, u, :], src).then_inc(s_wb[u], 16)

                with sp.Fori(0, NC) as c:
                    steps(sp, c, lambda f, u, n: step(c, f, u, n))

            @block.scalar
            def _(act):
                def step(f, u, n):
                    act.wait_ge(s_G[u], n + 1)
                    nc.scalar.activation(sg[:, u, :], G[:, u, :], ACT.Silu).then_inc(s_sg[u], 1)
                    act.wait_ge(s_a[u], n + 2)
                    act.wait_ge(s_O[u], n + 1)
                    nc.scalar.activation(ap[:, u, 0, :], a[:, u, :], ACT.Copy).then_inc(s_hi[u], 1)

                act.sem_inc(s_sg[0], 1)
                act.sem_inc(s_sg[1], 1)
                with act.Fori(0, NC) as c:
                    steps(act, c, step)

            @block.vector
            def _(dve):
                def step(f, u, n):
                    dve.wait_ge(s_wb[u], n * 32 + 32)
                    dve.wait_ge(s_sg[u], n + 2)
                    nc.vector.tensor_tensor(t1[:, u, :], sg[:, u, :], wb[:, u, :], ALU.mult).then_inc(s_t1[u], 1)
                    dve.wait_ge(s_t1[u], n + 2)
                    dve.wait_ge(s_U[u], n + 1)
                    nc.vector.tensor_tensor(a[:, u, :], U[:, u, :], t1[:, u, :], ALU.mult).then_inc(s_a[u], 1)
                    dve.wait_ge(s_hi[u], n + 1)
                    nc.vector.tensor_tensor(ap[:, u, 1, :], a[:, u, :], ap[:, u, 0, :], ALU.subtract).then_inc(s_lo[u], 1)

                nc.vector.memset(zero[:, :], 0.0).then_inc(s_zero, 1)
                for u in range(2):
                    dve.sem_inc(s_t1[u], 1)
                    dve.sem_inc(s_a[u], 1)
                dve.sem_inc(s_res, 1)
                with dve.Fori(0, NC) as c:
                    steps(dve, c, step)
                    u = (NF - 1) % 2
                    dve.wait_ge(s_O[u], (c + 1) * uses[u] + 1)
                    xs = sh.X[:, bass.ds(c * (CT // P), CT // P), :]
                    nc.vector.scalar_tensor_tensor(out=xs, in0=O[:, :, :], scalar=gate, in1=xs, op0=ALU.mult,
                                                   op1=ALU.add).then_inc(s_res, 1)

            @block.tensor
            def _(pe):
                def up(c, f, u, n):
                    for X_, s_free, s_done, base in ((G, s_sg, s_G, 0), (U, s_a, s_U, 2 * P)):
                        pe.wait_ge(s_free[u], n + 1)
                        i = 0
                        for wp, xp in PRODUCTS:
                            for k in range(KT):
                                last = nc.tensor.matmul(X_[:, u, :], sh.W[:, wp, bass.ds(f * TW + (base + k * P), P)],
                                                        sh.hT[:, xp, k, bass.ds(c * CT, CT)], start=i == 0, stop=i == 5)
                                i += 1
                        last.then_inc(s_done[u], 1)

                def down(f, u, n):
                    pe.wait_ge(s_lo[u], n + 1)
                    for t in range(CT // P):
                        for xp, wp in PRODUCTS:
                            last = nc.tensor.matmul(O[:, t, :], ap[:, u, xp, t * P:(t + 1) * P],
                                                    sh.W[:, wp, bass.ds(f * TW + 4 * P, D)], start=False, stop=False,
                                                    skip_group_check=True)
                    last.then_inc(s_O[u], 1)

                pe.sem_inc(s_O[0], 1)
                pe.sem_inc(s_O[1], 1)
                pe.wait_ge(s_zero, 1)
                with pe.Fori(0, NC) as c:
                    up(c, 0, 0, c * uses[0])
                    pe.wait_ge(s_res, c + 1)
                    for bank in range(2):
                        nc.tensor.matmul(O[:, 2 * bank:2 * bank + 2, :], zero[:, 0:P], zero[:, :], start=True, stop=False,
                                         skip_group_check=True)
                    NI = (NF - 1) // 2
                    with pe.Fori(0, NI) as i:
                        up(c, i * 2 + 1, 1, c * uses[1] + i)
                        down(i * 2, 0, c * uses[0] + i)
                        up(c, i * 2 + 2, 0, c * uses[0] + i + 1)
                        down(i * 2 + 1, 1, c * uses[1] + i)
                    if NF % 2 == 0:
                        up(c, NF - 1, 1, c * uses[1] + NI)
                        down(NF - 2, 0, c * uses[0] + NI)
                        down(NF - 1, 1, c * uses[1] + NI)
                    else:
                        down(NF - 1, 0, c * uses[0] + NI)


def load_split(nc, sems, items, name):
    s_load, s_hi = (nc.alloc_semaphore(name=f"{name}_{x}") for x in ("load", "hi"))
    with ExitStack() as ctx:
        stages = [ctx.enter_context(nc.sbuf_tensor(f"{name}_stage{i}", [P, src.shape[1]], F32))
                  for i, (_, src) in enumerate(items)]
        with nc.Block() as block:
            @block.sync
            def _(sp):
                for stage, (_, src) in zip(stages, items):
                    sp.dma_start(stage[:, :], src).then_inc(s_load, 16)

            @block.scalar
            def _(act):
                act.wait_ge(s_load, 16 * len(items))
                for stage, (dst, _) in zip(stages, items):
                    nc.scalar.activation(dst[:, 0, :], stage[:, :], ACT.Copy).then_inc(s_hi, 1)

            @block.vector
            def _(dve):
                for i, (stage, (dst, _)) in enumerate(zip(stages, items)):
                    dve.wait_ge(s_hi, i + 1)
                    nc.vector.tensor_tensor(dst[:, 1, :], stage[:, :], dst[:, 0, :], ALU.subtract)


def rms_attention(nc, sems, sh, ctxT, weights, gate):
    NH, HD = 32, 8
    SLOT = 32
    GH = P // SLOT
    NG = NH // GH
    HE = HD + 1
    with ExitStack() as ctx:
        def sb(n, shape, dt=F32):
            return ctx.enter_context(nc.sbuf_tensor("rms_" + n, shape, dt))

        def sem(n):
            return nc.alloc_semaphore(name="rms_" + n)

        qk = sb("qk", [P, NB, 2, NH, HD])
        vx = sb("vx", [P, NB, NH, HE])
        ss = sb("ss", [P, NB, 2 * NH])
        rs = sb("rs", [P, NB, 2 * NH])
        with ExitStack() as inner:
            cT = inner.enter_context(nc.sbuf_tensor("rms_cT", [P, 2, KT * T], F16))
            wq, wk, wv = (inner.enter_context(nc.sbuf_tensor(f"rms_{x}", [P, 2, KT * D], F16)) for x in ("wq", "wk", "wv"))
            load_split(nc, sems, [(cT, ctxT), (wq, weights["q"]), (wk, weights["k"]), (wv, weights["v"])], "rmsw")
            sq = inner.enter_context(nc.sbuf_tensor("rms_sq", [P, 2, 2 * D], F32))
            QK = inner.enter_context(nc.psum_tensor("rms_QK", [P, 2, 2, D], F32))
            V = inner.enter_context(nc.psum_tensor("rms_V", [P, 2, 512], F32))
            s_mm, s_sq, s_ev, s_v, s_qk, s_one = map(sem, ("mm", "sq", "red", "v", "qk", "one"))
            with nc.Block() as block:
                @block.tensor
                def _(pe):
                    with pe.Fori(0, NB // 2) as pair:
                        for par in range(2):
                            t = pair * 2 + par
                            pe.wait_ge(s_v, t + 1)
                            pe.wait_ge(s_qk, t + 1)
                            for out, x, w in ((QK[:, par, 0, :], None, wq), (QK[:, par, 1, :], cT, wk), (V[:, par, 0:D], cT, wv)):
                                i = 0
                                for a, b in PRODUCTS:
                                    for k in range(KT):
                                        lhs = sh.hT[:, a, k, bass.ds(t * P, P)] if x is None else x[:, a, bass.ds(t * P + k * T, P)]
                                        last = nc.tensor.matmul(out, lhs, w[:, b, k * D:(k + 1) * D], start=i == 0, stop=i == 5)
                                        i += 1
                            last.then_inc(s_mm, 1)

                @block.scalar
                def _(act):
                    act.sem_inc(s_v, 2)
                    act.wait_ge(s_one, 1)
                    with act.Fori(0, NB // 2) as pair:
                        for par in range(2):
                            t = pair * 2 + par
                            act.wait_ge(s_qk, t + 3)
                            act.wait_ge(s_ev, t + 1)
                            nc.scalar.activation(sq[:, par, :], qk[:, t, :, :, :].rearrange("p s h d -> p (s h d)"), ACT.Square).then_inc(s_sq, 1)
                            act.wait_ge(s_mm, t + 1)
                            nc.scalar.activation(vx[:, t, :, 0:HD], V[:, par, 0:D].rearrange("p (h d) -> p h d", d=HD),
                                                 ACT.Copy).then_inc(s_v, 1)

                @block.vector
                def _(dve):
                    dve.sem_inc(s_ev, 2)
                    dve.sem_inc(s_qk, 2)
                    nc.vector.memset(vx[:, :, :, HD:HE], 1.0).then_inc(s_one, 1)
                    with dve.Fori(0, NB // 2) as pair:
                        for par in range(2):
                            t = pair * 2 + par
                            dve.wait_ge(s_mm, t + 1)
                            copy_indexed(nc, qk[:, t, :, :, :], QK[:, par, :, :]).then_inc(s_qk, 1)
                            dve.wait_ge(s_sq, t + 1)
                            nc.vector.reduce_sum(ss[:, t, :], sq[:, par, :].rearrange("p (g d) -> p g d", d=HD),
                                                 axis=AXX).then_inc(s_ev, 1)

        s_root, s_rs = sem("root"), sem("rs")
        eps6 = sb("eps6", [P, 1])
        s_eps = sem("eps")
        s_n = sem("n")
        qs = sb("qs", [P, 2, NH, SLOT], F16)
        ks = sb("ks", [P, 2, NH, SLOT], F16)
        qT = sb("qT", [P, 2, NG, P], F16)
        kT = sb("kT", [P, 2, NG, P], F16)
        E = sb("E", [P, 2, 2, NG // 2, P])
        inv = sb("inv", [P, 2, NH])
        on = sb("on", [P, 2, NH, HD])
        NR = 4
        TQ = ctx.enter_context(nc.psum_tensor("rms_TQ", [P, NG, P], F16))
        TK = ctx.enter_context(nc.psum_tensor("rms_TK", [P, NG, P], F16))
        S = ctx.enter_context(nc.psum_tensor("rms_S", [P, 2, 2, NG // 2, P], F32))
        O = ctx.enter_context(nc.psum_tensor("rms_O", [P, 2, 512], F32))
        s_hi, s_lo, s_TQ, s_TK, s_qT, s_kT, s_S, s_E, s_O, s_inv, s_on, s_res = map(sem, (
            "hi", "lo", "TQ", "TK", "qT", "kT", "S", "E", "O", "inv", "on", "res"))
        with nc.Block() as block:
            @block.tensor
            def _(pe):
                pe.sem_inc(s_TK, 2)
                pe.sem_inc(s_S, 2 * NR)
                pe.sem_inc(s_O, 2)
                with pe.Fori(0, NB // 2) as pair:
                    for par in range(2):
                        t = pair * 2 + par
                        pe.wait_ge(s_lo, t + 1)
                        pe.wait_ge(s_qT, t + 1)
                        for g in range(NG):
                            last = nc.tensor.transpose(TQ[:, g, :], qs[:, par, g * GH:(g + 1) * GH, :].rearrange("p h s -> p (h s)"), sh.identh[:, :])
                        last.then_inc(s_TQ, 1)
                        pe.wait_ge(s_kT, t + 1)
                        for g in range(NG):
                            last = nc.tensor.transpose(TK[:, g, :], ks[:, par, g * GH:(g + 1) * GH, :].rearrange("p h s -> p (h s)"), sh.identh[:, :])
                        last.then_inc(s_TK, 1)
                        pe.wait_ge(s_qT, t + 2)
                        pe.wait_ge(s_kT, t + 2)

                        def scores(r):
                            pe.wait_ge(s_E, t * NR + r + 1)
                            for i in range(NG // 2):
                                for jj in range(2):
                                    g, j = r // 2 * (NG // 2) + i, r % 2 * 2 + jj
                                    last = nc.tensor.matmul(S[:, r % 2, jj, i, :], kT[j * SLOT:(j + 1) * SLOT, par, g, :],
                                                            qT[j * SLOT:(j + 1) * SLOT, par, g, :], start=True, stop=True,
                                                            skip_group_check=True)
                            last.then_inc(s_S, 1)

                        def values(r):
                            pe.wait_ge(s_E, t * NR + r + 3)
                            for i in range(NG // 2):
                                for jj in range(2):
                                    h = (r // 2 * (NG // 2) + i) * GH + r % 2 * 2 + jj
                                    last = nc.tensor.matmul(O[:, par, h * HE:(h + 1) * HE], E[:, r % 2, jj, i, :],
                                                            vx[:, t, h, :], start=True, stop=True, skip_group_check=True)
                            last.then_inc(s_O, 1)

                        scores(0)
                        pe.wait_ge(s_res, t + 1)
                        for r in range(NR):
                            if r + 1 < NR:
                                scores(r + 1)
                            values(r)

            @block.scalar
            def _(act):
                act.sem_inc(s_E, 2)
                act.sem_inc(s_qT, 1)
                act.wait_ge(s_eps, 1)
                nc.scalar.activation(rs[:, :, :], ss[:, :, :], ACT.Sqrt, bias=eps6[:, 0:1], scale=1.0 / HD).then_inc(s_root, 1)
                with act.Fori(0, NB // 2) as pair:
                    for par in range(2):
                        t = pair * 2 + par
                        act.wait_ge(s_TQ, t + 1)
                        act.wait_ge(s_S, t * NR + NR)
                        nc.scalar.activation(qT[:, par, :, :], TQ[:, :, :], ACT.Copy).then_inc(s_qT, 1)
                        for r in range(NR):
                            act.wait_ge(s_S, t * NR + r + 1 + 2 * NR)
                            act.wait_ge(s_O, t * NR + r + 1)
                            nc.scalar.activation(E[:, r % 2, :, :, :], S[:, r % 2, :, :, :], ACT.Exp,
                                                 scale=float(HD) ** -0.5).then_inc(s_E, 1)

            @block.vector
            def _(dve):
                dve.sem_inc(s_kT, 1)
                dve.sem_inc(s_res, 2)
                nc.vector.memset(eps6[:, :], 1e-6).then_inc(s_eps, 1)
                nc.vector.memset(qs[:, :, :, :], 0.0)
                nc.vector.memset(ks[:, :, :, :], 0.0).then_inc(s_n, 1)
                dve.wait_ge(s_root, 1)
                nc.vector.reciprocal(ss[:, :, :], rs[:, :, :]).then_inc(s_rs, 1)
                dve.wait_ge(s_rs, 1)

                def stacks(t, par):
                    x = qk[:, t, :, :, :].rearrange("p s h d -> p (s h) d")
                    nc.vector.tensor_tensor(x, x, ss[:, t, :].unsqueeze(2).to_broadcast([P, 2 * NH, HD]), ALU.mult).then_inc(s_n, 1)
                    dve.wait_ge(s_n, t + 2)
                    dve.wait_ge(s_TK, t + 1)
                    for side, st, second in ((0, qs, 1), (1, ks, 2)):
                        for slot in (0, second):
                            last = copy_indexed(nc, st[:, par, :, slot * HD:(slot + 1) * HD], qk[:, t, side, :, :])
                    last.then_inc(s_hi, 1)
                    dve.wait_ge(s_hi, t + 1)
                    nc.vector.tensor_tensor(qs[:, par, :, 2 * HD:3 * HD], qk[:, t, 0, :, :], qs[:, par, :, 0:HD], ALU.subtract)
                    nc.vector.tensor_tensor(ks[:, par, :, HD:2 * HD], qk[:, t, 1, :, :], ks[:, par, :, 0:HD], ALU.subtract).then_inc(s_lo, 1)

                def output(t, par):
                    o = O[:, par, 0:NH * HE].rearrange("p (h d) -> p h d", d=HE)
                    dve.wait_ge(s_O, t * NR + NR + 2)
                    nc.vector.reciprocal(inv[:, par, :], o[:, :, HD]).then_inc(s_inv, 1)
                    dve.wait_ge(s_inv, t + 1)
                    nc.vector.tensor_tensor(on[:, par, :, :], o[:, :, 0:HD], inv[:, par, :].unsqueeze(2).to_broadcast([P, NH, HD]),
                                            ALU.mult).then_inc(s_on, 1)
                    dve.wait_ge(s_on, t + 1)
                    nc.vector.scalar_tensor_tensor(out=sh.X[:, t, :], in0=on[:, par, :, :].rearrange("p h d -> p (h d)"),
                                                   scalar=gate, in1=sh.X[:, t, :], op0=ALU.mult, op1=ALU.add).then_inc(s_res, 1)

                with dve.Fori(0, NB // 2) as pair:
                    for par in range(2):
                        t = pair * 2 + par
                        stacks(t, par)
                        dve.wait_ge(s_TK, t + 3)
                        dve.wait_ge(s_S, t * NR + NR)
                        nc.vector.tensor_copy(kT[:, par, :, :], TK[:, :, :]).then_inc(s_kT, 1)
                        output(t, par)


MAGIC = 1.5 * 2.0 ** 23


def transpose_tiles(nc, sems, name, groups, source, target, ident):
    s_T, s_even, s_odd = (nc.alloc_semaphore(name=f"{name}_{n}") for n in ("T", "even", "odd"))
    with ExitStack() as ctx:
        TP = ctx.enter_context(nc.psum_tensor(name + "_TP", [P, 2, 4, P], F32))
        with nc.Block() as block:
            @block.scalar
            def _(act):
                act.sem_inc(s_even, 1)
                with act.Fori(0, NB // 2) as pair:
                    act.wait_ge(s_T, pair * 2 + 1)
                    nc.scalar.activation(target(pair * 2), TP[:, 0, 0:groups, :], ACT.Copy).then_inc(s_even, 1)

            @block.vector
            def _(dve):
                dve.sem_inc(s_odd, 1)
                with dve.Fori(0, NB // 2) as pair:
                    dve.wait_ge(s_T, pair * 2 + 2)
                    copy_indexed(nc, target(pair * 2 + 1), TP[:, 1, 0:groups, :]).then_inc(s_odd, 1)

            @block.tensor
            def _(pe):
                with pe.Fori(0, NB // 2) as pair:
                    for par in range(2):
                        pe.wait_ge((s_even, s_odd)[par], pair + 1)
                        for g in range(groups):
                            last = nc.tensor.matmul(TP[:, par, g, :], source(g, pair * 2 + par), ident, start=True, stop=True)
                        last.then_inc(s_T, 1)


def project(nc, sems, name, parts, weights, evacuate):
    s_mm, s_ev = (nc.alloc_semaphore(name=f"{name}_{n}") for n in ("mm", "ev"))
    with ExitStack() as ctx:
        Q = ctx.enter_context(nc.psum_tensor(name + "_Q", [P, 2, 512], F32))
        with nc.Block() as block:
            @block.tensor
            def _(pe):
                with pe.Fori(0, NB // 2) as pair:
                    for par in range(2):
                        t = pair * 2 + par
                        pe.wait_ge(s_ev, t + 1)
                        i = 0
                        for a, b in PRODUCTS:
                            for k in range(KT):
                                last = nc.tensor.matmul(Q[:, par, 0:D], parts(a, k, t), weights[:, b, k * D:(k + 1) * D],
                                                        start=i == 0, stop=i == 5)
                                i += 1
                        last.then_inc(s_mm, 1)

            @block.vector
            def _(dve):
                dve.sem_inc(s_ev, 2)
                with dve.Fori(0, NB // 2) as pair:
                    for par in range(2):
                        t = pair * 2 + par
                        dve.wait_ge(s_mm, t + 1)
                        evacuate(dve, t, Q[:, par, 0:D]).then_inc(s_ev, 1)


def quantised_attention(nc, sems, sh, a, gate):
    NH, HD = 16, 16
    SLOT = 2 * HD
    GH = P // SLOT
    NG = NH // GH
    HALF = T // 2
    KB = HALF // P
    LN255 = float(np.log(255.0))
    with ExitStack() as ctx:
        def sb(n, shape, dt=F32, where=ctx):
            return where.enter_context(nc.sbuf_tensor("qa_" + n, shape, dt))

        def sem(n):
            return nc.alloc_semaphore(name="qa_" + n)

        qT = sb("qT", [P, NG, T], F16)
        kT = sb("kT", [P, NG, T], F16)
        V = sb("V", [P, NB, D], BF16)
        neg_sq = sb("neg_sq", [P, NB, NH])
        sq = sb("sq", [P, NB, NH])
        svb = sb("svb", [P, D])
        bias = sb("bias", [P, 3, D])
        bv = sb("bv", [P, KT])
        wp = sb("wp", [P, 2, KT * D], F16)
        with ExitStack() as inner:
            cT = sb("cT", [P, 2, KT * T], F16, inner)
            wq, wk, wv = (sb(x, [P, 2, KT * D], F16, inner) for x in ("wq", "wk", "wv"))
            load_split(nc, sems, [(cT, a["ctxT"]), (wq, a["qa_wq"]), (wk, a["qa_wk"]), (wv, a["qa_wv"]), (wp, a["qa_wp"])], "qaw")
            Y = sb("Y", [P, NB, D], F32, inner)
            Z = sb("Z", [P, NB, D], F32, inner)
            stack = sb("stack", [P, NB, NH, SLOT], F16, inner)
            ints = sb("ints", [P, KT, T], BF16, inner)
            amax = sb("amax", [P, NB, NH], F32, inner)
            sv = sb("sv", [P, KT], F32, inner)
            rsv = sb("rsv", [P, KT], F32, inner)
            s_b, s_b4 = sem("bias"), sem("b4")
            with nc.Block() as block:
                @block.sync
                def _(sp):
                    for i, x in enumerate(("bq", "bk", "bp")):
                        sp.dma_start(bias[:, i, :], a["qa_" + x].partition_broadcast(P)).then_inc(s_b, 16)
                    sp.dma_start(bv[:, :], a["qa_bv"]).then_inc(s_b, 16)
                    sp.wait_ge(s_b, 64)

                @block.vector
                def _(dve):
                    dve.wait_ge(s_b, 64)
                    nc.vector.tensor_scalar_mul(bias[:, 0, :], bias[:, 0, :], float(HD) ** -0.5).then_inc(s_b4, 1)

            def quantise(side):
                s_c = sem("chain" + side)
                scale = sq if side == "q" else amax
                y = Y[:, :, :].rearrange("p t (h d) -> p (t h) d", d=HD)
                z = Z[:, :, :].rearrange("p t (h d) -> p (t h) d", d=HD)
                st = stack[:, :, :, :].rearrange("p t h s -> p (t h) s")
                flat = scale[:, :, :].rearrange("p t h -> p (t h)")
                inv = neg_sq[:, :, :].rearrange("p t h -> p (t h)")
                with nc.Block() as block:
                    @block.vector
                    def _(dve):
                        done = [0]

                        def chained(ins):
                            done[0] += 1
                            ins.then_inc(s_c, 1)
                            dve.wait_ge(s_c, done[0])

                        wide = [P, NB * NH, HD]
                        chained(nc.vector.tensor_reduce(out=flat, in_=y, axis=AXX, op=ALU.max, apply_absolute_value=True))
                        chained(nc.vector.tensor_scalar(flat, flat, 1.0 / 127.0, 1e-8, ALU.mult, ALU.max))
                        chained(nc.vector.reciprocal(inv, flat))
                        chained(nc.vector.tensor_tensor(z, y, inv.unsqueeze(2).to_broadcast(wide), ALU.mult))
                        chained(nc.vector.tensor_scalar(Z[:, :, :], Z[:, :, :], MAGIC, MAGIC, ALU.add, ALU.subtract))
                        if side == "q":
                            for slot in range(2):
                                nc.vector.tensor_scalar(st[:, :, slot * HD:(slot + 1) * HD], z, 127.0, -127.0, ALU.min, ALU.max)
                            nc.vector.tensor_scalar_mul(neg_sq[:, :, :], sq[:, :, :], -1.0)
                        else:
                            chained(nc.vector.tensor_scalar(Z[:, :, :], Z[:, :, :], 127.0, -127.0, ALU.min, ALU.max))
                            chained(nc.vector.tensor_tensor(y, z, flat.unsqueeze(2).to_broadcast(wide), ALU.mult))
                            chained(nc.vector.tensor_copy(st[:, :, 0:HD], y))
                            nc.vector.tensor_tensor(st[:, :, HD:SLOT], y, st[:, :, 0:HD], ALU.subtract)
                transpose_tiles(nc, sems, "qaT" + side, NG,
                                lambda g, t: stack[:, t, g * GH:(g + 1) * GH, :].rearrange("p h s -> p (h s)"),
                                lambda t: (qT if side == "q" else kT)[:, :, bass.ds(t * P, P)], sh.identh[:, :])

            project(nc, sems, "qapk", lambda part, k, t: cT[:, part, bass.ds(t * P + k * T, P)], wk,
                    lambda dve, t, psum: nc.vector.tensor_tensor(Y[:, t, :], psum, bias[:, 1, :], ALU.add))
            quantise("k")
            project(nc, sems, "qapq", lambda part, k, t: sh.hT[:, part, k, bass.ds(t * P, P)], wq,
                    lambda dve, t, psum: nc.vector.scalar_tensor_tensor(out=Y[:, t, :], in0=psum, scalar=float(HD) ** -0.5,
                                                                        in1=bias[:, 0, :], op0=ALU.mult, op1=ALU.add))
            quantise("q")

            vT = Y[:, :, :].rearrange("p t d -> p (t d)").rearrange("p (m n) -> p m n", m=KT)
            zT = Z[:, :, :].rearrange("p t d -> p (t d)").rearrange("p (m n) -> p m n", m=KT)
            sv_dram = nc.dram_tensor("qa_value_scales", [P, KT], F32, kind="Internal").ap()
            s_mm, s_ev, s_vc, s_sv, s_out, s_in = map(sem, ("vmm", "vev", "vchain", "sv", "svout", "svin"))
            with ExitStack() as pctx:
                VP = pctx.enter_context(nc.psum_tensor("qa_VP", [P, 2, 512], F32))
                with nc.Block() as block:
                    @block.tensor
                    def _(pe):
                        for m in range(KT):
                            for c in range(4):
                                n = m * 4 + c
                                if n >= 2:
                                    pe.wait_ge(s_ev, n - 1)
                                i = 0
                                for wpart, xpart in PRODUCTS:
                                    for k in range(KT):
                                        last = nc.tensor.matmul(VP[:, n % 2, :], wv[:, wpart, k * D + m * P:k * D + (m + 1) * P],
                                                                cT[:, xpart, k * T + c * 512:k * T + (c + 1) * 512],
                                                                start=i == 0, stop=i == 5)
                                        i += 1
                                last.then_inc(s_mm, 1)

                    @block.scalar
                    def _(act):
                        for m in range(KT):
                            for c in range(4):
                                n = m * 4 + c
                                act.wait_ge(s_mm, n + 1)
                                nc.scalar.activation(vT[:, m, c * 512:(c + 1) * 512], VP[:, n % 2, :], ACT.Identity,
                                                     bias=bv[:, m:m + 1]).then_inc(s_ev, 1)

                    @block.vector
                    def _(dve):
                        done = [0]

                        def chained(ins):
                            done[0] += 1
                            ins.then_inc(s_vc, 1)
                            dve.wait_ge(s_vc, done[0])

                        dve.wait_ge(s_ev, 4 * KT)
                        chained(nc.vector.tensor_reduce(out=sv[:, :], in_=vT, axis=AXX, op=ALU.max, apply_absolute_value=True))
                        nc.vector.tensor_scalar(sv[:, :], sv[:, :], 1.0 / 127.0, 1e-8, ALU.mult, ALU.max).then_inc(s_sv, 1)
                        dve.wait_ge(s_sv, 1)
                        chained(nc.vector.reciprocal(rsv[:, :], sv[:, :]))
                        for m in range(KT):
                            last = nc.vector.tensor_scalar(zT[:, m, :], vT[:, m, :], rsv[:, m:m + 1], MAGIC, ALU.mult, ALU.add)
                        chained(last)
                        chained(nc.vector.tensor_scalar(zT, zT, MAGIC, 127.0, ALU.subtract, ALU.min))
                        nc.vector.tensor_scalar(ints[:, :, :], zT, -127.0, None, ALU.max)

                    @block.sync
                    def _(sp):
                        sp.wait_ge(s_sv, 1)
                        sp.dma_start(sv_dram, sv[:, :]).then_inc(s_out, 16)
                        sp.wait_ge(s_out, 16)
                        sp.dma_start(svb[:, :], sv_dram.rearrange("p m -> (p m)").partition_broadcast(P)).then_inc(s_in, 16)
                        sp.wait_ge(s_in, 16)
            transpose_tiles(nc, sems, "qaTv", KT, lambda m, t: ints[:, m, bass.ds(t * P, P)],
                            lambda t: V[:, t, :].rearrange("p (m c) -> p m c", m=KT), sh.ident16[:, :])

        qb = sb("qb", [P, 2, NG // 2, P], F16)
        mx = sb("mx", [P, 2, 2])
        mm = sb("mm", [P, 2])
        nb = sb("nb", [P, 2])
        sums = sb("sums", [P, NB * NH, 2])
        e16 = sb("e16", [P, 2, 2, HALF], mybir.dt.uint16)
        pb = sb("pb", [P, 2, 2, KB, P], BF16)
        pT = sb("pT", [P, 2, 2, KB, P], BF16)
        s_q, s_S, s_E, s_mx, s_mm2, s_nb, s_cast, s_T, s_eva, s_evb, s_V, s_o = map(sem, (
            "q", "S", "E", "mx", "mm2", "nb", "cast", "T", "eva", "evb", "V", "o"))
        O_ALL = NB * NH
        with ExitStack() as pctx:
            S = pctx.enter_context(nc.psum_tensor("qa_S", [P, 2, HALF], F32))
            TP = pctx.enter_context(nc.psum_tensor("qa_TP", [P, 2, KB, P], BF16))
            O = pctx.enter_context(nc.psum_tensor("qa_O", [P, 2, 512], F32))

            def skewed(eng, step):
                LAG = 3
                units = NB * NH
                for i in range(LAG):
                    step(i, lambda lag, i=i: 0 if i >= lag else None)
                with eng.Fori(0, NB - 1) as t:
                    for i in range(NH):
                        h = (LAG + i) % NH
                        step(h, lambda lag, i=i, t=t: t + 1 if LAG + i - lag >= NH else t)
                for i in range(LAG + (NB - 1) * NH, units + LAG):
                    step(i % NH, lambda lag, i=i: (i - lag) // NH if i - lag < units else None)

            with nc.Block() as block:
                @block.gpsimd
                def _(pool):
                    with pool.Fori(0, NB) as t:
                        for half in range(2):
                            pool.wait_ge(s_S, t * 2 * NH + (NH if half == 0 else 2 * NH))
                            nc.gpsimd.tensor_copy(qb[:, half, :, :], qT[:, half * 2:half * 2 + 2, bass.ds(t * P, P)]).then_inc(s_q, 1)

                @block.tensor
                def _(pe):
                    pe.sem_inc(s_S, 2 * NH)
                    pe.sem_inc(s_T, 4)
                    pe.sem_inc(s_V, 2)

                    def step(i, tile):
                        if (t := tile(0)) is not None:
                            h = i % NH
                            u = t * NH + h
                            if h % 8 == 0:
                                pe.wait_ge(s_q, 2 * t + 1 + h // 8)
                            g, j = h // GH, h % GH
                            rows = slice(j * SLOT, (j + 1) * SLOT)
                            for half in range(2):
                                pe.wait_ge(s_E, 2 * u + 1 + half)
                                for c in range(2):
                                    last = nc.tensor.matmul(S[:, half, c * 512:(c + 1) * 512], qb[rows, g // 2, g % 2, :],
                                                            kT[rows, g, half * HALF + c * 512:half * HALF + (c + 1) * 512],
                                                            start=True, stop=True)
                                last.then_inc(s_S, 1)
                        if (t := tile(1)) is not None:
                            h = (i - 1) % NH
                            u = t * NH + h
                            pe.wait_ge(s_cast, u + 3)
                            for half in range(2):
                                pe.wait_ge((s_eva, s_evb)[half], u + 1)
                                for b in range(KB):
                                    last = nc.tensor.transpose(TP[:, half, b, :], pb[:, h % 2, half, b, :], sh.ident16[:, :])
                                last.then_inc(s_T, 1)
                        if (t := tile(2)) is not None:
                            h = (i - 2) % NH
                            u = t * NH + h
                            pe.wait_ge(s_eva, u + 2)
                            pe.wait_ge(s_evb, u + 2)
                            if h % 8 == 0:
                                pe.wait_ge(s_o, 2 * t + 1 + h // 8)
                            for b in range(2 * KB):
                                last = nc.tensor.matmul(O[:, h // 8, (h % 8) * HD:(h % 8 + 1) * HD], pT[:, h % 2, b // KB, b % KB, :],
                                                        V[:, b, h * HD:(h + 1) * HD], start=b == 0, stop=b == 2 * KB - 1)
                            last.then_inc(s_V, 1)

                    skewed(pe, step)

                @block.scalar
                def _(act):
                    act.sem_inc(s_E, 2)
                    act.sem_inc(s_eva, 1)

                    def step(i, tile):
                        if (t := tile(0)) is not None:
                            h = i % NH
                            u = t * NH + h
                            act.wait_ge(s_nb, u + 1)
                            act.wait_ge(s_cast, u + 1)
                            for half in range(2):
                                nc.scalar.activation(e16[:, h % 2, half, :], S[:, half, :], ACT.Exp, bias=nb[:, h % 2:h % 2 + 1],
                                                     scale=sq[:, t, h:h + 1], accum_out=sums[:, u, half:half + 1]).then_inc(s_E, 1)
                        if (t := tile(1)) is not None:
                            h = (i - 1) % NH
                            u = t * NH + h
                            act.wait_ge(s_T, 2 * u + 5)
                            act.wait_ge(s_V, u + 1)
                            nc.scalar.activation(pT[:, h % 2, 0, :, :], TP[:, 0, :, :], ACT.Copy).then_inc(s_eva, 1)

                    skewed(act, step)

                @block.vector
                def _(dve):
                    dve.sem_inc(s_cast, 2)
                    dve.sem_inc(s_evb, 1)
                    dve.sem_inc(s_o, 2)

                    def step(i, tile):
                        t = tile(0)
                        h = i % NH
                        if t is not None:
                            u = t * NH + h
                            dve.wait_ge(s_S, 2 * u + 1 + 2 * NH)
                            nc.vector.reduce_max(mx[:, h % 2, 0:1], S[:, 0, :], axis=AXX).then_inc(s_mx, 1)
                        if (t2 := tile(2)) is not None:
                            h2 = (i - 2) % NH
                            u2 = t2 * NH + h2
                            dve.wait_ge(s_T, 2 * u2 + 6)
                            dve.wait_ge(s_V, u2 + 1)
                            nc.vector.tensor_copy(pT[:, h2 % 2, 1, :, :], TP[:, 1, :, :]).then_inc(s_evb, 1)
                        if t is not None:
                            dve.wait_ge(s_S, 2 * u + 2 + 2 * NH)
                            nc.vector.reduce_max(mx[:, h % 2, 1:2], S[:, 1, :], axis=AXX).then_inc(s_mx, 1)
                            dve.wait_ge(s_mx, 2 * u + 2)
                            nc.vector.tensor_tensor(mm[:, h % 2:h % 2 + 1], mx[:, h % 2, 0:1], mx[:, h % 2, 1:2], ALU.max).then_inc(s_mm2, 1)
                            dve.wait_ge(s_mm2, u + 1)
                            nc.vector.tensor_scalar(nb[:, h % 2:h % 2 + 1], mm[:, h % 2:h % 2 + 1], neg_sq[:, t, h:h + 1], LN255,
                                                    ALU.mult, ALU.add).then_inc(s_nb, 1)
                        if (t1 := tile(1)) is not None:
                            h1 = (i - 1) % NH
                            u1 = t1 * NH + h1
                            dve.wait_ge(s_E, 2 * u1 + 4)
                            dve.wait_ge(s_T, 2 * u1 + 2)
                            nc.vector.tensor_copy(pb[:, h1 % 2, :, :, :], e16[:, h1 % 2, :, :]).then_inc(s_cast, 1)
                        h3 = (i - 3) % NH
                        if h3 % 8 == 7 and (t3 := tile(3)) is not None:
                            dve.wait_ge(s_V, t3 * NH + h3 + 3)
                            copy_indexed(nc, sh.H[:, t3, bass.ds(h3 // 8 * P, P)], O[:, h3 // 8, 0:P]).then_inc(s_o, 1)

                    skewed(dve, step)

        tot = sb("tot", [P, O_ALL])
        rtot = sb("rtot", [P, O_ALL])
        s_n = sem("norm")
        with nc.Block() as block:
            @block.vector
            def _(dve):
                nc.vector.tensor_tensor(tot[:, :], sums[:, :, 0], sums[:, :, 1], ALU.add).then_inc(s_n, 1)
                dve.wait_ge(s_n, 1)
                nc.vector.reciprocal(rtot[:, :], tot[:, :]).then_inc(s_n, 1)
                dve.wait_ge(s_n, 2)
                h = sh.H[:, :, :].rearrange("p t (h d) -> p (t h) d", d=HD)
                nc.vector.tensor_tensor(h, h, rtot[:, :].unsqueeze(2).to_broadcast([P, O_ALL, HD]), ALU.mult).then_inc(s_n, 1)
                dve.wait_ge(s_n, 3)
                for m in range(KT):
                    hm = sh.H[:, :, m * P:(m + 1) * P]
                    nc.vector.tensor_tensor(hm, hm, svb[:, m::KT].unsqueeze(1).to_broadcast([P, NB, P]), ALU.mult)
        split_transpose(nc, sems, sh, "qaO")
        tmp = sb("tmp", [P, NB, D])
        s_tmp = sem("tmp")

        def out_projection(dve, t, psum):
            nc.vector.tensor_tensor(tmp[:, t, :], psum, bias[:, 2, :], ALU.add).then_inc(s_tmp, 1)
            dve.wait_ge(s_tmp, t + 1)
            return nc.vector.scalar_tensor_tensor(out=sh.X[:, t, :], in0=tmp[:, t, :], scalar=gate, in1=sh.X[:, t, :],
                                                  op0=ALU.mult, op1=ALU.add)

        project(nc, sems, "qapo", lambda part, k, t: sh.hT[:, part, k, bass.ds(t * P, P)], wp, out_projection)


def chain_on(eng, s, start=0):
    done = [start]

    def chained(ins):
        done[0] += 1
        ins.then_inc(s, 1)
        eng.wait_ge(s, done[0])
    return chained


def quantised_ffn(nc, sems, sh, a, gate):
    F = 1024
    NF = F // P
    CT = 512
    with ExitStack() as ctx:
        def sb(n, shape, dt=F32, where=ctx):
            return where.enter_context(nc.sbuf_tensor("qf_" + n, shape, dt))

        def sem(n):
            return nc.alloc_semaphore(name="qf_" + n)

        w1 = sb("w1", [P, KT * F], F16)
        w2 = sb("w2", [P, NF * D], F16)
        b1 = sb("b1", [P, NF])
        b2 = sb("b2", [P, D])
        sa = sb("sa", [P, 2])
        rsa = sb("rsa", [P, 2])
        sw = sb("sw", [P, 2])
        rsw = sb("rsw", [P, 2])
        c = sb("c", [P, 8])
        ints = sb("ints", [P, NB, D], F16)
        with ExitStack() as inner:
            f1 = sb("f1", [P, KT * F], F32, inner)
            f2 = sb("f2", [P, NF * D], F32, inner)
            Z = sb("Z", [P, NB * D], F32, inner)
            am = sb("am", [P, 2], F32, inner)
            amx = sb("amx", [P, 2], F32, inner)
            s_load, s_am, s_amx, s_c = map(sem, ("load", "am", "amx", "chain"))
            with nc.Block() as block:
                @block.sync
                def _(sp):
                    sp.dma_start(f1[:, :], a["qf_w1"]).then_inc(s_load, 16)
                    sp.dma_start(f2[:, :], a["qf_w2"]).then_inc(s_load, 16)
                    sp.dma_start(b1[:, :], a["qf_b1"]).then_inc(s_load, 16)
                    sp.dma_start(b2[:, :], a["qf_b2"].partition_broadcast(P)).then_inc(s_load, 16)
                    sp.dma_start(sa[:, 0:1], a["qf_s1"].partition_broadcast(P)).then_inc(s_load, 16)
                    sp.dma_start(sa[:, 1:2], a["qf_s2"].partition_broadcast(P)).then_inc(s_load, 16)

                @block.gpsimd
                def _(pool):
                    pool.wait_ge(s_am, 2)
                    nc.gpsimd.partition_all_reduce(amx[:, :], am[:, :], P, bass.bass_isa.ReduceOp.max).then_inc(s_amx, 1)

                @block.vector
                def _(dve):
                    chained = chain_on(dve, s_c)
                    dve.wait_ge(s_load, 96)
                    for i, f in enumerate((f1, f2)):
                        nc.vector.tensor_reduce(out=am[:, i:i + 1], in_=f[:, :], axis=AXX, op=ALU.max,
                                                apply_absolute_value=True).then_inc(s_am, 1)
                    chained(nc.vector.reciprocal(rsa[:, :], sa[:, :]))
                    hf = sh.H[:, :, :].rearrange("p t d -> p (t d)")
                    chained(nc.vector.tensor_scalar(Z[:, :], hf, rsa[:, 0:1], MAGIC, ALU.mult, ALU.add))
                    chained(nc.vector.tensor_scalar(Z[:, :], Z[:, :], MAGIC, 7.0, ALU.subtract, ALU.min))
                    nc.vector.tensor_scalar(ints[:, :, :].rearrange("p t d -> p (t d)"), Z[:, :], -8.0, None, ALU.max)
                    dve.wait_ge(s_amx, 1)
                    chained(nc.vector.tensor_scalar(sw[:, :], amx[:, :], 1.0 / 7.0, None, ALU.mult))
                    chained(nc.vector.reciprocal(rsw[:, :], sw[:, :]))
                    for i, (f, w) in enumerate(((f1, w1), (f2, w2))):
                        chained(nc.vector.tensor_scalar(f[:, :], f[:, :], rsw[:, i:i + 1], MAGIC, ALU.mult, ALU.add))
                        chained(nc.vector.tensor_scalar(f[:, :], f[:, :], MAGIC, 7.0, ALU.subtract, ALU.min))
                        nc.vector.tensor_scalar(w[:, :], f[:, :], -8.0, None, ALU.max)
                    chained(nc.vector.tensor_tensor(c[:, 0:2], sa[:, :], sw[:, :], ALU.mult))
                    chained(nc.vector.reciprocal(c[:, 2:4], c[:, 0:2]))
                    chained(nc.vector.tensor_tensor(c[:, 4:5], c[:, 0:1], rsa[:, 1:2], ALU.mult))
                    chained(nc.vector.tensor_tensor(c[:, 5:6], c[:, 1:2], gate, ALU.mult))
                    for i, b in enumerate((b1, b2)):
                        chained(nc.vector.tensor_scalar(b[:, :], b[:, :], c[:, 2 + i:3 + i], MAGIC, ALU.mult, ALU.add))
                        chained(nc.vector.tensor_scalar(b[:, :], b[:, :], MAGIC, 2.0 ** 31 - 1, ALU.subtract, ALU.min))
                        chained(nc.vector.tensor_scalar(b[:, :], b[:, :], -2.0 ** 31, c[:, i:i + 1], ALU.max, ALU.mult))
                    nc.vector.tensor_scalar(b1[:, :], b1[:, :], rsa[:, 1:2], None, ALU.mult)
                    chained(nc.vector.tensor_scalar(b2[:, :], b2[:, :], gate, None, ALU.mult))
                    nc.vector.tensor_tensor(sh.X[:, :, :], sh.X[:, :, :], b2[:, :].unsqueeze(1).to_broadcast([P, NB, D]), ALU.add)
        transpose_tiles(nc, sems, "qfT", KT, lambda k, t: ints[:, t, k * P:(k + 1) * P],
                        lambda t: sh.hT[:, 0, :, bass.ds(t * P, P)], sh.identh[:, :])

        r = sb("r", [P, 2, CT])
        z = sb("z", [P, 2, CT])
        hq = sb("hq", [P, 2, NF, CT], F16)
        NT = CT // P
        Hp = ctx.enter_context(nc.psum_tensor("qf_H", [P, 2, CT], F32))
        O = ctx.enter_context(nc.psum_tensor("qf_O", [P, 2, 2, D], F32))
        s_H, s_r, s_z, s_hq, s_O, s_res = map(sem, ("H", "r", "z", "hq", "O", "res"))
        with nc.Block() as block:
            @block.tensor
            def _(pe):
                def hidden(ch, f):
                    n = ch * NF + f
                    pe.wait_ge(s_r, n + 1)
                    for k in range(KT):
                        last = nc.tensor.matmul(Hp[:, f % 2, :], w1[:, k * F + f * P:k * F + (f + 1) * P],
                                                sh.hT[:, 0, k, bass.ds(ch * CT, CT)], start=k == 0, stop=k == KT - 1)
                    last.then_inc(s_H, 1)

                pe.sem_inc(s_O, 4)
                with pe.Fori(0, T // CT // 2) as pair:
                    for par in range(2):
                        ch = pair * 2 + par
                        for f in range(NF):
                            hidden(ch, f)
                        pe.wait_ge(s_hq, ch * NF + NF)
                        for bank in range(2):
                            pe.wait_ge(s_res, 2 * ch + bank + 1)
                            for i in range(2):
                                t = bank * 2 + i
                                for f in range(NF):
                                    last = nc.tensor.matmul(O[:, bank, i, :], hq[:, par, f, t * P:(t + 1) * P], w2[:, f * D:(f + 1) * D],
                                                            start=f == 0, stop=f == NF - 1)
                            last.then_inc(s_O, 1)

            @block.scalar
            def _(act):
                act.sem_inc(s_r, 2)
                with act.Fori(0, T // CT // 2) as pair:
                    for par in range(2):
                        ch = pair * 2 + par
                        for f in range(NF):
                            n = ch * NF + f
                            act.wait_ge(s_H, n + 1)
                            act.wait_ge(s_z, n + 1)
                            nc.scalar.activation(r[:, f % 2, :], Hp[:, f % 2, :], ACT.Relu, bias=b1[:, f:f + 1], scale=c[:, 4:5]).then_inc(s_r, 1)

            @block.vector
            def _(dve):
                dve.sem_inc(s_z, 2)
                dve.sem_inc(s_res, 2)

                def outputs(ch):
                    for bank in range(2):
                        dve.wait_ge(s_O, 2 * ch + bank + 5)
                        xs = sh.X[:, bass.ds(ch * NT + bank * 2, 2), :]
                        nc.vector.scalar_tensor_tensor(out=xs, in0=O[:, bank, :, :], scalar=c[:, 5:6], in1=xs, op0=ALU.mult,
                                                       op1=ALU.add).then_inc(s_res, 1)

                with dve.Fori(0, T // CT // 2) as pair:
                    for par in range(2):
                        ch = pair * 2 + par
                        dve.wait_ge(s_O, 2 * ch + 2)
                        for f in range(NF):
                            n = ch * NF + f
                            dve.wait_ge(s_r, n + 3)
                            nc.vector.tensor_scalar(z[:, f % 2, :], r[:, f % 2, :], 15.0, MAGIC, ALU.min, ALU.add).then_inc(s_z, 1)
                            dve.wait_ge(s_z, n + 3)
                            nc.vector.tensor_scalar(hq[:, par, f, :], z[:, f % 2, :], MAGIC, None, ALU.subtract).then_inc(s_hq, 1)
                        outputs(ch)


def causal_attention(nc, sems, sh, a, gate):
    NH, HD = 16, 16
    SLOT = 64
    NG = NH // 2
    HE = HD + 1
    SCALE = float(HD) ** -0.5
    with ExitStack() as ctx:
        def sb(n, shape, dt=F32):
            return ctx.enter_context(nc.sbuf_tensor("ca_" + n, shape, dt))

        def sem(n):
            return nc.alloc_semaphore(name="ca_" + n)

        cx = sb("cx", [P, NB, D])
        vx = sb("vx", [P, NB, NH, HE])
        mask = sb("mask", [P, 4, P], BF16)
        maskf = sb("maskf", [P, 4, P])
        qs = sb("qs", [P, 2, NH, SLOT], F16)
        ks = sb("ks", [P, 2, NH, SLOT], F16)
        qT = sb("qT", [P, 2, NG, P], F16)
        kT = sb("kT", [P, 2, NG, P], F16)
        kc = sb("kc", [P, 2, NH, HD])
        m = sb("m", [P, 2, 2, 4])
        d = sb("d", [P, 2, 2, 4, P])
        E = sb("E", [P, 2, 8, P])
        eT = sb("eT", [P, 2, 8, P])
        inv = sb("inv", [P, NH])
        on = sb("on", [P, NH, HD])
        S = ctx.enter_context(nc.psum_tensor("ca_S", [P, 2, 2, 4, P], F32))
        TQ = ctx.enter_context(nc.psum_tensor("ca_TQ", [P, NG, P], F16))
        ET = ctx.enter_context(nc.psum_tensor("ca_ET", [P, 8, P], F32))
        O = ctx.enter_context(nc.psum_tensor("ca_O", [P, 512], F32))
        s_load, s_set, s_set1, s_mask, s_vx, s_qlo, s_klo, s_hi, s_khi, s_T, s_tr, s_S, s_m, s_d, s_E, s_ET, s_eT, s_V, s_inv, s_on, s_res = map(sem, (
            "load", "set", "set1", "mask", "vx", "qlo", "klo", "hi", "khi", "T", "tr", "S", "m", "d", "E", "ET", "eT", "V", "inv", "on", "res"))
        with nc.Block() as block:
            @block.sync
            def _(sp):
                sp.dma_start(cx[:, :, :], a["ctx"].rearrange("b p d -> p b d")).then_inc(s_load, 16)

            @block.gpsimd
            def _(pool):
                nc.gpsimd.memset(maskf[:, :, :], 0.0).then_inc(s_set, 1)
                nc.gpsimd.memset(ks[:, :, :, :], 0.0).then_inc(s_set, 1)
                nc.gpsimd.memset(qs[:, :, :, :], 0.0).then_inc(s_set, 1)
                pool.wait_ge(s_set, 3)
                nc.gpsimd.affine_select(out=maskf[:, :, :], in_=maskf[:, :, :], compare_op=ALU.is_ge, fill=LOW,
                                        base=0, pattern=[[0, 4], [-1, P]], channel_multiplier=1).then_inc(s_mask, 1)
                pool.wait_ge(s_load, 16)
                with pool.Fori(0, NB // 2) as pair:
                    for par in range(2):
                        t = pair * 2 + par
                        k = cx[:, t, :].rearrange("p (h d) -> p h d", d=HD)
                        pool.wait_ge(s_T, 2 * t + 2)
                        for slot in (0, 2):
                            last = nc.gpsimd.tensor_copy(ks[:, par, :, slot * HD:(slot + 1) * HD], k)
                        last.then_inc(s_khi, 1)
                        nc.gpsimd.tensor_copy(kc[:, par, :, :], k).then_inc(s_khi, 1)
                        pool.wait_ge(s_khi, 2 * t + 2)
                        nc.gpsimd.tensor_tensor(ks[:, par, :, HD:2 * HD], kc[:, par, :, :], ks[:, par, :, 0:HD], ALU.subtract).then_inc(s_klo, 1)

            @block.tensor
            def _(pe):
                pe.sem_inc(s_T, 4)
                pe.sem_inc(s_S, 4)
                pe.sem_inc(s_ET, 2)
                pe.sem_inc(s_V, 2)
                pe.wait_ge(s_vx, 2)
                pe.wait_ge(s_set1, 1)

                def scores(t, par, r):
                    n = t * 2 + r
                    pe.wait_ge(s_d, n + 1)
                    for j in range(2):
                        nc.tensor.matmul(S[:, r, j, :, :], sh.ident16[:, :], mask[:, :, :], start=True, stop=False, skip_group_check=True)
                    for i in range(4):
                        for j in range(2):
                            rows = slice(j * SLOT, (j + 1) * SLOT)
                            last = nc.tensor.matmul(S[:, r, j, i, :], qT[rows, par, r * 4 + i, :], kT[rows, par, r * 4 + i, :],
                                                    start=False, stop=True, skip_group_check=True)
                    last.then_inc(s_S, 1)

                def values(t, r):
                    n = t * 2 + r
                    pe.wait_ge(s_E, n + 3)
                    pe.wait_ge(s_eT, n + 1)
                    for i in range(8):
                        last = nc.tensor.transpose(ET[:, i, :], E[:, r, i, :], sh.ident[:, :])
                    last.then_inc(s_ET, 1)
                    pe.wait_ge(s_eT, n + 2)
                    if r == 0:
                        pe.wait_ge(s_res, t + 1)
                    for i in range(8):
                        h = (r * 4 + i % 4) * 2 + i // 4
                        last = nc.tensor.matmul(O[:, h * HE:(h + 1) * HE], eT[:, r, i, :], vx[:, t, h, :], start=True, stop=True,
                                                skip_group_check=True)
                    last.then_inc(s_V, 1)

                with pe.Fori(0, NB // 2) as pair:
                    for par in range(2):
                        t = pair * 2 + par
                        for side, (s_st, stack) in enumerate(((s_qlo, qs), (s_klo, ks))):
                            pe.wait_ge(s_st, t + 1)
                            pe.wait_ge(s_tr, 2 * t + side + 1)
                            for g in range(NG):
                                last = nc.tensor.transpose(TQ[:, g, :], stack[:, par, 2 * g:2 * g + 2, :].rearrange("p h s -> p (h s)"), sh.identh[:, :])
                            last.then_inc(s_T, 1)
                        pe.wait_ge(s_tr, 2 * t + 3)
                        for r in range(2):
                            scores(t, par, r)
                        for r in range(2):
                            values(t, r)

            @block.scalar
            def _(act):
                act.sem_inc(s_tr, 1)
                act.sem_inc(s_eT, 1)
                act.sem_inc(s_E, 2)
                act.wait_ge(s_load, 16)
                nc.scalar.activation(vx[:, :, :, 0:HD].rearrange("p t h d -> p (t h) d"),
                                     cx[:, :, :].rearrange("p t (h d) -> p (t h) d", d=HD), ACT.Copy).then_inc(s_vx, 1)
                act.wait_ge(s_mask, 1)
                nc.scalar.activation(mask[:, :, :], maskf[:, :, :], ACT.Copy).then_inc(s_vx, 1)
                with act.Fori(0, NB // 2) as pair:
                    for par in range(2):
                        t = pair * 2 + par
                        act.wait_ge(s_S, 2 * t + 2)
                        for side, x in enumerate((qT, kT)):
                            act.wait_ge(s_T, 2 * t + side + 5)
                            nc.scalar.activation(x[:, par, :, :], TQ[:, :, :], ACT.Copy).then_inc(s_tr, 1)
                        for r in range(2):
                            n = t * 2 + r
                            act.wait_ge(s_d, n + 3)
                            act.wait_ge(s_ET, n + 1)
                            nc.scalar.activation(E[:, r, :, :], d[:, r, :, :, :].rearrange("p a b c -> p (a b) c"), ACT.Exp, scale=SCALE).then_inc(s_E, 1)
                        for r in range(2):
                            n = t * 2 + r
                            act.wait_ge(s_ET, n + 3)
                            act.wait_ge(s_V, n + 1)
                            nc.scalar.activation(eT[:, r, :, :], ET[:, :, :], ACT.Copy).then_inc(s_eT, 1)

            @block.vector
            def _(dve):
                dve.sem_inc(s_d, 2)
                dve.sem_inc(s_res, 1)
                dve.wait_ge(s_set, 3)
                nc.vector.memset(vx[:, :, :, HD:HE], 1.0).then_inc(s_set1, 1)

                def stack(t, par):
                    q = sh.H[:, t, :].rearrange("p (h d) -> p h d", d=HD)
                    dve.wait_ge(s_T, 2 * t + 1)
                    for slot in (0, 1):
                        last = copy_indexed(nc, qs[:, par, :, slot * HD:(slot + 1) * HD], q)
                    last.then_inc(s_hi, 1)
                    dve.wait_ge(s_hi, t + 1)
                    nc.vector.tensor_tensor(qs[:, par, :, 2 * HD:3 * HD], q, qs[:, par, :, 0:HD], ALU.subtract).then_inc(s_qlo, 1)

                def output(t):
                    o = O[:, 0:NH * HE].rearrange("p (h d) -> p h d", d=HE)
                    dve.wait_ge(s_V, 2 * t + 4)
                    nc.vector.reciprocal(inv[:, :], o[:, :, HD]).then_inc(s_inv, 1)
                    dve.wait_ge(s_inv, t + 1)
                    nc.vector.tensor_tensor(on[:, :, :], o[:, :, 0:HD], inv[:, :].unsqueeze(2).to_broadcast([P, NH, HD]),
                                            ALU.mult).then_inc(s_on, 1)
                    dve.wait_ge(s_on, t + 1)
                    nc.vector.scalar_tensor_tensor(out=sh.X[:, t, :], in0=on[:, :, :].rearrange("p h d -> p (h d)"), scalar=gate,
                                                   in1=sh.X[:, t, :], op0=ALU.mult, op1=ALU.add).then_inc(s_res, 1)

                def tile(t, par, last):
                        for r in range(2):
                            n = t * 2 + r
                            dve.wait_ge(s_S, n + 5)
                            nc.vector.reduce_max(m[:, r, :, :], S[:, r, :, :, :], axis=AXX).then_inc(s_m, 1)
                            dve.wait_ge(s_m, n + 1)
                            dve.wait_ge(s_E, n + 1)
                            nc.vector.tensor_tensor(d[:, r, :, :, :], S[:, r, :, :, :], m[:, r, :, :].unsqueeze(3).to_broadcast([P, 2, 4, P]),
                                                    ALU.subtract).then_inc(s_d, 1)
                        if not last:
                            stack(t + 1, 1 - par)
                        output(t)

                stack(0, 0)
                with dve.Fori(0, NB // 2 - 1) as pair:
                    for par in range(2):
                        tile(pair * 2 + par, par, False)
                tile(NB - 2, 0, False)
                tile(NB - 1, 1, True)


def ternary_ffn(nc, sems, sh, a, gate):
    F = 1024
    NF = F // P
    with ExitStack() as ctx:
        def sb(n, shape, dt=F32, where=ctx):
            return where.enter_context(nc.sbuf_tensor("tf_" + n, shape, dt))

        def sem(n):
            return nc.alloc_semaphore(name="tf_" + n)

        w1 = sb("w1", [P, KT, F], F16)
        w2 = sb("w2", [P, NF, D], F16)
        s1b = sb("s1b", [P, F])
        s2b = sb("s2b", [P, D])
        inv1 = sb("inv1", [P, NB])
        ints = sb("ints", [P, NB, D], F16)
        with ExitStack() as inner:
            f1 = sb("f1", [P, KT, F], F32, inner)
            f2 = sb("f2", [P, NF, D], F32, inner)
            Z = sb("Z", [P, NB, D], F32, inner)
            ab = sb("ab", [P, KT * F], F32, inner)
            ab2 = sb("ab2", [P, NF * D], F32, inner)
            r1 = sb("r1", [P, F], F32, inner)
            r2 = sb("r2", [P, D], F32, inner)
            am = sb("am", [P, NB], F32, inner)
            ra = sb("ra", [P, NB], F32, inner)
            ones = sb("ones", [P, P], F32, inner)
            M1 = inner.enter_context(nc.psum_tensor("tf_M1", [P, F], F32))
            M2 = inner.enter_context(nc.psum_tensor("tf_M2", [P, 512], F32))
            s_load, s_abs, s_ones, s_mean, s_c = map(sem, ("load", "abs", "ones", "mean", "chain"))
            with nc.Block() as block:
                @block.sync
                def _(sp):
                    sp.dma_start(f1[:, :, :].rearrange("p k n -> p (k n)"), a["tf_w1"]).then_inc(s_load, 16)
                    sp.dma_start(f2[:, :, :].rearrange("p k n -> p (k n)"), a["tf_w2"]).then_inc(s_load, 16)

                @block.scalar
                def _(act):
                    act.wait_ge(s_load, 32)
                    nc.scalar.activation(ab[:, :], f1[:, :, :].rearrange("p k n -> p (k n)"), ACT.Abs).then_inc(s_abs, 1)
                    nc.scalar.activation(ab2[:, :], f2[:, :, :].rearrange("p k n -> p (k n)"), ACT.Abs).then_inc(s_abs, 1)

                @block.tensor
                def _(pe):
                    pe.wait_ge(s_ones, 1)
                    pe.wait_ge(s_abs, 2)
                    for half in range(2):
                        for k in range(KT):
                            nc.tensor.matmul(M1[:, half * 512:(half + 1) * 512], ones[:, :],
                                             ab[:, k * F + half * 512:k * F + (half + 1) * 512], start=k == 0, stop=k == KT - 1)
                    for k in range(NF):
                        last = nc.tensor.matmul(M2[:, 0:D], ones[:, :], ab2[:, k * D:(k + 1) * D], start=k == 0, stop=k == NF - 1)
                    last.then_inc(s_mean, 1)

                @block.vector
                def _(dve):
                    chained = chain_on(dve, s_c)
                    nc.vector.memset(ones[:, :], 1.0).then_inc(s_ones, 1)
                    chained(nc.vector.tensor_reduce(out=am[:, :], in_=sh.H[:, :, :], axis=AXX, op=ALU.max, apply_absolute_value=True))
                    chained(nc.vector.tensor_scalar(inv1[:, :], am[:, :], 1e-5, 1.0 / 127.0, ALU.max, ALU.mult))
                    chained(nc.vector.reciprocal(ra[:, :], inv1[:, :]))
                    chained(nc.vector.tensor_tensor(Z[:, :, :], sh.H[:, :, :], ra[:, :].unsqueeze(2).to_broadcast([P, NB, D]), ALU.mult))
                    chained(nc.vector.tensor_scalar(Z[:, :, :], Z[:, :, :], MAGIC, MAGIC, ALU.add, ALU.subtract))
                    nc.vector.tensor_scalar(ints[:, :, :], Z[:, :, :], 127.0, -128.0, ALU.min, ALU.max)
                    dve.wait_ge(s_mean, 1)
                    for M, s, r, f, w, n in ((M1[:, :], s1b, r1, f1, w1, KT), (M2[:, 0:D], s2b, r2, f2, w2, NF)):
                        width = [P, n, s.shape[1]]
                        chained(nc.vector.tensor_scalar(s[:, :], M, 1.0 / (n * P), 1e-5, ALU.mult, ALU.max))
                        chained(nc.vector.reciprocal(r[:, :], s[:, :]))
                        chained(nc.vector.tensor_tensor(f[:, :, :], f[:, :, :], r[:, :].unsqueeze(1).to_broadcast(width), ALU.mult))
                        chained(nc.vector.tensor_scalar(f[:, :, :], f[:, :, :], MAGIC, MAGIC, ALU.add, ALU.subtract))
                        nc.vector.tensor_scalar(w[:, :, :], f[:, :, :], 1.0, -1.0, ALU.min, ALU.max)
        transpose_tiles(nc, sems, "tfT", KT, lambda k, t: ints[:, t, k * P:(k + 1) * P],
                        lambda t: sh.hT[:, 0, :, bass.ds(t * P, P)], sh.identh[:, :])

        h = sb("h", [P, 2, F])
        g = sb("g", [P, 2, F])
        z = sb("z", [P, 2, F])
        gi = sb("gi", [P, 2, F], F16)
        gT = sb("gT", [P, 2, NF, P], F16)
        am2 = sb("am2", [P, 2])
        inv2 = sb("inv2", [P, 2])
        ra2 = sb("ra2", [P, 2])
        ga2 = sb("ga2", [P, 2])
        tmp = sb("tmp", [P, 2, D])
        Hp = ctx.enter_context(nc.psum_tensor("tf_H", [P, 2, F], F32))
        TP = ctx.enter_context(nc.psum_tensor("tf_TP", [P, 2, NF, P], F16))
        O = ctx.enter_context(nc.psum_tensor("tf_O", [P, 2, 512], F32))
        s_H, s_h, s_g, s_c, s_gi, s_T, s_gT, s_O, s_tmp, s_res = map(sem, ("H", "h", "g", "chain2", "gi", "T", "gT", "O", "tmp", "res"))
        with nc.Block() as block:
            @block.tensor
            def _(pe):
                pe.sem_inc(s_T, 2)
                pe.sem_inc(s_O, 2)

                def hidden(t, par):
                    pe.wait_ge(s_h, t + 1)
                    for half in range(2):
                        for k in range(KT):
                            last = nc.tensor.matmul(Hp[:, par, half * 512:(half + 1) * 512], sh.hT[:, 0, k, bass.ds(t * P, P)],
                                                    w1[:, k, half * 512:(half + 1) * 512], start=k == 0, stop=k == KT - 1)
                    last.then_inc(s_H, 1)

                def down(t, par):
                    pe.wait_ge(s_gi, t + 3)
                    pe.wait_ge(s_gT, t + 1)
                    for f in range(NF):
                        last = nc.tensor.transpose(TP[:, par, f, :], gi[:, par, f * P:(f + 1) * P], sh.identh[:, :])
                    last.then_inc(s_T, 1)
                    pe.wait_ge(s_gT, t + 3)
                    pe.wait_ge(s_res, t + 1)
                    for f in range(NF):
                        last = nc.tensor.matmul(O[:, par, 0:D], gT[:, par, f, :], w2[:, f, :], start=f == 0, stop=f == NF - 1)
                    last.then_inc(s_O, 1)

                with pe.Fori(0, NB // 2) as pair:
                    hidden(pair * 2, 0)
                    hidden(pair * 2 + 1, 1)
                    down(pair * 2, 0)
                    down(pair * 2 + 1, 1)

            @block.scalar
            def _(act):
                act.sem_inc(s_gT, 2)
                with act.Fori(0, NB // 2) as pair:
                    for par in range(2):
                        t = pair * 2 + par
                        act.wait_ge(s_h, t + 3)
                        act.wait_ge(s_gi, t + 1)
                        nc.scalar.activation(g[:, par, :], h[:, par, :], ACT.Gelu_apprx_tanh).then_inc(s_g, 1)
                    for par in range(2):
                        t = pair * 2 + par
                        act.wait_ge(s_T, t + 3)
                        act.wait_ge(s_O, t + 1)
                        nc.scalar.activation(gT[:, par, :, :], TP[:, par, :, :], ACT.Copy).then_inc(s_gT, 1)

            @block.vector
            def _(dve):
                dve.sem_inc(s_h, 2)
                dve.sem_inc(s_gi, 2)
                dve.sem_inc(s_res, 2)
                with dve.Fori(0, NB // 2) as pair:
                    for par in range(2):
                        t = pair * 2 + par
                        dve.wait_ge(s_H, t + 1)
                        nc.vector.scalar_tensor_tensor(out=h[:, par, :], in0=Hp[:, par, :], scalar=inv1[:, bass.ds(t, 1)],
                                                       in1=s1b[:, :], op0=ALU.mult, op1=ALU.mult).then_inc(s_h, 1)
                    for par in range(2):
                        t = pair * 2 + par
                        i = slice(par, par + 1)
                        steps = iter(range(1, 9))

                        def chained(ins):
                            ins.then_inc(s_c, 1)
                            dve.wait_ge(s_c, t * 5 + next(steps))

                        dve.wait_ge(s_g, t + 1)
                        chained(nc.vector.tensor_reduce(out=am2[:, i], in_=g[:, par, :], axis=AXX, op=ALU.max, apply_absolute_value=True))
                        chained(nc.vector.tensor_scalar(inv2[:, i], am2[:, i], 1e-5, 1.0 / 127.0, ALU.max, ALU.mult))
                        nc.vector.tensor_tensor(ga2[:, i], inv2[:, i], gate, ALU.mult)
                        chained(nc.vector.reciprocal(ra2[:, i], inv2[:, i]))
                        chained(nc.vector.tensor_scalar(z[:, par, :], g[:, par, :], ra2[:, i], MAGIC, ALU.mult, ALU.add))
                        chained(nc.vector.tensor_scalar(z[:, par, :], z[:, par, :], MAGIC, 127.0, ALU.subtract, ALU.min))
                        dve.wait_ge(s_T, t + 1)
                        nc.vector.tensor_scalar(gi[:, par, :], z[:, par, :], -128.0, None, ALU.max).then_inc(s_gi, 1)
                    for par in range(2):
                        t = pair * 2 + par
                        dve.wait_ge(s_O, t + 3)
                        nc.vector.scalar_tensor_tensor(out=tmp[:, par, :], in0=O[:, par, 0:D], scalar=ga2[:, par:par + 1],
                                                       in1=s2b[:, :], op0=ALU.mult, op1=ALU.mult).then_inc(s_tmp, 1)
                        dve.wait_ge(s_tmp, t + 1)
                        nc.vector.tensor_tensor(sh.X[:, t, :], sh.X[:, t, :], tmp[:, par, :], ALU.add).then_inc(s_res, 1)


def store(nc, sems, sh, out):
    s_out = nc.alloc_semaphore(name="store_out")
    with nc.Block() as block:
        @block.sync
        def _(sp):
            sp.dma_start(out.rearrange("b p d -> p b d"), sh.X[:, :, :]).then_inc(s_out, 16)
            sp.wait_ge(s_out, 16)


@contextmanager
def own_semaphores(nc):
    before = nc.snapshot_sems()
    yield
    nc.clear_and_free_semaphores(nc.allocated_since(before))
    nc.all_engine_barrier()


def program(nc, a, out):
    with ExitStack() as sems:
        sh = make_shared(nc, sems, a["x"], a["g_xattn"], a["g_ffn"])
        with own_semaphores(nc):
            layernorm(nc, sems, sh, "ln0")
            long_convolution(nc, sh, sems, a["ctx_flip"], a["ctxT_flip"], a["ssm_pad"], a["ssm_D"])
        sh.hT = sems.enter_context(nc.sbuf_tensor("hT", [P, 2, KT, T], F16))
        weights_T = nc.dram_tensor("weights_T", [MOE1.rows, T], F32, kind="Internal").ap()

        def mixture(m, layer):
            layernorm(nc, sems, sh, f"ln_moe{layer}")
            split_transpose(nc, sems, sh, f"st_moe{layer}")
            with ExitStack() as wide:
                sh.W = wide.enter_context(nc.sbuf_tensor(f"W{layer}", [P, 2, m.tiles * TW], F16))
                load_expert_weights(nc, sems, sh, m, a[f"moe{layer}_w"], f"moe{layer}w")
                route(nc, sems, sh, m, a[f"moe{layer}_router"], weights_T[0:m.rows, :], f"moe{layer}r")
                experts(nc, sems, sh, m, weights_T, sh.gates[:, 2 * layer + 1:2 * layer + 2], f"moe{layer}")

        with own_semaphores(nc):
            mixture(MOE0, 0)
        with own_semaphores(nc):
            layernorm(nc, sems, sh, "ln2")
            split_transpose(nc, sems, sh, "st2")
            rms_attention(nc, sems, sh, a["ctxT"], {x: a["rms_w" + x] for x in "qkv"}, sh.gates[:, 2:3])
        with own_semaphores(nc):
            mixture(MOE1, 1)
        with own_semaphores(nc):
            layernorm(nc, sems, sh, "ln4")
            split_transpose(nc, sems, sh, "st4")
            quantised_attention(nc, sems, sh, a, sh.gates[:, 4:5])
        with own_semaphores(nc):
            layernorm(nc, sems, sh, "ln5")
            quantised_ffn(nc, sems, sh, a, sh.gates[:, 5:6])
        with own_semaphores(nc):
            layernorm(nc, sems, sh, "ln6")
            causal_attention(nc, sems, sh, a, sh.gates[:, 6:7])
        with own_semaphores(nc):
            layernorm(nc, sems, sh, "ln7")
            ternary_ffn(nc, sems, sh, a, sh.gates[:, 7:8])
        store(nc, sems, sh, out)


def stationary(w):
    return w.T.reshape(-1, P, w.shape[0]).transpose(1, 0, 2).reshape(P, -1)


def by_tile(gate, up, down):
    F = down.shape[0] // P
    cols = [w.reshape(KT, P, F, P).transpose(1, 2, 0, 3).reshape(P, F, KT * P) for w in (gate, up)]
    cols.append(down.reshape(F, P, D).transpose(1, 0, 2))
    return np.concatenate(cols, axis=2).reshape(P, F * TW)


def expert_layouts(n):
    gu = n["L0_ffn_gate_up_proj"]
    I = gu.shape[1] // 2
    none = np.zeros((P - I, D), gu.dtype)
    gate0 = np.concatenate([gu[:, :I].reshape(-1, D), n["L0_ffn_shared_gate_w"], none]).T
    up0 = np.concatenate([gu[:, I:].reshape(-1, D), n["L0_ffn_shared_up_w"], none]).T
    down0 = np.concatenate([n["L0_ffn_down_proj"].transpose(0, 2, 1).reshape(-1, D), n["L0_ffn_shared_down_w"].T, none])
    router0 = np.concatenate([n["L0_ffn_router_w"], n["L0_ffn_shared_expert_gate_w"]]).T
    w1 = n["L1_ffn_w1"]
    F = w1.shape[2] // 2
    gate1 = np.concatenate([w1[:, :, :F].transpose(1, 0, 2).reshape(D, -1), n["L1_ffn_w_gate"]], axis=1)
    up1 = np.concatenate([w1[:, :, F:].transpose(1, 0, 2).reshape(D, -1), n["L1_ffn_w_up"]], axis=1)
    down1 = np.concatenate([n["L1_ffn_w2"].reshape(-1, D), n["L1_ffn_w_down"]])
    return {
        "moe0_w": by_tile(gate0, up0, down0), "moe0_router": router0.reshape(KT, P, -1).transpose(1, 0, 2),
        "moe1_w": by_tile(gate1, up1, down1), "moe1_router": n["L1_ffn_router_w"].reshape(KT, P, -1).transpose(1, 0, 2),
    }


def kernel(**inputs):
    import concourse.bacc as bacc
    from concourse.bass_utils import run_bass_kernel_spmd

    n = {k: np.asarray(v) for k, v in inputs.items()}
    c = n["ctx_2048"]
    ssm = n["L0_xattn_ssm_kernel"]
    arrays = {
        "x": n["x"], "g_xattn": n["g_xattn"], "g_ffn": n["g_ffn"],
        "ctx_flip": c.reshape(NB, P, KT, P)[:, :, :, ::-1].reshape(NB, P, D),
        "ctxT_flip": c.reshape(NB, P, KT, P)[:, :, :, ::-1].transpose(3, 0, 2, 1),
        "ssm_pad": np.concatenate([np.zeros((16, P - 1), ssm.dtype), ssm], axis=1),
        "ssm_D": n["L0_xattn_D"],
    }
    arrays |= expert_layouts(n)
    kv = np.concatenate([n["L1_xattn_Wk"], n["L1_xattn_Wv"]])
    arrays |= {
        "ctxT": stationary(c.reshape(T, D)),
        "rms_wq": stationary(n["L1_xattn_Wq"]), "rms_wk": stationary(kv[0::2]), "rms_wv": stationary(kv[1::2]),
    }
    wkv, bkv = n["L2_xattn_Wkv"], n["L2_xattn_bkv"]
    arrays |= {
        "qa_wq": stationary(n["L2_xattn_Wq"].T), "qa_wk": stationary(wkv[:, :D].T), "qa_wv": stationary(wkv[:, D:].T),
        "qa_wp": stationary(n["L2_xattn_Wp"].T), "qa_bq": n["L2_xattn_bq"], "qa_bk": bkv[:D],
        "qa_bv": bkv[D:].reshape(KT, P).T, "qa_bp": n["L2_xattn_bp"],
    }
    arrays |= {
        "qf_w1": stationary(n["L2_ffn_W1"]), "qf_w2": stationary(n["L2_ffn_W2"]),
        "qf_b1": n["L2_ffn_b1"].reshape(-1, P).T, "qf_b2": n["L2_ffn_b2"], "qf_s1": n["L2_ffn_s_act1"], "qf_s2": n["L2_ffn_s_act2"],
        "ctx": c, "tf_w1": stationary(n["L3_ffn_w1"]), "tf_w2": stationary(n["L3_ffn_w2"]),
    }
    arrays = {f"in_{k}": np.ascontiguousarray(v) for k, v in arrays.items()}
    nc = bacc.Bacc("TRN2", target_bir_lowering=False, num_devices=1)
    args = {k[3:]: nc.dram_tensor(k, v.shape, mybir.dt.from_np(v.dtype), kind="ExternalInput").ap() for k, v in arrays.items()}
    out = nc.dram_tensor("out_0_dram", (NB, P, D), F32, kind="ExternalOutput").ap()
    program(nc, args, out)
    r = run_bass_kernel_spmd(nc, [arrays], core_ids=[0])
    return r.results[0]["out_0_dram"]
```

```python
from contextlib import ExitStack, contextmanager
import numpy as np
import concourse.bass as bass
from concourse import mybir


F32 = mybir.dt.float32
F16 = mybir.dt.float16
BF16 = mybir.dt.bfloat16
ALU = mybir.AluOpType
ACT = mybir.ActivationFunctionType
AXX = mybir.AxisListType.X

P = 128
NB = 16
D = 256
KT = D // P
T = NB * P
EPS = 1e-5


class Shared:
    pass


def make_shared(nc, ctx, x, g_xattn, g_ffn):
    sh = Shared()

    def sb(n, shape, dt=F32):
        return ctx.enter_context(nc.sbuf_tensor(n, shape, dt))

    sh.X = sb("X", [P, NB, D])
    sh.H = sb("H", [P, NB, D])
    sh.gates = sb("gates", [P, 8])
    graw = sb("graw", [P, 8])
    sh.eps = sb("eps", [P, 1])
    sh.ident = sb("ident", [P, P])
    sh.ident16 = sb("ident16", [P, P], BF16)
    sh.identh = sb("identh", [P, P], F16)
    s_load = nc.alloc_semaphore(name="setup_load")
    s_ident = nc.alloc_semaphore(name="setup_ident")
    s_set = nc.alloc_semaphore(name="setup_set")
    with nc.Block() as block:
        @block.sync
        def _(sp):
            sp.dma_start(sh.X[:, :, :], x.rearrange("b p d -> p b d")).then_inc(s_load, 16)
            sp.dma_start(graw[:, 0:4], g_xattn.partition_broadcast(P)).then_inc(s_load, 16)
            sp.dma_start(graw[:, 4:8], g_ffn.partition_broadcast(P)).then_inc(s_load, 16)
            sp.wait_ge(s_load, 48)

        @block.gpsimd
        def _(pool):
            nc.gpsimd.memset(sh.eps[:, :], EPS).then_inc(s_set, 1)
            nc.gpsimd.memset(sh.ident[:, :], 0.0).then_inc(s_set, 1)
            pool.wait_ge(s_set, 2)
            nc.gpsimd.affine_select(out=sh.ident[:, :], in_=sh.ident[:, :], compare_op=ALU.not_equal, fill=1.0,
                                    base=0, pattern=[[-1, P]], channel_multiplier=1).then_inc(s_ident, 1)

        @block.vector
        def _(dve):
            dve.wait_ge(s_ident, 1)
            nc.vector.tensor_copy(sh.ident16[:, :], sh.ident[:, :])
            nc.vector.tensor_copy(sh.identh[:, :], sh.ident[:, :])

        @block.scalar
        def _(act):
            act.wait_ge(s_load, 48)
            nc.scalar.activation(sh.gates[:, 0::2], graw[:, 0:4], ACT.Tanh)
            nc.scalar.activation(sh.gates[:, 1::2], graw[:, 4:8], ACT.Tanh)
    return sh


class Layernorm:

    def __init__(self, nc, ctx, sh, name):
        self.nc, self.sh = nc, sh
        self.s_stats, self.s_mv, self.s_std, self.s_rstd, self.s_norm = (
            nc.alloc_semaphore(name=f"{name}_{x}") for x in ("stats", "mv", "std", "rstd", "norm"))
        self.stats = ctx.enter_context(nc.sbuf_tensor(name + "_stats", [P, NB, 6], F32))
        self.mv = ctx.enter_context(nc.sbuf_tensor(name + "_mv", [P, NB, 2], F32))
        self.std = ctx.enter_context(nc.sbuf_tensor(name + "_std", [P, NB], F32))
        self.rstd = ctx.enter_context(nc.sbuf_tensor(name + "_rstd", [P, NB], F32))

    def statistics(self, dve):
        nc = self.nc
        with dve.Fori(0, NB) as t:
            nc.vector.bn_stats(self.stats[:, bass.ds(t, 1), :], self.sh.X[:, bass.ds(t, 1), :]).then_inc(self.s_stats, 1)
        dve.wait_ge(self.s_stats, NB)
        for t in range(NB):
            nc.vector.bn_aggr(self.mv[:, t, :], self.stats[:, t, :]).then_inc(self.s_mv, 1)
        dve.wait_ge(self.s_std, 1)
        nc.vector.reciprocal(self.rstd[:, :], self.std[:, :]).then_inc(self.s_rstd, 1)
        dve.wait_ge(self.s_rstd, 1)

    def tile(self, t):
        self.nc.vector.tensor_scalar(self.sh.H[:, bass.ds(t, 1), :], self.sh.X[:, bass.ds(t, 1), :],
                                     self.mv[:, bass.ds(t, 1), 0], self.rstd[:, bass.ds(t, 1)],
                                     ALU.subtract, ALU.mult).then_inc(self.s_norm, 1)

    def vector(self, dve):
        self.statistics(dve)
        with dve.Fori(0, NB) as t:
            self.tile(t)

    def scalar(self, act):
        act.wait_ge(self.s_mv, NB)
        self.nc.scalar.activation(self.std[:, :], self.mv[:, :, 1], ACT.Sqrt, bias=self.sh.eps[:, 0:1]).then_inc(self.s_std, 1)

    def whole(self, eng):
        eng.wait_ge(self.s_norm, NB)


def long_convolution(nc, sh, sems, ctx_flip, ctxT_flip, ssm_pad, ssm_D):
    NH, HD = 16, 8
    W = D + P
    HG = 2
    NG = NH // HG
    R = 3 * HD
    with ExitStack() as ctx:
        def sb(n, shape, dt=F32):
            return ctx.enter_context(nc.sbuf_tensor("conv_" + n, shape, dt))

        def sem(n):
            return nc.alloc_semaphore(name="conv_" + n)

        toep = sb("toep", [P, NH, W])
        anti = sb("anti", [P, P])
        dvals = sb("dvals", [P, NH])
        kf = sb("kf", [P, NB, D])
        vt = sb("vt", [P, NB, KT, P])
        parts = sb("parts", [P, 4, NB, D], F16)
        qst = sb("qst", [R, 2, NH, D], F16)
        kst = sb("kst", [R, 2, NH, D], F16)
        vpad = sb("vpad", [P, 2, KT, NH, P])
        A = sb("A", [P, 2, HG, W])
        rows = nc.dram_tensor("conv_rows", [4, NB, P, D], F16, kind="Internal").ap()
        s_rows = sem("rows")
        gate = sh.gates[:, 0:1]
        S = ctx.enter_context(nc.psum_tensor("conv_S", [P, 2, HG, 512], F32))
        Y = ctx.enter_context(nc.psum_tensor("conv_Y", [P, 2, 512], F32))
        s_load, s_zero, s_anti, s_toep = sem("load"), sem("zero"), sem("anti"), sem("toep")
        s_hi, s_lo = sem("hi"), sem("lo")
        s_stack = [sem("stack0"), sem("stack1")]
        s_vpad = sem("vpad")
        s_S, s_A, s_Y, s_res = sem("S"), sem("A"), sem("Y"), sem("res")
        norm = Layernorm(nc, ctx, sh, "conv_ln")
        with nc.Block() as block:
            @block.sync
            def _(sp):
                sp.dma_start(kf[:, :, :], ctx_flip.rearrange("b p d -> p b d")).then_inc(s_load, 16)
                sp.dma_start(vt[:, :, :, :], ctxT_flip).then_inc(s_load, 16)
                for h in range(NH):
                    sp.dma_start(toep[:, h, 0:D], bass.AP(ssm_pad.tensor, h * (P - 1 + D), [[1, P], [1, D]])).then_inc(s_load, 16)
                sp.dma_start(dvals[:, :], ssm_D.partition_broadcast(P)).then_inc(s_load, 16)
                sp.wait_ge(s_hi, 2)
                sp.wait_ge(s_lo, 2)
                for part in range(4):
                    sp.dma_start(rows[part, :, :, :].rearrange("b p l -> p b l"), parts[:, part, :, :]).then_inc(s_rows, 16)
                sp.wait_ge(s_rows, 64)
                with sp.Fori(0, NB // 2) as pair:
                    for par in range(2):
                        b = pair * 2 + par
                        sp.wait_ge(s_S, b * NG + NG)
                        for stack, order in ((qst, (0, 0, 1)), (kst, (2, 3, 2))):
                            for r, part in enumerate(order):
                                sp.dma_start(stack[r * HD:(r + 1) * HD, par, :, :],
                                             rows[part, b, :, :].rearrange("(h i) l -> i h l", i=HD)).then_inc(s_stack[par], 16)

            @block.scalar
            def _(act):
                norm.scalar(act)
                norm.whole(act)
                nc.scalar.activation(parts[:, 0, :, :], sh.H[:, :, :], ACT.Copy).then_inc(s_hi, 1)
                act.wait_ge(s_load, 16 * (NH + 3))
                nc.scalar.activation(parts[:, 2, :, :], kf[:, :, :], ACT.Copy).then_inc(s_hi, 1)

            @block.gpsimd
            def _(pool):
                nc.gpsimd.memset(vpad[:, :, :, :, :], 0.0).then_inc(s_zero, 1)
                nc.gpsimd.memset(anti[:, :], 0.0).then_inc(s_zero, 1)
                pool.wait_ge(s_zero, 2)
                nc.gpsimd.affine_select(out=anti[:, :], in_=anti[:, :], compare_op=ALU.not_equal, fill=1.0,
                                        base=-(P - 1), pattern=[[1, P]], channel_multiplier=1).then_inc(s_anti, 1)
                pool.wait_ge(s_load, 16 * (NH + 3))
                with pool.Fori(0, NB // 2) as pair:
                    for par in range(2):
                        b = pair * 2 + par
                        pool.wait_ge(s_Y, b * NG + NG)
                        for mt in range(KT):
                            flat = vpad[:, par, mt, :, :].rearrange("p h c -> p (h c)")
                            dst = bass.AP(flat.tensor, flat.offset, [flat.ap[0], [P + HD, NH], [1, HD]])
                            nc.gpsimd.tensor_copy(dst, vt[:, b, mt, :].rearrange("p (h j) -> p h j", j=HD)).then_inc(s_vpad, 1)

            @block.vector
            def _(dve):
                dve.sem_inc(s_A, 2)
                dve.sem_inc(s_res, 2)
                norm.vector(dve)
                dve.wait_ge(s_hi, 1)
                nc.vector.tensor_tensor(parts[:, 1, :, :], sh.H[:, :, :], parts[:, 0, :, :], ALU.subtract).then_inc(s_lo, 1)
                dve.wait_ge(s_hi, 2)
                nc.vector.tensor_tensor(parts[:, 3, :, :], kf[:, :, :], parts[:, 2, :, :], ALU.subtract).then_inc(s_lo, 1)
                dve.wait_ge(s_load, 16 * (NH + 3))
                dve.wait_ge(s_anti, 1)
                for h in range(NH):
                    nc.vector.scalar_tensor_tensor(out=toep[:, h, 0:P], in0=anti[:, :], scalar=dvals[:, h:h + 1],
                                                   in1=toep[:, h, 0:P], op0=ALU.mult, op1=ALU.add).then_inc(s_toep, 1)
                dve.wait_ge(s_toep, NH)
                nc.vector.tensor_copy(toep[:, :, D:W], toep[:, :, 0:P]).then_inc(s_toep, 1)
                dve.wait_ge(s_toep, NH + 1)
                with dve.Fori(0, NB // 2) as pair:
                    for par in range(2):
                        b = pair * 2 + par
                        for g in range(NG):
                            k = b * NG + g
                            dve.wait_ge(s_S, k + 2 * NG + 1)
                            dve.wait_ge(s_Y, k + 2 * NG - 1)
                            nc.vector.tensor_tensor(A[:, g % 2, :, :], S[:, g % 2, :, 0:W],
                                                    toep[:, g * HG:(g + 1) * HG, :], ALU.mult).then_inc(s_A, 1)
                        dve.wait_ge(s_Y, b * NG + 3 * NG)
                        nc.vector.scalar_tensor_tensor(out=sh.X[:, b, :], in0=Y[:, par, 0:D], scalar=gate,
                                                       in1=sh.X[:, b, :], op0=ALU.mult, op1=ALU.add).then_inc(s_res, 1)

            @block.tensor
            def _(pe):
                pe.sem_inc(s_S, 2 * NG)
                pe.sem_inc(s_Y, 2 * NG)

                def scores(b, par, g):
                    k = b * NG + g
                    pe.wait_ge(s_A, k + 1)
                    for i in range(HG):
                        h = g * HG + i
                        nc.tensor.matmul(S[:, g % 2, i, 0:D], kst[:, par, h, 0:P], qst[:, par, h, :], start=True, stop=True)
                        last = nc.tensor.matmul(S[:, g % 2, i, D:W], kst[:, par, h, P:D], qst[:, par, h, P:D], start=True, stop=True)
                    last.then_inc(s_S, 1)

                def values(b, par, g):
                    pe.wait_ge(s_A, b * NG + g + 3)
                    for i in range(HG):
                        h = g * HG + i
                        nc.tensor.matmul(Y[:, par, 0:D], vpad[:, par, 0, h, :], A[:, g % 2, i, 0:D], start=h == 0, stop=False)
                        last = nc.tensor.matmul(Y[:, par, P:D], vpad[:, par, 1, h, :], A[:, g % 2, i, D:W], start=False, stop=h == NH - 1)
                    last.then_inc(s_Y, 1)

                with pe.Fori(0, NB // 2) as pair:
                    for par in range(2):
                        b = pair * 2 + par
                        pe.wait_ge(s_stack[par], pair * 96 + 96)
                        scores(b, par, 0)
                        pe.wait_ge(s_vpad, b * 2 + 2)
                        pe.wait_ge(s_res, b + 1)
                        for g in range(NG):
                            if g + 1 < NG:
                                scores(b, par, g + 1)
                            values(b, par, g)


def copy_indexed(nc, out, in_):
    return nc.vector.tensor_scalar(out, in_, 1.0, None, ALU.mult)


class Transposed:
    PAIRS = NB // 2

    def __init__(self, nc, ctx, sh, name, norm=None):
        self.nc, self.sh, self.norm = nc, sh, norm
        self.s_hi, self.s_lo, self.s_T, self.s_even, self.s_odd = (
            nc.alloc_semaphore(name=f"{name}_{n}") for n in ("hi", "lo", "T", "even", "odd"))
        self.parts = ctx.enter_context(nc.sbuf_tensor(name + "_parts", [P, 2, 2, 2, D], F16))
        self.TP = ctx.enter_context(nc.psum_tensor(name + "_TP", [P, 2, 2, 8 * P], F16))

    def in_pairs(self, eng, ahead, behind):
        ahead(0, 0)
        with eng.Fori(0, self.PAIRS // 2 - 1) as q:
            for i in range(2):
                ahead(q * 2 + i + 1, (i + 1) % 2)
                behind(q * 2 + i, i)
        ahead(self.PAIRS - 1, 1)
        behind(self.PAIRS - 2, 0)
        behind(self.PAIRS - 1, 1)

    def target(self, p, par):
        return self.sh.hT[:, :, :, bass.ds((p * 2 + par) * P, P)]

    def transposes(self, slot, par):
        return self.TP[:, slot, par, 0:2 * KT * P].rearrange("p (a k c) -> p a k c", a=2, k=KT)

    def vector(self, dve):
        nc, sh = self.nc, self.sh
        if self.norm:
            self.norm.statistics(dve)
        dve.sem_inc(self.s_odd, 2)

        def ahead(p, slot):
            if self.norm:
                for par in range(2):
                    self.norm.tile(p * 2 + par)
            for par in range(2):
                t = p * 2 + par
                dve.wait_ge(self.s_hi, t + 1)
                nc.vector.tensor_tensor(self.parts[:, slot, par, 1, :], sh.H[:, t, :], self.parts[:, slot, par, 0, :],
                                        ALU.subtract).then_inc(self.s_lo, 1)

        def behind(p, slot):
            dve.wait_ge(self.s_T, p * 2 + 2 + 4)
            copy_indexed(nc, self.target(p, 1), self.transposes(slot, 1)).then_inc(self.s_odd, 1)

        self.in_pairs(dve, ahead, behind)

    def scalar(self, act):
        nc, sh = self.nc, self.sh
        if self.norm:
            self.norm.scalar(act)
        act.sem_inc(self.s_even, 2)

        def ahead(p, slot):
            for par in range(2):
                t = p * 2 + par
                if self.norm:
                    act.wait_ge(self.norm.s_norm, t + 1)
                act.wait_ge(self.s_T, t + 1)
                nc.scalar.activation(self.parts[:, slot, par, 0, :], sh.H[:, t, :], ACT.Copy).then_inc(self.s_hi, 1)

        def behind(p, slot):
            act.wait_ge(self.s_T, p * 2 + 1 + 4)
            nc.scalar.activation(self.target(p, 0), self.transposes(slot, 0), ACT.Copy).then_inc(self.s_even, 1)

        self.in_pairs(act, ahead, behind)

    def tensor(self, pe):
        nc = self.nc
        pe.sem_inc(self.s_T, 4)
        with pe.Fori(0, self.PAIRS // 2) as q:
            for slot in range(2):
                p = q * 2 + slot
                for par in range(2):
                    pe.wait_ge(self.s_lo, p * 2 + par + 1)
                    pe.wait_ge((self.s_even, self.s_odd)[par], p + 1)
                    out = self.transposes(slot, par)
                    for part in range(2):
                        for k in range(KT):
                            last = nc.tensor.transpose(out[:, part, k, :], self.parts[:, slot, par, part, k * P:(k + 1) * P],
                                                       self.sh.identh[:, :])
                    last.then_inc(self.s_T, 1)

    def sync(self, sp):
        pass

    def whole(self, eng):
        eng.wait_ge(self.s_even, self.PAIRS + 2)
        eng.wait_ge(self.s_odd, self.PAIRS + 2)


def run(nc, *steps):
    with nc.Block() as block:
        @block.sync
        def _(sp):
            for step in steps:
                step.sync(sp)

        @block.scalar
        def _(act):
            for step in steps:
                step.scalar(act)

        @block.vector
        def _(dve):
            for step in steps:
                step.vector(dve)

        @block.tensor
        def _(pe):
            for step in steps:
                step.tensor(pe)


PRODUCTS = ((0, 0), (0, 1), (1, 0))


class MoE:

    def __init__(self, experts, top, tiles, rows, chunk):
        self.experts, self.top, self.tiles, self.rows, self.chunk = experts, top, tiles, rows, chunk


MOE0 = MoE(64, 8, 33, 66, 3)
MOE1 = MoE(8, 2, 40, 80, 2)
TW = 6 * P


class ExpertWeights:

    def __init__(self, nc, ctx, sh, m, w, name):
        self.nc, self.sh, self.m, self.w = nc, sh, m, w
        self.n = m.tiles // m.chunk
        self.s_load = [nc.alloc_semaphore(name=f"{name}_load{i}") for i in range(self.n)]
        self.s_hi, self.s_lo = (nc.alloc_semaphore(name=f"{name}_{x}") for x in ("hi", "lo"))
        sh.W = ctx.enter_context(nc.sbuf_tensor(name, [P, m.tiles + 2 * m.chunk, 2, TW], F16))

    def source(self, i):
        C = self.m.chunk
        return self.sh.W[:, (i + 2) * C:(i + 3) * C, :, :].rearrange("p f a c -> p (f a c)").bitcast(F32)

    def parts(self, i, part):
        C = self.m.chunk
        return self.sh.W[:, i * C:(i + 1) * C, part, :]

    def sync(self, sp):
        C = self.m.chunk * TW
        for i in range(self.n):
            sp.dma_start(self.source(i), self.w[:, i * C:(i + 1) * C]).then_inc(self.s_load[i], 16)

    def scalar(self, act, chunks):
        for i in chunks:
            act.wait_ge(self.s_load[i], 16)
            if i >= 2:
                act.wait_ge(self.s_lo, i - 1)
            self.nc.scalar.activation(self.parts(i, 0), self.source(i).rearrange("p (f c) -> p f c", c=TW), ACT.Copy).then_inc(self.s_hi, 1)

    def vector(self, dve, chunks):
        for i in chunks:
            dve.wait_ge(self.s_hi, i + 1)
            self.nc.vector.tensor_tensor(self.parts(i, 1), self.source(i).rearrange("p (f c) -> p f c", c=TW), self.parts(i, 0),
                                         ALU.subtract).then_inc(self.s_lo, 1)


LOW = -1.0e30
TAKEN = -3.0e38


def route(nc, sh, m, hT, load, router, weights_T, name):
    NE = m.experts
    NR = 65 if m is MOE0 else NE
    NL = NE + 8
    first, rest_of = range(0, load.n // 3), range(load.n // 3, load.n)
    with ExitStack() as ctx:
        def sb(n, shape, dt=F32):
            return ctx.enter_context(nc.sbuf_tensor(f"{name}_{n}", shape, dt))

        def sem(n):
            return nc.alloc_semaphore(name=f"{name}_{n}")

        rw = sb("rw", [P, KT, NR])
        rwp = sb("rwp", [P, 2, KT, NR], F16)
        L = sb("L", [P, NB, NL])
        rest = sb("rest", [P, NB, NL])
        top8 = sb("top8", [P, NB, 8])
        chosen = sb("chosen", [P, NB, 8])
        shifted = sb("shifted", [P, NB, NE])
        e = sb("e", [P, NB, NE])
        em = sb("em", [P, NB, NE])
        total = sb("total", [P, NB])
        inv = sb("inv", [P, NB])
        sig = sb("sig", [P, NB])
        sig1 = sb("sig1", [P, NB])
        comb = sb("comb", [P, NB, m.rows])
        combT = sb("combT", [m.rows, T])
        LP = ctx.enter_context(nc.psum_tensor(name + "_LP", [P, NB, P], F32))
        CP = LP
        s_load, s_hi, s_lo, s_L, s_d, s_e, s_comb, s_CT, s_ct, s_out, s_pad, s_Lc = map(sem, (
            "load", "hi", "lo", "L", "chain", "exp", "comb", "CT", "ct", "out", "pad", "Lc"))
        with nc.Block() as block:
            @block.sync
            def _(sp):
                sp.dma_start(rw[:, :, :], router).then_inc(s_load, 16)
                load.sync(sp)
                sp.wait_ge(s_ct, 1)
                sp.dma_start(weights_T, combT[:, :]).then_inc(s_out, 16)
                sp.wait_ge(s_out, 16)

            @block.scalar
            def _(act):
                hT.scalar(act)
                act.wait_ge(s_load, 16)
                nc.scalar.activation(rwp[:, 0, :, :], rw[:, :, :], ACT.Copy).then_inc(s_hi, 1)
                load.scalar(act, first)
                act.wait_ge(s_Lc, 2)
                nc.scalar.activation(e[:, :, :], shifted[:, :, :], ACT.Exp).then_inc(s_e, 1)
                if m is MOE0:
                    nc.scalar.activation(sig[:, :], LP[:, :, NE], ACT.Exp, scale=-1.0).then_inc(s_e, 1)
                act.wait_ge(s_CT, 1)
                nc.scalar.activation(combT[:, :], CP[0:m.rows, :, :].rearrange("p t c -> p (t c)"), ACT.Copy).then_inc(s_ct, 1)
                load.scalar(act, rest_of)

            @block.tensor
            def _(pe):
                hT.tensor(pe)
                hT.whole(pe)
                pe.wait_ge(s_lo, 1)
                with pe.Fori(0, NB) as t:
                    i = 0
                    for a, b in PRODUCTS:
                        for k in range(KT):
                            last = nc.tensor.matmul(LP[:, bass.ds(t, 1), 0:NR], sh.hT[:, a, k, bass.ds(t * P, P)], rwp[:, b, k, :],
                                                    start=i == 0, stop=i == 5)
                            i += 1
                    last.then_inc(s_L, 1)
                pe.wait_ge(s_comb, 1)
                for t in range(NB):
                    last = nc.tensor.transpose(CP[0:m.rows, t, :], comb[:, t, :], sh.ident[:, :])
                last.then_inc(s_CT, 1)

            @block.vector
            def _(dve):
                done = [0]

                def chained(ins):
                    done[0] += 1
                    ins.then_inc(s_d, 1)
                    dve.wait_ge(s_d, done[0])

                hT.vector(dve)
                dve.wait_ge(s_hi, 1)
                nc.vector.tensor_tensor(rwp[:, 1, :, :], rw[:, :, :], rwp[:, 0, :, :], ALU.subtract).then_inc(s_lo, 1)
                nc.vector.memset(L[:, :, NE:NL], LOW)
                nc.vector.memset(chosen[:, :, :], LOW)
                nc.vector.memset(comb[:, :, :], 1.0 if m is MOE1 else 0.0)
                load.vector(dve, first)
                dve.wait_ge(s_L, NB)
                chained(nc.vector.tensor_copy(L[:, :, 0:NE], LP[:, :, 0:NE]))
                for t in range(NB):
                    last = nc.vector.max(top8[:, t, :], L[:, t, :])
                chained(last)
                nc.vector.tensor_copy(chosen[:, :, 0:m.top], top8[:, :, 0:m.top]).then_inc(s_Lc, 1)
                nc.vector.tensor_tensor(shifted[:, :, :], L[:, :, 0:NE], top8[:, :, 0:1].to_broadcast([P, NB, NE]),
                                        ALU.subtract).then_inc(s_Lc, 1)
                dve.wait_ge(s_Lc, 2)
                for t in range(NB):
                    last = nc.vector.match_replace(rest[:, t, :], chosen[:, t, :], L[:, t, :], TAKEN)
                chained(last)
                dve.wait_ge(s_e, 2 if m is MOE0 else 1)
                chained(nc.vector.scalar_tensor_tensor(out=em[:, :, :], in0=rest[:, :, 0:NE], scalar=-2.0e38, in1=e[:, :, :],
                                                       op0=ALU.is_le, op1=ALU.mult))
                chained(nc.vector.reduce_sum(total[:, :], em[:, :, :], axis=AXX))
                chained(nc.vector.reciprocal(inv[:, :], total[:, :]))
                rep = 64 // NE
                dst = comb[:, :, 0:64].rearrange("p t (e r) -> p t e r", r=rep)
                if rep == 1:
                    chained(nc.vector.tensor_tensor(comb[:, :, 0:64], em[:, :, :], inv[:, :].unsqueeze(2).to_broadcast([P, NB, NE]), ALU.mult))
                    chained(nc.vector.tensor_scalar_add(sig1[:, :], sig[:, :], 1.0))
                    nc.vector.reciprocal(comb[:, :, 64], sig1[:, :]).then_inc(s_comb, 1)
                else:
                    chained(nc.vector.tensor_tensor(shifted[:, :, :], em[:, :, :], inv[:, :].unsqueeze(2).to_broadcast([P, NB, NE]), ALU.mult))
                    nc.vector.tensor_copy(dst, shifted[:, :, :].unsqueeze(3).to_broadcast([P, NB, NE, rep])).then_inc(s_comb, 1)
                load.vector(dve, rest_of)


def experts(nc, sems, sh, m, weights_T, gate, name):
    CT = 512
    NC = T // CT
    NF = m.tiles
    uses = ((NF + 1) // 2, NF // 2)
    with ExitStack() as ctx:
        def sb(n, shape, dt=F32):
            return ctx.enter_context(nc.sbuf_tensor(f"{name}_{n}", shape, dt))

        def sems2(n):
            return [nc.alloc_semaphore(name=f"{name}_{n}{u}") for u in range(2)]

        wb = sb("wb", [P, 2, CT])
        sg = sb("sg", [P, 2, CT])
        t1 = sb("t1", [P, 2, CT])
        a = sb("a", [P, 2, CT])
        ap = sb("ap", [P, 2, 2, CT], F16)
        zero = sb("zero", [P, CT], F16)
        G = ctx.enter_context(nc.psum_tensor(name + "_G", [P, 2, CT], F32))
        U = ctx.enter_context(nc.psum_tensor(name + "_U", [P, 2, CT], F32))
        O = ctx.enter_context(nc.psum_tensor(name + "_O", [P, CT // P, D], F32))
        s_wb, s_G, s_U, s_sg, s_t1, s_a, s_hi, s_lo, s_O = map(sems2, ("wb", "G", "U", "sg", "t1", "a", "hi", "lo", "O"))
        s_res = nc.alloc_semaphore(name=name + "_res")
        s_zero = nc.alloc_semaphore(name=name + "_zero")

        def steps(eng, c, step):
            with eng.Fori(0, NF // 2) as i:
                for u in range(2):
                    step(i * 2 + u, u, c * uses[u] + i)
            if NF % 2:
                step(NF - 1, 0, c * uses[0] + NF // 2)

        with nc.Block() as block:
            @block.sync
            def _(sp):
                def step(c, f, u, n):
                    sp.wait_ge(s_t1[u], n + 1)
                    for half in range(2):
                        src = weights_T[bass.ds(f * 2 + half, 1), bass.ds(c * CT, CT)].to_broadcast([P // 2, CT])
                        sp.dma_start(wb[half * 64:half * 64 + 64, u, :], src).then_inc(s_wb[u], 16)

                with sp.Fori(0, NC) as c:
                    steps(sp, c, lambda f, u, n: step(c, f, u, n))

            @block.scalar
            def _(act):
                def step(f, u, n):
                    act.wait_ge(s_G[u], n + 1)
                    nc.scalar.activation(sg[:, u, :], G[:, u, :], ACT.Silu).then_inc(s_sg[u], 1)
                    act.wait_ge(s_a[u], n + 2)
                    act.wait_ge(s_O[u], n + 1)
                    nc.scalar.activation(ap[:, u, 0, :], a[:, u, :], ACT.Copy).then_inc(s_hi[u], 1)

                act.sem_inc(s_sg[0], 1)
                act.sem_inc(s_sg[1], 1)
                with act.Fori(0, NC) as c:
                    steps(act, c, step)

            @block.vector
            def _(dve):
                def step(f, u, n):
                    dve.wait_ge(s_wb[u], n * 32 + 32)
                    dve.wait_ge(s_sg[u], n + 2)
                    nc.vector.tensor_tensor(t1[:, u, :], sg[:, u, :], wb[:, u, :], ALU.mult).then_inc(s_t1[u], 1)
                    dve.wait_ge(s_t1[u], n + 2)
                    dve.wait_ge(s_U[u], n + 1)
                    nc.vector.tensor_tensor(a[:, u, :], U[:, u, :], t1[:, u, :], ALU.mult).then_inc(s_a[u], 1)
                    dve.wait_ge(s_hi[u], n + 1)
                    nc.vector.tensor_tensor(ap[:, u, 1, :], a[:, u, :], ap[:, u, 0, :], ALU.subtract).then_inc(s_lo[u], 1)

                nc.vector.memset(zero[:, :], 0.0).then_inc(s_zero, 1)
                for u in range(2):
                    dve.sem_inc(s_t1[u], 1)
                    dve.sem_inc(s_a[u], 1)
                dve.sem_inc(s_res, 1)
                with dve.Fori(0, NC) as c:
                    steps(dve, c, step)
                    u = (NF - 1) % 2
                    dve.wait_ge(s_O[u], (c + 1) * uses[u] + 1)
                    xs = sh.X[:, bass.ds(c * (CT // P), CT // P), :]
                    nc.vector.scalar_tensor_tensor(out=xs, in0=O[:, :, :], scalar=gate, in1=xs, op0=ALU.mult,
                                                   op1=ALU.add).then_inc(s_res, 1)

            @block.tensor
            def _(pe):
                def up(c, f, u, n):
                    for X_, s_free, s_done, base in ((G, s_sg, s_G, 0), (U, s_a, s_U, 2 * P)):
                        pe.wait_ge(s_free[u], n + 1)
                        i = 0
                        for wp, xp in PRODUCTS:
                            for k in range(KT):
                                last = nc.tensor.matmul(X_[:, u, :], sh.W[:, f, wp, base + k * P:base + (k + 1) * P],
                                                        sh.hT[:, xp, k, bass.ds(c * CT, CT)], start=i == 0, stop=i == 5)
                                i += 1
                        last.then_inc(s_done[u], 1)

                def down(f, u, n):
                    pe.wait_ge(s_lo[u], n + 1)
                    for t in range(CT // P):
                        for xp, wp in PRODUCTS:
                            last = nc.tensor.matmul(O[:, t, :], ap[:, u, xp, t * P:(t + 1) * P],
                                                    sh.W[:, f, wp, 4 * P:TW], start=False, stop=False,
                                                    skip_group_check=True)
                    last.then_inc(s_O[u], 1)

                pe.sem_inc(s_O[0], 1)
                pe.sem_inc(s_O[1], 1)
                pe.wait_ge(s_zero, 1)
                with pe.Fori(0, NC) as c:
                    up(c, 0, 0, c * uses[0])
                    pe.wait_ge(s_res, c + 1)
                    for bank in range(2):
                        nc.tensor.matmul(O[:, 2 * bank:2 * bank + 2, :], zero[:, 0:P], zero[:, :], start=True, stop=False,
                                         skip_group_check=True)
                    NI = (NF - 1) // 2
                    with pe.Fori(0, NI) as i:
                        up(c, i * 2 + 1, 1, c * uses[1] + i)
                        down(i * 2, 0, c * uses[0] + i)
                        up(c, i * 2 + 2, 0, c * uses[0] + i + 1)
                        down(i * 2 + 1, 1, c * uses[1] + i)
                    if NF % 2 == 0:
                        up(c, NF - 1, 1, c * uses[1] + NI)
                        down(NF - 2, 0, c * uses[0] + NI)
                        down(NF - 1, 1, c * uses[1] + NI)
                    else:
                        down(NF - 1, 0, c * uses[0] + NI)


class LoadSplit:

    def __init__(self, nc, ctx, items, name):
        self.nc, self.items = nc, items
        self.s_load = [nc.alloc_semaphore(name=f"{name}_load{i}") for i in range(len(items))]
        self.s_hi = nc.alloc_semaphore(name=name + "_hi")
        self.stages = [ctx.enter_context(nc.sbuf_tensor(f"{name}_stage{i}", [P, src.shape[1]], F32)) for i, (_, src) in enumerate(items)]

    def sync(self, sp):
        for s_load, stage, (_, src) in zip(self.s_load, self.stages, self.items):
            sp.dma_start(stage[:, :], src).then_inc(s_load, 16)

    def scalar(self, act):
        for s_load, stage, (dst, _) in zip(self.s_load, self.stages, self.items):
            act.wait_ge(s_load, 16)
            self.nc.scalar.activation(dst[:, 0, :], stage[:, :], ACT.Copy).then_inc(self.s_hi, 1)

    def vector(self, dve):
        for i, (stage, (dst, _)) in enumerate(zip(self.stages, self.items)):
            dve.wait_ge(self.s_hi, i + 1)
            self.nc.vector.tensor_tensor(dst[:, 1, :], stage[:, :], dst[:, 0, :], ALU.subtract)

    def tensor(self, pe):
        pass


def rms_attention(nc, sems, sh, ctxT, weights, gate):
    NH, HD = 32, 8
    SLOT = 32
    GH = P // SLOT
    NG = NH // GH
    HE = HD + 1
    with ExitStack() as ctx:
        def sb(n, shape, dt=F32):
            return ctx.enter_context(nc.sbuf_tensor("rms_" + n, shape, dt))

        def sem(n):
            return nc.alloc_semaphore(name="rms_" + n)

        qk = sb("qk", [P, NB, 2, NH, HD])
        vx = sb("vx", [P, NB, NH, HE])
        ss = sb("ss", [P, NB, 2 * NH])
        rs = sb("rs", [P, NB, 2 * NH])
        with ExitStack() as inner:
            cT = inner.enter_context(nc.sbuf_tensor("rms_cT", [P, 2, KT * T], F16))
            wq, wk, wv = (inner.enter_context(nc.sbuf_tensor(f"rms_{x}", [P, 2, KT * D], F16)) for x in ("wq", "wk", "wv"))
            with ExitStack() as head:
                norm = Layernorm(nc, head, sh, "rms_ln")
                items = [(cT, ctxT), (wq, weights["q"]), (wk, weights["k"]), (wv, weights["v"])]
                run(nc, Transposed(nc, head, sh, "rms_hT", norm), LoadSplit(nc, head, items, "rms_load"))
            sq = inner.enter_context(nc.sbuf_tensor("rms_sq", [P, 2, 2 * D], F32))
            QK = inner.enter_context(nc.psum_tensor("rms_QK", [P, 2, 2, D], F32))
            V = inner.enter_context(nc.psum_tensor("rms_V", [P, 2, 512], F32))
            s_mm, s_sq, s_ev, s_v, s_qk, s_one = map(sem, ("mm", "sq", "red", "v", "qk", "one"))
            with nc.Block() as block:
                @block.tensor
                def _(pe):
                    with pe.Fori(0, NB // 2) as pair:
                        for par in range(2):
                            t = pair * 2 + par
                            pe.wait_ge(s_v, t + 1)
                            pe.wait_ge(s_qk, t + 1)
                            for out, x, w in ((QK[:, par, 0, :], None, wq), (QK[:, par, 1, :], cT, wk), (V[:, par, 0:D], cT, wv)):
                                i = 0
                                for a, b in PRODUCTS:
                                    for k in range(KT):
                                        lhs = sh.hT[:, a, k, bass.ds(t * P, P)] if x is None else x[:, a, bass.ds(t * P + k * T, P)]
                                        last = nc.tensor.matmul(out, lhs, w[:, b, k * D:(k + 1) * D], start=i == 0, stop=i == 5)
                                        i += 1
                            last.then_inc(s_mm, 1)

                @block.scalar
                def _(act):
                    act.sem_inc(s_v, 2)
                    act.wait_ge(s_one, 1)
                    with act.Fori(0, NB // 2) as pair:
                        for par in range(2):
                            t = pair * 2 + par
                            act.wait_ge(s_qk, t + 3)
                            act.wait_ge(s_ev, t + 1)
                            nc.scalar.activation(sq[:, par, :], qk[:, t, :, :, :].rearrange("p s h d -> p (s h d)"), ACT.Square).then_inc(s_sq, 1)
                            act.wait_ge(s_mm, t + 1)
                            nc.scalar.activation(vx[:, t, :, 0:HD], V[:, par, 0:D].rearrange("p (h d) -> p h d", d=HD),
                                                 ACT.Copy).then_inc(s_v, 1)

                @block.vector
                def _(dve):
                    dve.sem_inc(s_ev, 2)
                    dve.sem_inc(s_qk, 2)
                    nc.vector.memset(vx[:, :, :, HD:HE], 1.0).then_inc(s_one, 1)
                    with dve.Fori(0, NB // 2) as pair:
                        for par in range(2):
                            t = pair * 2 + par
                            dve.wait_ge(s_mm, t + 1)
                            copy_indexed(nc, qk[:, t, :, :, :], QK[:, par, :, :]).then_inc(s_qk, 1)
                            dve.wait_ge(s_sq, t + 1)
                            nc.vector.reduce_sum(ss[:, t, :], sq[:, par, :].rearrange("p (g d) -> p g d", d=HD),
                                                 axis=AXX).then_inc(s_ev, 1)

        s_root, s_rs = sem("root"), sem("rs")
        eps6 = sb("eps6", [P, 1])
        s_eps = sem("eps")
        s_n = sem("n")
        qs = sb("qs", [P, 2, NH, SLOT], F16)
        ks = sb("ks", [P, 2, NH, SLOT], F16)
        qT = sb("qT", [P, 2, NG, P], F16)
        kT = sb("kT", [P, 2, NG, P], F16)
        E = sb("E", [P, 2, 2, NG // 2, P])
        inv = sb("inv", [P, 2, NH])
        on = sb("on", [P, 2, NH, HD])
        NR = 4
        TQ = ctx.enter_context(nc.psum_tensor("rms_TQ", [P, NG, P], F16))
        TK = ctx.enter_context(nc.psum_tensor("rms_TK", [P, NG, P], F16))
        S = ctx.enter_context(nc.psum_tensor("rms_S", [P, 2, 2, NG // 2, P], F32))
        O = ctx.enter_context(nc.psum_tensor("rms_O", [P, 2, 512], F32))
        s_hi, s_lo, s_TQ, s_TK, s_qT, s_kT, s_S, s_E, s_O, s_inv, s_on, s_res = map(sem, (
            "hi", "lo", "TQ", "TK", "qT", "kT", "S", "E", "O", "inv", "on", "res"))
        with nc.Block() as block:
            @block.tensor
            def _(pe):
                pe.sem_inc(s_TK, 2)
                pe.sem_inc(s_S, 2 * NR)
                pe.sem_inc(s_O, 2)

                def transposes(t, par):
                    pe.wait_ge(s_lo, t + 1)
                    for side, st, out, read, done in ((0, qs, TQ, s_qT, s_TQ), (1, ks, TK, s_kT, s_TK)):
                        pe.wait_ge(read, t + 1)
                        for g in range(NG):
                            last = nc.tensor.transpose(out[:, g, :], st[:, par, g * GH:(g + 1) * GH, :].rearrange("p h s -> p (h s)"), sh.identh[:, :])
                        last.then_inc(done, 1)

                def scores(t, par, r):
                    if r == 0:
                        pe.wait_ge(s_qT, t + 2)
                        pe.wait_ge(s_kT, t + 2)
                    pe.wait_ge(s_E, t * NR + r + 1)
                    for i in range(NG // 2):
                        for jj in range(2):
                            g, j = r // 2 * (NG // 2) + i, r % 2 * 2 + jj
                            last = nc.tensor.matmul(S[:, r % 2, jj, i, :], kT[j * SLOT:(j + 1) * SLOT, par, g, :],
                                                    qT[j * SLOT:(j + 1) * SLOT, par, g, :], start=True, stop=True,
                                                    skip_group_check=True)
                    last.then_inc(s_S, 1)

                def values(t, par, r):
                    if r == 0:
                        pe.wait_ge(s_res, t + 1)
                    pe.wait_ge(s_E, t * NR + r + 3)
                    for i in range(NG // 2):
                        for jj in range(2):
                            h = (r // 2 * (NG // 2) + i) * GH + r % 2 * 2 + jj
                            last = nc.tensor.matmul(O[:, par, h * HE:(h + 1) * HE], E[:, r % 2, jj, i, :],
                                                    vx[:, t, h, :], start=True, stop=True, skip_group_check=True)
                    last.then_inc(s_O, 1)

                def tile(t, par, last):
                    for r in range(1, NR):
                        scores(t, par, r)
                        values(t, par, r - 1) if r < NR - 1 else None
                    if not last:
                        transposes(t + 1, 1 - par)
                    values(t, par, NR - 2)
                    if not last:
                        scores(t + 1, 1 - par, 0)
                    values(t, par, NR - 1)

                transposes(0, 0)
                scores(0, 0, 0)
                with pe.Fori(0, NB // 2 - 1) as pair:
                    for par in range(2):
                        tile(pair * 2 + par, par, False)
                tile(NB - 2, 0, False)
                tile(NB - 1, 1, True)

            @block.scalar
            def _(act):
                act.sem_inc(s_E, 2)
                act.sem_inc(s_qT, 1)
                act.wait_ge(s_eps, 1)
                nc.scalar.activation(rs[:, :, :], ss[:, :, :], ACT.Sqrt, bias=eps6[:, 0:1], scale=1.0 / HD).then_inc(s_root, 1)

                def queries(t, par):
                    act.wait_ge(s_TQ, t + 1)
                    act.wait_ge(s_S, t * NR + NR)
                    nc.scalar.activation(qT[:, par, :, :], TQ[:, :, :], ACT.Copy).then_inc(s_qT, 1)

                def exponentials(t, r):
                    act.wait_ge(s_S, t * NR + r + 1 + 2 * NR)
                    act.wait_ge(s_O, t * NR + r + 1)
                    nc.scalar.activation(E[:, r % 2, :, :, :], S[:, r % 2, :, :, :], ACT.Exp,
                                         scale=float(HD) ** -0.5).then_inc(s_E, 1)

                def tile(t, par, last):
                    for r in range(1, NR):
                        exponentials(t, r)
                    if not last:
                        queries(t + 1, 1 - par)
                        exponentials(t + 1, 0)

                queries(0, 0)
                exponentials(0, 0)
                with act.Fori(0, NB // 2 - 1) as pair:
                    for par in range(2):
                        tile(pair * 2 + par, par, False)
                tile(NB - 2, 0, False)
                tile(NB - 1, 1, True)

            @block.vector
            def _(dve):
                dve.sem_inc(s_kT, 1)
                dve.sem_inc(s_res, 2)
                nc.vector.memset(eps6[:, :], 1e-6).then_inc(s_eps, 1)
                nc.vector.memset(qs[:, :, :, :], 0.0)
                nc.vector.memset(ks[:, :, :, :], 0.0).then_inc(s_n, 1)
                dve.wait_ge(s_root, 1)
                nc.vector.reciprocal(ss[:, :, :], rs[:, :, :]).then_inc(s_rs, 1)
                dve.wait_ge(s_rs, 1)

                def stacks(t, par):
                    x = qk[:, t, :, :, :].rearrange("p s h d -> p (s h) d")
                    nc.vector.tensor_tensor(x, x, ss[:, t, :].unsqueeze(2).to_broadcast([P, 2 * NH, HD]), ALU.mult).then_inc(s_n, 1)
                    dve.wait_ge(s_n, t + 2)
                    dve.wait_ge(s_TK, t + 1)
                    for side, st, second in ((0, qs, 1), (1, ks, 2)):
                        for slot in (0, second):
                            last = copy_indexed(nc, st[:, par, :, slot * HD:(slot + 1) * HD], qk[:, t, side, :, :])
                    last.then_inc(s_hi, 1)
                    dve.wait_ge(s_hi, t + 1)
                    nc.vector.tensor_tensor(qs[:, par, :, 2 * HD:3 * HD], qk[:, t, 0, :, :], qs[:, par, :, 0:HD], ALU.subtract)
                    nc.vector.tensor_tensor(ks[:, par, :, HD:2 * HD], qk[:, t, 1, :, :], ks[:, par, :, 0:HD], ALU.subtract).then_inc(s_lo, 1)

                def output(t, par):
                    o = O[:, par, 0:NH * HE].rearrange("p (h d) -> p h d", d=HE)
                    dve.wait_ge(s_O, t * NR + NR + 2)
                    nc.vector.reciprocal(inv[:, par, :], o[:, :, HD]).then_inc(s_inv, 1)
                    dve.wait_ge(s_inv, t + 1)
                    nc.vector.tensor_tensor(on[:, par, :, :], o[:, :, 0:HD], inv[:, par, :].unsqueeze(2).to_broadcast([P, NH, HD]),
                                            ALU.mult).then_inc(s_on, 1)
                    dve.wait_ge(s_on, t + 1)
                    nc.vector.scalar_tensor_tensor(out=sh.X[:, t, :], in0=on[:, par, :, :].rearrange("p h d -> p (h d)"),
                                                   scalar=gate, in1=sh.X[:, t, :], op0=ALU.mult, op1=ALU.add).then_inc(s_res, 1)

                def keys(t, par):
                    dve.wait_ge(s_TK, t + 3)
                    dve.wait_ge(s_S, t * NR + NR)
                    nc.vector.tensor_copy(kT[:, par, :, :], TK[:, :, :]).then_inc(s_kT, 1)

                def tile(t, par, last):
                    if not last:
                        stacks(t + 1, 1 - par)
                        keys(t + 1, 1 - par)
                    output(t, par)

                stacks(0, 0)
                keys(0, 0)
                with dve.Fori(0, NB // 2 - 1) as pair:
                    for par in range(2):
                        tile(pair * 2 + par, par, False)
                tile(NB - 2, 0, False)
                tile(NB - 1, 1, True)


MAGIC = 1.5 * 2.0 ** 23


def transpose_tiles(nc, sems, name, groups, source, target, ident):
    s_T, s_even, s_odd = (nc.alloc_semaphore(name=f"{name}_{n}") for n in ("T", "even", "odd"))
    with ExitStack() as ctx:
        TP = ctx.enter_context(nc.psum_tensor(name + "_TP", [P, 2, 4, P], F32))
        with nc.Block() as block:
            @block.scalar
            def _(act):
                act.sem_inc(s_even, 1)
                with act.Fori(0, NB // 2) as pair:
                    act.wait_ge(s_T, pair * 2 + 1)
                    nc.scalar.activation(target(pair * 2), TP[:, 0, 0:groups, :], ACT.Copy).then_inc(s_even, 1)

            @block.vector
            def _(dve):
                dve.sem_inc(s_odd, 1)
                with dve.Fori(0, NB // 2) as pair:
                    dve.wait_ge(s_T, pair * 2 + 2)
                    copy_indexed(nc, target(pair * 2 + 1), TP[:, 1, 0:groups, :]).then_inc(s_odd, 1)

            @block.tensor
            def _(pe):
                with pe.Fori(0, NB // 2) as pair:
                    for par in range(2):
                        pe.wait_ge((s_even, s_odd)[par], pair + 1)
                        for g in range(groups):
                            last = nc.tensor.matmul(TP[:, par, g, :], source(g, pair * 2 + par), ident, start=True, stop=True)
                        last.then_inc(s_T, 1)


def project(nc, sems, name, parts, weights, evacuate):
    s_mm, s_ev = (nc.alloc_semaphore(name=f"{name}_{n}") for n in ("mm", "ev"))
    with ExitStack() as ctx:
        Q = ctx.enter_context(nc.psum_tensor(name + "_Q", [P, 2, 512], F32))
        with nc.Block() as block:
            @block.tensor
            def _(pe):
                with pe.Fori(0, NB // 2) as pair:
                    for par in range(2):
                        t = pair * 2 + par
                        pe.wait_ge(s_ev, t + 1)
                        i = 0
                        for a, b in PRODUCTS:
                            for k in range(KT):
                                last = nc.tensor.matmul(Q[:, par, 0:D], parts(a, k, t), weights[:, b, k * D:(k + 1) * D],
                                                        start=i == 0, stop=i == 5)
                                i += 1
                        last.then_inc(s_mm, 1)

            @block.vector
            def _(dve):
                dve.sem_inc(s_ev, 2)
                with dve.Fori(0, NB // 2) as pair:
                    for par in range(2):
                        t = pair * 2 + par
                        dve.wait_ge(s_mm, t + 1)
                        evacuate(dve, t, Q[:, par, 0:D]).then_inc(s_ev, 1)


def quantised_attention(nc, sems, sh, a, gate):
    NH, HD = 16, 16
    SLOT = 2 * HD
    GH = P // SLOT
    NG = NH // GH
    HALF = T // 2
    KB = HALF // P
    LN255 = float(np.log(255.0))
    with ExitStack() as ctx:
        def sb(n, shape, dt=F32, where=ctx):
            return where.enter_context(nc.sbuf_tensor("qa_" + n, shape, dt))

        def sem(n):
            return nc.alloc_semaphore(name="qa_" + n)

        qT = sb("qT", [P, NG, T], F16)
        kT = sb("kT", [P, NG, T], F16)
        V = sb("V", [P, NB, D], BF16)
        neg_sq = sb("neg_sq", [P, NB, NH])
        sq = sb("sq", [P, NB, NH])
        svb = sb("svb", [P, D])
        bias = sb("bias", [P, 3, D])
        bv = sb("bv", [P, KT])
        wp = sb("wp", [P, 2, KT * D], F16)
        with ExitStack() as inner:
            cT = sb("cT", [P, 2, KT * T], F16, inner)
            wq, wk, wv = (sb(x, [P, 2, KT * D], F16, inner) for x in ("wq", "wk", "wv"))
            with ExitStack() as head:
                norm = Layernorm(nc, head, sh, "qa_ln")
                items = [(cT, a["ctxT"]), (wq, a["qa_wq"]), (wk, a["qa_wk"]), (wv, a["qa_wv"]), (wp, a["qa_wp"])]
                run(nc, Transposed(nc, head, sh, "qa_hT", norm), LoadSplit(nc, head, items, "qa_load"))
            Y = sb("Y", [P, NB, D], F32, inner)
            Z = sb("Z", [P, NB, D], F32, inner)
            stack = sb("stack", [P, NB, NH, SLOT], F16, inner)
            ints = sb("ints", [P, KT, T], BF16, inner)
            amax = sb("amax", [P, NB, NH], F32, inner)
            sv = sb("sv", [P, KT], F32, inner)
            rsv = sb("rsv", [P, KT], F32, inner)
            s_b, s_b4 = sem("bias"), sem("b4")
            with nc.Block() as block:
                @block.sync
                def _(sp):
                    for i, x in enumerate(("bq", "bk", "bp")):
                        sp.dma_start(bias[:, i, :], a["qa_" + x].partition_broadcast(P)).then_inc(s_b, 16)
                    sp.dma_start(bv[:, :], a["qa_bv"]).then_inc(s_b, 16)
                    sp.wait_ge(s_b, 64)

                @block.vector
                def _(dve):
                    dve.wait_ge(s_b, 64)
                    nc.vector.tensor_scalar_mul(bias[:, 0, :], bias[:, 0, :], float(HD) ** -0.5).then_inc(s_b4, 1)

            def quantise(side):
                s_c = sem("chain" + side)
                scale = sq if side == "q" else amax
                y = Y[:, :, :].rearrange("p t (h d) -> p (t h) d", d=HD)
                z = Z[:, :, :].rearrange("p t (h d) -> p (t h) d", d=HD)
                st = stack[:, :, :, :].rearrange("p t h s -> p (t h) s")
                flat = scale[:, :, :].rearrange("p t h -> p (t h)")
                inv = neg_sq[:, :, :].rearrange("p t h -> p (t h)")
                with nc.Block() as block:
                    @block.vector
                    def _(dve):
                        done = [0]

                        def chained(ins):
                            done[0] += 1
                            ins.then_inc(s_c, 1)
                            dve.wait_ge(s_c, done[0])

                        wide = [P, NB * NH, HD]
                        chained(nc.vector.tensor_reduce(out=flat, in_=y, axis=AXX, op=ALU.max, apply_absolute_value=True))
                        chained(nc.vector.tensor_scalar(flat, flat, 1.0 / 127.0, 1e-8, ALU.mult, ALU.max))
                        chained(nc.vector.reciprocal(inv, flat))
                        chained(nc.vector.tensor_tensor(z, y, inv.unsqueeze(2).to_broadcast(wide), ALU.mult))
                        chained(nc.vector.tensor_scalar(Z[:, :, :], Z[:, :, :], MAGIC, MAGIC, ALU.add, ALU.subtract))
                        if side == "q":
                            for slot in range(2):
                                nc.vector.tensor_scalar(st[:, :, slot * HD:(slot + 1) * HD], z, 127.0, -127.0, ALU.min, ALU.max)
                            nc.vector.tensor_scalar_mul(neg_sq[:, :, :], sq[:, :, :], -1.0)
                        else:
                            chained(nc.vector.tensor_scalar(Z[:, :, :], Z[:, :, :], 127.0, -127.0, ALU.min, ALU.max))
                            chained(nc.vector.tensor_tensor(y, z, flat.unsqueeze(2).to_broadcast(wide), ALU.mult))
                            chained(nc.vector.tensor_copy(st[:, :, 0:HD], y))
                            nc.vector.tensor_tensor(st[:, :, HD:SLOT], y, st[:, :, 0:HD], ALU.subtract)
                transpose_tiles(nc, sems, "qaT" + side, NG,
                                lambda g, t: stack[:, t, g * GH:(g + 1) * GH, :].rearrange("p h s -> p (h s)"),
                                lambda t: (qT if side == "q" else kT)[:, :, bass.ds(t * P, P)], sh.identh[:, :])

            project(nc, sems, "qapk", lambda part, k, t: cT[:, part, bass.ds(t * P + k * T, P)], wk,
                    lambda dve, t, psum: nc.vector.tensor_tensor(Y[:, t, :], psum, bias[:, 1, :], ALU.add))
            quantise("k")
            project(nc, sems, "qapq", lambda part, k, t: sh.hT[:, part, k, bass.ds(t * P, P)], wq,
                    lambda dve, t, psum: nc.vector.scalar_tensor_tensor(out=Y[:, t, :], in0=psum, scalar=float(HD) ** -0.5,
                                                                        in1=bias[:, 0, :], op0=ALU.mult, op1=ALU.add))
            quantise("q")

            vT = Y[:, :, :].rearrange("p t d -> p (t d)").rearrange("p (m n) -> p m n", m=KT)
            zT = Z[:, :, :].rearrange("p t d -> p (t d)").rearrange("p (m n) -> p m n", m=KT)
            sv_dram = nc.dram_tensor("qa_value_scales", [P, KT], F32, kind="Internal").ap()
            s_mm, s_ev, s_vc, s_sv, s_out, s_in = map(sem, ("vmm", "vev", "vchain", "sv", "svout", "svin"))
            with ExitStack() as pctx:
                VP = pctx.enter_context(nc.psum_tensor("qa_VP", [P, 2, 512], F32))
                with nc.Block() as block:
                    @block.tensor
                    def _(pe):
                        for m in range(KT):
                            for c in range(4):
                                n = m * 4 + c
                                if n >= 2:
                                    pe.wait_ge(s_ev, n - 1)
                                i = 0
                                for wpart, xpart in PRODUCTS:
                                    for k in range(KT):
                                        last = nc.tensor.matmul(VP[:, n % 2, :], wv[:, wpart, k * D + m * P:k * D + (m + 1) * P],
                                                                cT[:, xpart, k * T + c * 512:k * T + (c + 1) * 512],
                                                                start=i == 0, stop=i == 5)
                                        i += 1
                                last.then_inc(s_mm, 1)

                    @block.scalar
                    def _(act):
                        for m in range(KT):
                            for c in range(4):
                                n = m * 4 + c
                                act.wait_ge(s_mm, n + 1)
                                nc.scalar.activation(vT[:, m, c * 512:(c + 1) * 512], VP[:, n % 2, :], ACT.Identity,
                                                     bias=bv[:, m:m + 1]).then_inc(s_ev, 1)

                    @block.vector
                    def _(dve):
                        done = [0]

                        def chained(ins):
                            done[0] += 1
                            ins.then_inc(s_vc, 1)
                            dve.wait_ge(s_vc, done[0])

                        dve.wait_ge(s_ev, 4 * KT)
                        chained(nc.vector.tensor_reduce(out=sv[:, :], in_=vT, axis=AXX, op=ALU.max, apply_absolute_value=True))
                        nc.vector.tensor_scalar(sv[:, :], sv[:, :], 1.0 / 127.0, 1e-8, ALU.mult, ALU.max).then_inc(s_sv, 1)
                        dve.wait_ge(s_sv, 1)
                        chained(nc.vector.reciprocal(rsv[:, :], sv[:, :]))
                        for m in range(KT):
                            last = nc.vector.tensor_scalar(zT[:, m, :], vT[:, m, :], rsv[:, m:m + 1], MAGIC, ALU.mult, ALU.add)
                        chained(last)
                        chained(nc.vector.tensor_scalar(zT, zT, MAGIC, 127.0, ALU.subtract, ALU.min))
                        nc.vector.tensor_scalar(ints[:, :, :], zT, -127.0, None, ALU.max)

                    @block.sync
                    def _(sp):
                        sp.wait_ge(s_sv, 1)
                        sp.dma_start(sv_dram, sv[:, :]).then_inc(s_out, 16)
                        sp.wait_ge(s_out, 16)
                        sp.dma_start(svb[:, :], sv_dram.rearrange("p m -> (p m)").partition_broadcast(P)).then_inc(s_in, 16)
                        sp.wait_ge(s_in, 16)
            transpose_tiles(nc, sems, "qaTv", KT, lambda m, t: ints[:, m, bass.ds(t * P, P)],
                            lambda t: V[:, t, :].rearrange("p (m c) -> p m c", m=KT), sh.ident16[:, :])

        qb = sb("qb", [P, 2, NG // 2, P], F16)
        mx = sb("mx", [P, 2, 2])
        mm = sb("mm", [P, 2])
        nb = sb("nb", [P, 2])
        sums = sb("sums", [P, NB * NH, 2])
        e16 = sb("e16", [P, 2, 2, HALF], mybir.dt.uint16)
        pb = sb("pb", [P, 4, 2, KB, P], BF16)
        pT = sb("pT", [P, 2, 2, KB, P], BF16)
        s_q, s_Sa, s_Sb, s_Ea, s_Eb, s_mx, s_mm2, s_nb, s_cast, s_Ta, s_Tb, s_eva, s_evb, s_V, s_o = map(sem, (
            "q", "Sa", "Sb", "Ea", "Eb", "mx", "mm2", "nb", "cast", "Ta", "Tb", "eva", "evb", "V", "o"))
        O_ALL = NB * NH
        with ExitStack() as pctx:
            Sa = pctx.enter_context(nc.psum_tensor("qa_Sa", [P, 2, HALF], F32))
            Sb = pctx.enter_context(nc.psum_tensor("qa_Sb", [P, HALF], F32))
            TP = pctx.enter_context(nc.psum_tensor("qa_TP", [P, KB, P], BF16))
            O = pctx.enter_context(nc.psum_tensor("qa_O", [P, NH * HD], F32))
            LAG = 5

            def skewed(eng, step):
                units = NB * NH
                for i in range(LAG):
                    step(i, lambda lag, i=i: 0 if i >= lag else None)
                with eng.Fori(0, NB - 1) as t:
                    for i in range(LAG, LAG + NH):
                        step(i % NH, lambda lag, i=i, t=t: t + 1 if i - lag >= NH else t)
                for i in range(LAG + (NB - 1) * NH, units + LAG):
                    step(i % NH, lambda lag, i=i: (i - lag) // NH if i - lag < units else None)

            with nc.Block() as block:
                @block.gpsimd
                def _(pool):
                    with pool.Fori(0, NB) as t:
                        for half in range(2):
                            pool.wait_ge(s_Sb, t * NH + (half + 1) * (NH // 2))
                            nc.gpsimd.tensor_copy(qb[:, half, :, :], qT[:, half * 2:half * 2 + 2, bass.ds(t * P, P)]).then_inc(s_q, 1)

                @block.tensor
                def _(pe):
                    pe.sem_inc(s_Sb, NH)

                    def scores(h, out, first):
                        g, j = h // GH, h % GH
                        rows = slice(j * SLOT, (j + 1) * SLOT)
                        for c in range(0, HALF, 512):
                            last = nc.tensor.matmul(out[:, c:c + 512], qb[rows, g // 2, g % 2, :],
                                                    kT[rows, g, first + c:first + c + 512], start=True, stop=True)
                        return last

                    def transposes(h, half):
                        for b in range(KB):
                            last = nc.tensor.transpose(TP[:, b, :], pb[:, h % 4, half, b, :], sh.ident16[:, :])
                        return last

                    def step(i, tile):
                        if (t := tile(1)) is not None:
                            h = (i - 1) % NH
                            pe.wait_ge(s_Eb, t * NH + h + 1)
                            scores(h, Sb, HALF).then_inc(s_Sb, 1)
                        if (t := tile(4)) is not None:
                            h = (i - 4) % NH
                            pe.wait_ge(s_cast, t * NH + h + 3)
                            pe.wait_ge(s_evb, t * NH + h + 1)
                            transposes(h, 0).then_inc(s_Ta, 1)
                        if (t := tile(0)) is not None:
                            h = i
                            if h % 8 == 0:
                                pe.wait_ge(s_q, 2 * t + 1 + h // 8)
                            pe.wait_ge(s_Ea, t * NH + h + 1)
                            scores(h, Sa[:, h % 2, :], 0).then_inc(s_Sa, 1)
                        if (t := tile(5)) is not None:
                            h = (i - 5) % NH
                            pe.wait_ge(s_eva, t * NH + h + 1)
                            pe.wait_ge(s_evb, t * NH + h + 2)
                            if h == 0:
                                pe.wait_ge(s_o, t + 1)
                            for b in range(2 * KB):
                                last = nc.tensor.matmul(O[:, h * HD:(h + 1) * HD], pT[:, h % 2, b // KB, b % KB, :],
                                                        V[:, b, h * HD:(h + 1) * HD], start=b == 0, stop=b == 2 * KB - 1)
                            last.then_inc(s_V, 1)
                        if (t := tile(4)) is not None:
                            h = (i - 4) % NH
                            pe.wait_ge(s_eva, t * NH + h + 1)
                            transposes(h, 1).then_inc(s_Tb, 1)

                    pe.sem_inc(s_V, 2)
                    pe.sem_inc(s_Tb, 4)
                    skewed(pe, step)

                @block.scalar
                def _(act):
                    act.sem_inc(s_Ea, 2)
                    act.sem_inc(s_Eb, 1)

                    def exponential(t, h, half, scores):
                        return nc.scalar.activation(e16[:, h % 2, half, :], scores, ACT.Exp, bias=nb[:, h % 2:h % 2 + 1],
                                                    scale=sq[:, t, h:h + 1], accum_out=sums[:, t * NH + h, half:half + 1])

                    def step(i, tile):
                        if (t := tile(1)) is not None:
                            h = (i - 1) % NH
                            act.wait_ge(s_nb, t * NH + h + 1)
                            act.wait_ge(s_cast, t * NH + h + 1)
                            exponential(t, h, 1, Sb[:, :]).then_inc(s_Eb, 1)
                            exponential(t, h, 0, Sa[:, h % 2, :]).then_inc(s_Ea, 1)
                        if (t := tile(3)) is not None:
                            h = (i - 3) % NH
                            act.wait_ge(s_Ta, t * NH + h + 1)
                            act.wait_ge(s_V, t * NH + h + 1)
                            nc.scalar.activation(pT[:, h % 2, 0, :, :], TP[:, :, :], ACT.Copy).then_inc(s_eva, 1)

                    skewed(act, step)

                @block.vector
                def _(dve):
                    dve.sem_inc(s_cast, 2)
                    dve.sem_inc(s_evb, 1)
                    dve.sem_inc(s_o, 1)

                    def step(i, tile):
                        if (t := tile(1)) is not None:
                            h = (i - 1) % NH
                            u = t * NH + h
                            dve.wait_ge(s_Sb, u + 1 + NH)
                            nc.vector.reduce_max(mx[:, h % 2, 1:2], Sb[:, :], axis=AXX).then_inc(s_mx, 1)
                            dve.wait_ge(s_mx, 2 * u + 2)
                            nc.vector.tensor_tensor(mm[:, h % 2:h % 2 + 1], mx[:, h % 2, 0:1], mx[:, h % 2, 1:2], ALU.max).then_inc(s_mm2, 1)
                            dve.wait_ge(s_mm2, u + 1)
                            nc.vector.tensor_scalar(nb[:, h % 2:h % 2 + 1], mm[:, h % 2:h % 2 + 1], neg_sq[:, t, h:h + 1], LN255,
                                                    ALU.mult, ALU.add).then_inc(s_nb, 1)
                        if (t := tile(0)) is not None:
                            h = i
                            dve.wait_ge(s_Sa, t * NH + h + 1)
                            nc.vector.reduce_max(mx[:, h % 2, 0:1], Sa[:, h % 2, :], axis=AXX).then_inc(s_mx, 1)
                        if (t := tile(4)) is not None:
                            h = (i - 4) % NH
                            dve.wait_ge(s_Tb, t * NH + h + 5)
                            dve.wait_ge(s_V, t * NH + h + 1)
                            nc.vector.tensor_copy(pT[:, h % 2, 1, :, :], TP[:, :, :]).then_inc(s_evb, 1)
                        if (t := tile(2)) is not None:
                            h = (i - 2) % NH
                            dve.wait_ge(s_Ea, t * NH + h + 3)
                            dve.wait_ge(s_Tb, t * NH + h + 1)
                            nc.vector.tensor_copy(pb[:, h % 4, :, :, :], e16[:, h % 2, :, :]).then_inc(s_cast, 1)
                        if (i - 5) % NH == NH - 1 and (t := tile(5)) is not None:
                            dve.wait_ge(s_V, t * NH + NH + 2)
                            copy_indexed(nc, sh.H[:, t, :], O[:, :]).then_inc(s_o, 1)

                    skewed(dve, step)

        tot = sb("tot", [P, O_ALL])
        rtot = sb("rtot", [P, O_ALL])
        s_n = sem("norm")
        with nc.Block() as block:
            @block.vector
            def _(dve):
                nc.vector.tensor_tensor(tot[:, :], sums[:, :, 0], sums[:, :, 1], ALU.add).then_inc(s_n, 1)
                dve.wait_ge(s_n, 1)
                nc.vector.reciprocal(rtot[:, :], tot[:, :]).then_inc(s_n, 1)
                dve.wait_ge(s_n, 2)
                h = sh.H[:, :, :].rearrange("p t (h d) -> p (t h) d", d=HD)
                nc.vector.tensor_tensor(h, h, rtot[:, :].unsqueeze(2).to_broadcast([P, O_ALL, HD]), ALU.mult).then_inc(s_n, 1)
                dve.wait_ge(s_n, 3)
                for m in range(KT):
                    hm = sh.H[:, :, m * P:(m + 1) * P]
                    nc.vector.tensor_tensor(hm, hm, svb[:, m::KT].unsqueeze(1).to_broadcast([P, NB, P]), ALU.mult)
        with ExitStack() as tail:
            run(nc, Transposed(nc, tail, sh, "qa_oT"))
        tmp = sb("tmp", [P, NB, D])
        s_tmp = sem("tmp")

        def out_projection(dve, t, psum):
            nc.vector.tensor_tensor(tmp[:, t, :], psum, bias[:, 2, :], ALU.add).then_inc(s_tmp, 1)
            dve.wait_ge(s_tmp, t + 1)
            return nc.vector.scalar_tensor_tensor(out=sh.X[:, t, :], in0=tmp[:, t, :], scalar=gate, in1=sh.X[:, t, :],
                                                  op0=ALU.mult, op1=ALU.add)

        project(nc, sems, "qapo", lambda part, k, t: sh.hT[:, part, k, bass.ds(t * P, P)], wp, out_projection)


def chain_on(eng, s, start=0):
    done = [start]

    def chained(ins):
        done[0] += 1
        ins.then_inc(s, 1)
        eng.wait_ge(s, done[0])
    return chained


def quantised_ffn(nc, sems, sh, a, gate):
    F = 1024
    NF = F // P
    CT = 512
    with ExitStack() as ctx:
        def sb(n, shape, dt=F32, where=ctx):
            return where.enter_context(nc.sbuf_tensor("qf_" + n, shape, dt))

        def sem(n):
            return nc.alloc_semaphore(name="qf_" + n)

        w1 = sb("w1", [P, KT * F], F16)
        w2 = sb("w2", [P, NF * D], F16)
        b1 = sb("b1", [P, NF])
        b2 = sb("b2", [P, D])
        sa = sb("sa", [P, 2])
        rsa = sb("rsa", [P, 2])
        sw = sb("sw", [P, 2])
        rsw = sb("rsw", [P, 2])
        c = sb("c", [P, 8])
        ints = sb("ints", [P, NB, D], F16)
        with ExitStack() as inner:
            f1 = sb("f1", [P, KT * F], F32, inner)
            f2 = sb("f2", [P, NF * D], F32, inner)
            Z = sb("Z", [P, NB * D], F32, inner)
            am = sb("am", [P, 2], F32, inner)
            amx = sb("amx", [P, 2], F32, inner)
            s_load, s_am, s_amx, s_c = map(sem, ("load", "am", "amx", "chain"))
            norm = Layernorm(nc, inner, sh, "qf_ln")
            with nc.Block() as block:
                @block.sync
                def _(sp):
                    sp.dma_start(f1[:, :], a["qf_w1"]).then_inc(s_load, 16)
                    sp.dma_start(f2[:, :], a["qf_w2"]).then_inc(s_load, 16)
                    sp.dma_start(b1[:, :], a["qf_b1"]).then_inc(s_load, 16)
                    sp.dma_start(b2[:, :], a["qf_b2"].partition_broadcast(P)).then_inc(s_load, 16)
                    sp.dma_start(sa[:, 0:1], a["qf_s1"].partition_broadcast(P)).then_inc(s_load, 16)
                    sp.dma_start(sa[:, 1:2], a["qf_s2"].partition_broadcast(P)).then_inc(s_load, 16)

                @block.gpsimd
                def _(pool):
                    pool.wait_ge(s_am, 2)
                    nc.gpsimd.partition_all_reduce(amx[:, :], am[:, :], P, bass.bass_isa.ReduceOp.max).then_inc(s_amx, 1)

                @block.scalar
                def _(act):
                    norm.scalar(act)

                @block.vector
                def _(dve):
                    chained = chain_on(dve, s_c)
                    norm.vector(dve)
                    norm.whole(dve)
                    dve.wait_ge(s_load, 96)
                    for i, f in enumerate((f1, f2)):
                        nc.vector.tensor_reduce(out=am[:, i:i + 1], in_=f[:, :], axis=AXX, op=ALU.max,
                                                apply_absolute_value=True).then_inc(s_am, 1)
                    chained(nc.vector.reciprocal(rsa[:, :], sa[:, :]))
                    hf = sh.H[:, :, :].rearrange("p t d -> p (t d)")
                    chained(nc.vector.tensor_scalar(Z[:, :], hf, rsa[:, 0:1], MAGIC, ALU.mult, ALU.add))
                    chained(nc.vector.tensor_scalar(Z[:, :], Z[:, :], MAGIC, 7.0, ALU.subtract, ALU.min))
                    nc.vector.tensor_scalar(ints[:, :, :].rearrange("p t d -> p (t d)"), Z[:, :], -8.0, None, ALU.max)
                    dve.wait_ge(s_amx, 1)
                    chained(nc.vector.tensor_scalar(sw[:, :], amx[:, :], 1.0 / 7.0, None, ALU.mult))
                    chained(nc.vector.reciprocal(rsw[:, :], sw[:, :]))
                    for i, (f, w) in enumerate(((f1, w1), (f2, w2))):
                        chained(nc.vector.tensor_scalar(f[:, :], f[:, :], rsw[:, i:i + 1], MAGIC, ALU.mult, ALU.add))
                        chained(nc.vector.tensor_scalar(f[:, :], f[:, :], MAGIC, 7.0, ALU.subtract, ALU.min))
                        nc.vector.tensor_scalar(w[:, :], f[:, :], -8.0, None, ALU.max)
                    chained(nc.vector.tensor_tensor(c[:, 0:2], sa[:, :], sw[:, :], ALU.mult))
                    chained(nc.vector.reciprocal(c[:, 2:4], c[:, 0:2]))
                    chained(nc.vector.tensor_tensor(c[:, 4:5], c[:, 0:1], rsa[:, 1:2], ALU.mult))
                    chained(nc.vector.tensor_tensor(c[:, 5:6], c[:, 1:2], gate, ALU.mult))
                    for i, b in enumerate((b1, b2)):
                        chained(nc.vector.tensor_scalar(b[:, :], b[:, :], c[:, 2 + i:3 + i], MAGIC, ALU.mult, ALU.add))
                        chained(nc.vector.tensor_scalar(b[:, :], b[:, :], MAGIC, 2.0 ** 31 - 1, ALU.subtract, ALU.min))
                        chained(nc.vector.tensor_scalar(b[:, :], b[:, :], -2.0 ** 31, c[:, i:i + 1], ALU.max, ALU.mult))
                    nc.vector.tensor_scalar(b1[:, :], b1[:, :], rsa[:, 1:2], None, ALU.mult)
                    chained(nc.vector.tensor_scalar(b2[:, :], b2[:, :], gate, None, ALU.mult))
                    nc.vector.tensor_tensor(sh.X[:, :, :], sh.X[:, :, :], b2[:, :].unsqueeze(1).to_broadcast([P, NB, D]), ALU.add)
        transpose_tiles(nc, sems, "qfT", KT, lambda k, t: ints[:, t, k * P:(k + 1) * P],
                        lambda t: sh.hT[:, 0, :, bass.ds(t * P, P)], sh.identh[:, :])

        r = sb("r", [P, 2, CT])
        z = sb("z", [P, 2, CT])
        hq = sb("hq", [P, 2, NF, CT], F16)
        NT = CT // P
        Hp = ctx.enter_context(nc.psum_tensor("qf_H", [P, 2, CT], F32))
        O = ctx.enter_context(nc.psum_tensor("qf_O", [P, 2, 2, D], F32))
        s_H, s_r, s_z, s_hq, s_O, s_res = map(sem, ("H", "r", "z", "hq", "O", "res"))
        with nc.Block() as block:
            @block.tensor
            def _(pe):
                def hidden(ch, f):
                    n = ch * NF + f
                    pe.wait_ge(s_r, n + 1)
                    for k in range(KT):
                        last = nc.tensor.matmul(Hp[:, f % 2, :], w1[:, k * F + f * P:k * F + (f + 1) * P],
                                                sh.hT[:, 0, k, bass.ds(ch * CT, CT)], start=k == 0, stop=k == KT - 1)
                    last.then_inc(s_H, 1)

                pe.sem_inc(s_O, 4)
                with pe.Fori(0, T // CT // 2) as pair:
                    for par in range(2):
                        ch = pair * 2 + par
                        for f in range(NF):
                            hidden(ch, f)
                        pe.wait_ge(s_hq, ch * NF + NF)
                        for bank in range(2):
                            pe.wait_ge(s_res, 2 * ch + bank + 1)
                            for i in range(2):
                                t = bank * 2 + i
                                for f in range(NF):
                                    last = nc.tensor.matmul(O[:, bank, i, :], hq[:, par, f, t * P:(t + 1) * P], w2[:, f * D:(f + 1) * D],
                                                            start=f == 0, stop=f == NF - 1)
                            last.then_inc(s_O, 1)

            @block.scalar
            def _(act):
                act.sem_inc(s_r, 2)
                with act.Fori(0, T // CT // 2) as pair:
                    for par in range(2):
                        ch = pair * 2 + par
                        for f in range(NF):
                            n = ch * NF + f
                            act.wait_ge(s_H, n + 1)
                            act.wait_ge(s_z, n + 1)
                            nc.scalar.activation(r[:, f % 2, :], Hp[:, f % 2, :], ACT.Relu, bias=b1[:, f:f + 1], scale=c[:, 4:5]).then_inc(s_r, 1)

            @block.vector
            def _(dve):
                dve.sem_inc(s_z, 2)
                dve.sem_inc(s_res, 2)

                def outputs(ch):
                    for bank in range(2):
                        dve.wait_ge(s_O, 2 * ch + bank + 5)
                        xs = sh.X[:, bass.ds(ch * NT + bank * 2, 2), :]
                        nc.vector.scalar_tensor_tensor(out=xs, in0=O[:, bank, :, :], scalar=c[:, 5:6], in1=xs, op0=ALU.mult,
                                                       op1=ALU.add).then_inc(s_res, 1)

                with dve.Fori(0, T // CT // 2) as pair:
                    for par in range(2):
                        ch = pair * 2 + par
                        dve.wait_ge(s_O, 2 * ch + 2)
                        for f in range(NF):
                            n = ch * NF + f
                            dve.wait_ge(s_r, n + 3)
                            nc.vector.tensor_scalar(z[:, f % 2, :], r[:, f % 2, :], 15.0, MAGIC, ALU.min, ALU.add).then_inc(s_z, 1)
                            dve.wait_ge(s_z, n + 3)
                            nc.vector.tensor_scalar(hq[:, par, f, :], z[:, f % 2, :], MAGIC, None, ALU.subtract).then_inc(s_hq, 1)
                        outputs(ch)


def causal_attention(nc, sems, sh, a, gate):
    NH, HD = 16, 16
    SLOT = 64
    NG = NH // 2
    HE = HD + 1
    SCALE = float(HD) ** -0.5
    with ExitStack() as ctx:
        def sb(n, shape, dt=F32):
            return ctx.enter_context(nc.sbuf_tensor("ca_" + n, shape, dt))

        def sem(n):
            return nc.alloc_semaphore(name="ca_" + n)

        cx = sb("cx", [P, NB, D])
        vx = sb("vx", [P, NB, NH, HE])
        mask = sb("mask", [P, 4, P], BF16)
        maskf = sb("maskf", [P, 4, P])
        qs = sb("qs", [P, 2, NH, SLOT], F16)
        ks = sb("ks", [P, 2, NH, SLOT], F16)
        qT = sb("qT", [P, 2, NG, P], F16)
        kT = sb("kT", [P, 2, NG, P], F16)
        kc = sb("kc", [P, 2, NH, HD])
        m = sb("m", [P, 2, 2, 4])
        d = sb("d", [P, 2, 2, 4, P])
        E = sb("E", [P, 2, 8, P])
        eT = sb("eT", [P, 2, 8, P])
        inv = sb("inv", [P, NH])
        on = sb("on", [P, NH, HD])
        S = ctx.enter_context(nc.psum_tensor("ca_S", [P, 2, 2, 4, P], F32))
        TQ = ctx.enter_context(nc.psum_tensor("ca_TQ", [P, NG, P], F16))
        ET = ctx.enter_context(nc.psum_tensor("ca_ET", [P, 8, P], F32))
        O = ctx.enter_context(nc.psum_tensor("ca_O", [P, 512], F32))
        s_load, s_set, s_set1, s_mask, s_vx, s_qlo, s_klo, s_hi, s_khi, s_T, s_tr, s_S, s_m, s_d, s_E, s_ET, s_eT, s_V, s_inv, s_on, s_res = map(sem, (
            "load", "set", "set1", "mask", "vx", "qlo", "klo", "hi", "khi", "T", "tr", "S", "m", "d", "E", "ET", "eT", "V", "inv", "on", "res"))
        norm = Layernorm(nc, ctx, sh, "ca_ln")
        with nc.Block() as block:
            @block.sync
            def _(sp):
                sp.dma_start(cx[:, :, :], a["ctx"].rearrange("b p d -> p b d")).then_inc(s_load, 16)

            @block.gpsimd
            def _(pool):
                nc.gpsimd.memset(maskf[:, :, :], 0.0).then_inc(s_set, 1)
                nc.gpsimd.memset(ks[:, :, :, :], 0.0).then_inc(s_set, 1)
                nc.gpsimd.memset(qs[:, :, :, :], 0.0).then_inc(s_set, 1)
                pool.wait_ge(s_set, 3)
                nc.gpsimd.affine_select(out=maskf[:, :, :], in_=maskf[:, :, :], compare_op=ALU.is_ge, fill=LOW,
                                        base=0, pattern=[[0, 4], [-1, P]], channel_multiplier=1).then_inc(s_mask, 1)
                pool.wait_ge(s_load, 16)
                with pool.Fori(0, NB // 2) as pair:
                    for par in range(2):
                        t = pair * 2 + par
                        k = cx[:, t, :].rearrange("p (h d) -> p h d", d=HD)
                        pool.wait_ge(s_T, 2 * t + 2)
                        for slot in (0, 2):
                            last = nc.gpsimd.tensor_copy(ks[:, par, :, slot * HD:(slot + 1) * HD], k)
                        last.then_inc(s_khi, 1)
                        nc.gpsimd.tensor_copy(kc[:, par, :, :], k).then_inc(s_khi, 1)
                        pool.wait_ge(s_khi, 2 * t + 2)
                        nc.gpsimd.tensor_tensor(ks[:, par, :, HD:2 * HD], kc[:, par, :, :], ks[:, par, :, 0:HD], ALU.subtract).then_inc(s_klo, 1)

            @block.tensor
            def _(pe):
                pe.sem_inc(s_T, 4)
                pe.sem_inc(s_S, 4)
                pe.sem_inc(s_ET, 2)
                pe.sem_inc(s_V, 2)
                pe.wait_ge(s_vx, 2)
                pe.wait_ge(s_set1, 1)

                def scores(t, par, r):
                    n = t * 2 + r
                    pe.wait_ge(s_d, n + 1)
                    for j in range(2):
                        nc.tensor.matmul(S[:, r, j, :, :], sh.ident16[:, :], mask[:, :, :], start=True, stop=False, skip_group_check=True)
                    for i in range(4):
                        for j in range(2):
                            rows = slice(j * SLOT, (j + 1) * SLOT)
                            last = nc.tensor.matmul(S[:, r, j, i, :], qT[rows, par, r * 4 + i, :], kT[rows, par, r * 4 + i, :],
                                                    start=False, stop=True, skip_group_check=True)
                    last.then_inc(s_S, 1)

                def values(t, r):
                    n = t * 2 + r
                    pe.wait_ge(s_E, n + 3)
                    pe.wait_ge(s_eT, n + 1)
                    for i in range(8):
                        last = nc.tensor.transpose(ET[:, i, :], E[:, r, i, :], sh.ident[:, :])
                    last.then_inc(s_ET, 1)
                    pe.wait_ge(s_eT, n + 2)
                    if r == 0:
                        pe.wait_ge(s_res, t + 1)
                    for i in range(8):
                        h = (r * 4 + i % 4) * 2 + i // 4
                        last = nc.tensor.matmul(O[:, h * HE:(h + 1) * HE], eT[:, r, i, :], vx[:, t, h, :], start=True, stop=True,
                                                skip_group_check=True)
                    last.then_inc(s_V, 1)

                with pe.Fori(0, NB // 2) as pair:
                    for par in range(2):
                        t = pair * 2 + par
                        for side, (s_st, stack) in enumerate(((s_qlo, qs), (s_klo, ks))):
                            pe.wait_ge(s_st, t + 1)
                            pe.wait_ge(s_tr, 2 * t + side + 1)
                            for g in range(NG):
                                last = nc.tensor.transpose(TQ[:, g, :], stack[:, par, 2 * g:2 * g + 2, :].rearrange("p h s -> p (h s)"), sh.identh[:, :])
                            last.then_inc(s_T, 1)
                        pe.wait_ge(s_tr, 2 * t + 3)
                        for r in range(2):
                            scores(t, par, r)
                        for r in range(2):
                            values(t, r)

            @block.scalar
            def _(act):
                norm.scalar(act)
                act.sem_inc(s_tr, 1)
                act.sem_inc(s_eT, 1)
                act.sem_inc(s_E, 2)
                act.wait_ge(s_load, 16)
                nc.scalar.activation(vx[:, :, :, 0:HD].rearrange("p t h d -> p (t h) d"),
                                     cx[:, :, :].rearrange("p t (h d) -> p (t h) d", d=HD), ACT.Copy).then_inc(s_vx, 1)
                act.wait_ge(s_mask, 1)
                nc.scalar.activation(mask[:, :, :], maskf[:, :, :], ACT.Copy).then_inc(s_vx, 1)
                with act.Fori(0, NB // 2) as pair:
                    for par in range(2):
                        t = pair * 2 + par
                        act.wait_ge(s_S, 2 * t + 2)
                        for side, x in enumerate((qT, kT)):
                            act.wait_ge(s_T, 2 * t + side + 5)
                            nc.scalar.activation(x[:, par, :, :], TQ[:, :, :], ACT.Copy).then_inc(s_tr, 1)
                        for r in range(2):
                            n = t * 2 + r
                            act.wait_ge(s_d, n + 3)
                            act.wait_ge(s_ET, n + 1)
                            nc.scalar.activation(E[:, r, :, :], d[:, r, :, :, :].rearrange("p a b c -> p (a b) c"), ACT.Exp, scale=SCALE).then_inc(s_E, 1)
                        for r in range(2):
                            n = t * 2 + r
                            act.wait_ge(s_ET, n + 3)
                            act.wait_ge(s_V, n + 1)
                            nc.scalar.activation(eT[:, r, :, :], ET[:, :, :], ACT.Copy).then_inc(s_eT, 1)

            @block.vector
            def _(dve):
                norm.vector(dve)
                norm.whole(dve)
                dve.sem_inc(s_d, 2)
                dve.sem_inc(s_res, 1)
                dve.wait_ge(s_set, 3)
                nc.vector.memset(vx[:, :, :, HD:HE], 1.0).then_inc(s_set1, 1)

                def stack(t, par):
                    q = sh.H[:, t, :].rearrange("p (h d) -> p h d", d=HD)
                    dve.wait_ge(s_T, 2 * t + 1)
                    for slot in (0, 1):
                        last = copy_indexed(nc, qs[:, par, :, slot * HD:(slot + 1) * HD], q)
                    last.then_inc(s_hi, 1)
                    dve.wait_ge(s_hi, t + 1)
                    nc.vector.tensor_tensor(qs[:, par, :, 2 * HD:3 * HD], q, qs[:, par, :, 0:HD], ALU.subtract).then_inc(s_qlo, 1)

                def output(t):
                    o = O[:, 0:NH * HE].rearrange("p (h d) -> p h d", d=HE)
                    dve.wait_ge(s_V, 2 * t + 4)
                    nc.vector.reciprocal(inv[:, :], o[:, :, HD]).then_inc(s_inv, 1)
                    dve.wait_ge(s_inv, t + 1)
                    nc.vector.tensor_tensor(on[:, :, :], o[:, :, 0:HD], inv[:, :].unsqueeze(2).to_broadcast([P, NH, HD]),
                                            ALU.mult).then_inc(s_on, 1)
                    dve.wait_ge(s_on, t + 1)
                    nc.vector.scalar_tensor_tensor(out=sh.X[:, t, :], in0=on[:, :, :].rearrange("p h d -> p (h d)"), scalar=gate,
                                                   in1=sh.X[:, t, :], op0=ALU.mult, op1=ALU.add).then_inc(s_res, 1)

                def tile(t, par, last):
                        for r in range(2):
                            n = t * 2 + r
                            dve.wait_ge(s_S, n + 5)
                            nc.vector.reduce_max(m[:, r, :, :], S[:, r, :, :, :], axis=AXX).then_inc(s_m, 1)
                            dve.wait_ge(s_m, n + 1)
                            dve.wait_ge(s_E, n + 1)
                            nc.vector.tensor_tensor(d[:, r, :, :, :], S[:, r, :, :, :], m[:, r, :, :].unsqueeze(3).to_broadcast([P, 2, 4, P]),
                                                    ALU.subtract).then_inc(s_d, 1)
                        if not last:
                            stack(t + 1, 1 - par)
                        output(t)

                stack(0, 0)
                with dve.Fori(0, NB // 2 - 1) as pair:
                    for par in range(2):
                        tile(pair * 2 + par, par, False)
                tile(NB - 2, 0, False)
                tile(NB - 1, 1, True)


def ternary_ffn(nc, sems, sh, a, gate):
    F = 1024
    NF = F // P
    with ExitStack() as ctx:
        def sb(n, shape, dt=F32, where=ctx):
            return where.enter_context(nc.sbuf_tensor("tf_" + n, shape, dt))

        def sem(n):
            return nc.alloc_semaphore(name="tf_" + n)

        w1 = sb("w1", [P, KT, F], F16)
        w2 = sb("w2", [P, NF, D], F16)
        s1b = sb("s1b", [P, F])
        s2b = sb("s2b", [P, D])
        inv1 = sb("inv1", [P, NB])
        ints = sb("ints", [P, NB, D], F16)
        with ExitStack() as inner:
            f1 = sb("f1", [P, KT, F], F32, inner)
            f2 = sb("f2", [P, NF, D], F32, inner)
            Z = sb("Z", [P, NB, D], F32, inner)
            ab = sb("ab", [P, KT * F], F32, inner)
            ab2 = sb("ab2", [P, NF * D], F32, inner)
            r1 = sb("r1", [P, F], F32, inner)
            r2 = sb("r2", [P, D], F32, inner)
            am = sb("am", [P, NB], F32, inner)
            ra = sb("ra", [P, NB], F32, inner)
            ones = sb("ones", [P, P], F32, inner)
            M1 = inner.enter_context(nc.psum_tensor("tf_M1", [P, F], F32))
            M2 = inner.enter_context(nc.psum_tensor("tf_M2", [P, 512], F32))
            s_load, s_abs, s_ones, s_mean, s_c = map(sem, ("load", "abs", "ones", "mean", "chain"))
            norm = Layernorm(nc, inner, sh, "tf_ln")
            with nc.Block() as block:
                @block.sync
                def _(sp):
                    sp.dma_start(f1[:, :, :].rearrange("p k n -> p (k n)"), a["tf_w1"]).then_inc(s_load, 16)
                    sp.dma_start(f2[:, :, :].rearrange("p k n -> p (k n)"), a["tf_w2"]).then_inc(s_load, 16)

                @block.scalar
                def _(act):
                    norm.scalar(act)
                    act.wait_ge(s_load, 32)
                    nc.scalar.activation(ab[:, :], f1[:, :, :].rearrange("p k n -> p (k n)"), ACT.Abs).then_inc(s_abs, 1)
                    nc.scalar.activation(ab2[:, :], f2[:, :, :].rearrange("p k n -> p (k n)"), ACT.Abs).then_inc(s_abs, 1)

                @block.tensor
                def _(pe):
                    pe.wait_ge(s_ones, 1)
                    pe.wait_ge(s_abs, 2)
                    for half in range(2):
                        for k in range(KT):
                            nc.tensor.matmul(M1[:, half * 512:(half + 1) * 512], ones[:, :],
                                             ab[:, k * F + half * 512:k * F + (half + 1) * 512], start=k == 0, stop=k == KT - 1)
                    for k in range(NF):
                        last = nc.tensor.matmul(M2[:, 0:D], ones[:, :], ab2[:, k * D:(k + 1) * D], start=k == 0, stop=k == NF - 1)
                    last.then_inc(s_mean, 1)

                @block.vector
                def _(dve):
                    chained = chain_on(dve, s_c)
                    nc.vector.memset(ones[:, :], 1.0).then_inc(s_ones, 1)
                    norm.vector(dve)
                    norm.whole(dve)
                    chained(nc.vector.tensor_reduce(out=am[:, :], in_=sh.H[:, :, :], axis=AXX, op=ALU.max, apply_absolute_value=True))
                    chained(nc.vector.tensor_scalar(inv1[:, :], am[:, :], 1e-5, 1.0 / 127.0, ALU.max, ALU.mult))
                    chained(nc.vector.reciprocal(ra[:, :], inv1[:, :]))
                    chained(nc.vector.tensor_tensor(Z[:, :, :], sh.H[:, :, :], ra[:, :].unsqueeze(2).to_broadcast([P, NB, D]), ALU.mult))
                    chained(nc.vector.tensor_scalar(Z[:, :, :], Z[:, :, :], MAGIC, MAGIC, ALU.add, ALU.subtract))
                    nc.vector.tensor_scalar(ints[:, :, :], Z[:, :, :], 127.0, -128.0, ALU.min, ALU.max)
                    dve.wait_ge(s_mean, 1)
                    for M, s, r, f, w, n in ((M1[:, :], s1b, r1, f1, w1, KT), (M2[:, 0:D], s2b, r2, f2, w2, NF)):
                        width = [P, n, s.shape[1]]
                        chained(nc.vector.tensor_scalar(s[:, :], M, 1.0 / (n * P), 1e-5, ALU.mult, ALU.max))
                        chained(nc.vector.reciprocal(r[:, :], s[:, :]))
                        chained(nc.vector.tensor_tensor(f[:, :, :], f[:, :, :], r[:, :].unsqueeze(1).to_broadcast(width), ALU.mult))
                        chained(nc.vector.tensor_scalar(f[:, :, :], f[:, :, :], MAGIC, MAGIC, ALU.add, ALU.subtract))
                        nc.vector.tensor_scalar(w[:, :, :], f[:, :, :], 1.0, -1.0, ALU.min, ALU.max)
        transpose_tiles(nc, sems, "tfT", KT, lambda k, t: ints[:, t, k * P:(k + 1) * P],
                        lambda t: sh.hT[:, 0, :, bass.ds(t * P, P)], sh.identh[:, :])

        h = sb("h", [P, 2, F])
        g = sb("g", [P, 2, F])
        z = sb("z", [P, 2, F])
        gi = sb("gi", [P, 2, F], F16)
        gT = sb("gT", [P, 2, NF, P], F16)
        am2 = sb("am2", [P, 2])
        inv2 = sb("inv2", [P, 2])
        ra2 = sb("ra2", [P, 2])
        ga2 = sb("ga2", [P, 2])
        tmp = sb("tmp", [P, 2, D])
        Hp = ctx.enter_context(nc.psum_tensor("tf_H", [P, 2, F], F32))
        TP = ctx.enter_context(nc.psum_tensor("tf_TP", [P, 2, NF, P], F16))
        O = ctx.enter_context(nc.psum_tensor("tf_O", [P, 2, 512], F32))
        s_H, s_h, s_g, s_c, s_gi, s_T, s_gT, s_O, s_tmp, s_res = map(sem, ("H", "h", "g", "chain2", "gi", "T", "gT", "O", "tmp", "res"))
        with nc.Block() as block:
            @block.tensor
            def _(pe):
                pe.sem_inc(s_T, 2)
                pe.sem_inc(s_O, 2)

                def hidden(t, par):
                    pe.wait_ge(s_h, t + 1)
                    for half in range(2):
                        for k in range(KT):
                            last = nc.tensor.matmul(Hp[:, par, half * 512:(half + 1) * 512], sh.hT[:, 0, k, bass.ds(t * P, P)],
                                                    w1[:, k, half * 512:(half + 1) * 512], start=k == 0, stop=k == KT - 1)
                    last.then_inc(s_H, 1)

                def down(t, par):
                    pe.wait_ge(s_gi, t + 3)
                    pe.wait_ge(s_gT, t + 1)
                    for f in range(NF):
                        last = nc.tensor.transpose(TP[:, par, f, :], gi[:, par, f * P:(f + 1) * P], sh.identh[:, :])
                    last.then_inc(s_T, 1)
                    pe.wait_ge(s_gT, t + 3)
                    pe.wait_ge(s_res, t + 1)
                    for f in range(NF):
                        last = nc.tensor.matmul(O[:, par, 0:D], gT[:, par, f, :], w2[:, f, :], start=f == 0, stop=f == NF - 1)
                    last.then_inc(s_O, 1)

                with pe.Fori(0, NB // 2) as pair:
                    hidden(pair * 2, 0)
                    hidden(pair * 2 + 1, 1)
                    down(pair * 2, 0)
                    down(pair * 2 + 1, 1)

            @block.scalar
            def _(act):
                act.sem_inc(s_gT, 2)
                with act.Fori(0, NB // 2) as pair:
                    for par in range(2):
                        t = pair * 2 + par
                        act.wait_ge(s_h, t + 3)
                        act.wait_ge(s_gi, t + 1)
                        nc.scalar.activation(g[:, par, :], h[:, par, :], ACT.Gelu_apprx_tanh).then_inc(s_g, 1)
                    for par in range(2):
                        t = pair * 2 + par
                        act.wait_ge(s_T, t + 3)
                        act.wait_ge(s_O, t + 1)
                        nc.scalar.activation(gT[:, par, :, :], TP[:, par, :, :], ACT.Copy).then_inc(s_gT, 1)

            @block.vector
            def _(dve):
                dve.sem_inc(s_h, 2)
                dve.sem_inc(s_gi, 2)
                dve.sem_inc(s_res, 2)
                with dve.Fori(0, NB // 2) as pair:
                    for par in range(2):
                        t = pair * 2 + par
                        dve.wait_ge(s_H, t + 1)
                        nc.vector.scalar_tensor_tensor(out=h[:, par, :], in0=Hp[:, par, :], scalar=inv1[:, bass.ds(t, 1)],
                                                       in1=s1b[:, :], op0=ALU.mult, op1=ALU.mult).then_inc(s_h, 1)
                    for par in range(2):
                        t = pair * 2 + par
                        i = slice(par, par + 1)
                        steps = iter(range(1, 9))

                        def chained(ins):
                            ins.then_inc(s_c, 1)
                            dve.wait_ge(s_c, t * 5 + next(steps))

                        dve.wait_ge(s_g, t + 1)
                        chained(nc.vector.tensor_reduce(out=am2[:, i], in_=g[:, par, :], axis=AXX, op=ALU.max, apply_absolute_value=True))
                        chained(nc.vector.tensor_scalar(inv2[:, i], am2[:, i], 1e-5, 1.0 / 127.0, ALU.max, ALU.mult))
                        nc.vector.tensor_tensor(ga2[:, i], inv2[:, i], gate, ALU.mult)
                        chained(nc.vector.reciprocal(ra2[:, i], inv2[:, i]))
                        chained(nc.vector.tensor_scalar(z[:, par, :], g[:, par, :], ra2[:, i], MAGIC, ALU.mult, ALU.add))
                        chained(nc.vector.tensor_scalar(z[:, par, :], z[:, par, :], MAGIC, 127.0, ALU.subtract, ALU.min))
                        dve.wait_ge(s_T, t + 1)
                        nc.vector.tensor_scalar(gi[:, par, :], z[:, par, :], -128.0, None, ALU.max).then_inc(s_gi, 1)
                    for par in range(2):
                        t = pair * 2 + par
                        dve.wait_ge(s_O, t + 3)
                        nc.vector.scalar_tensor_tensor(out=tmp[:, par, :], in0=O[:, par, 0:D], scalar=ga2[:, par:par + 1],
                                                       in1=s2b[:, :], op0=ALU.mult, op1=ALU.mult).then_inc(s_tmp, 1)
                        dve.wait_ge(s_tmp, t + 1)
                        nc.vector.tensor_tensor(sh.X[:, t, :], sh.X[:, t, :], tmp[:, par, :], ALU.add).then_inc(s_res, 1)


def store(nc, sems, sh, out):
    s_out = nc.alloc_semaphore(name="store_out")
    with nc.Block() as block:
        @block.sync
        def _(sp):
            sp.dma_start(out.rearrange("b p d -> p b d"), sh.X[:, :, :]).then_inc(s_out, 16)
            sp.wait_ge(s_out, 16)


@contextmanager
def own_semaphores(nc):
    before = nc.snapshot_sems()
    yield
    nc.clear_and_free_semaphores(nc.allocated_since(before))
    nc.all_engine_barrier()


def program(nc, a, out):
    with ExitStack() as sems:
        sh = make_shared(nc, sems, a["x"], a["g_xattn"], a["g_ffn"])
        with own_semaphores(nc):
            long_convolution(nc, sh, sems, a["ctx_flip"], a["ctxT_flip"], a["ssm_pad"], a["ssm_D"])
        sh.hT = sems.enter_context(nc.sbuf_tensor("hT", [P, 2, KT, T], F16))
        weights_T = nc.dram_tensor("weights_T", [MOE1.rows, T], F32, kind="Internal").ap()

        def mixture(m, layer):
            with ExitStack() as wide:
                load = ExpertWeights(nc, wide, sh, m, a[f"moe{layer}_w"], f"moe{layer}_W")
                with ExitStack() as head:
                    norm = Layernorm(nc, head, sh, f"moe{layer}_ln")
                    hT = Transposed(nc, head, sh, f"moe{layer}_hT", norm)
                    route(nc, sh, m, hT, load, a[f"moe{layer}_router"], weights_T[0:m.rows, :], f"moe{layer}_route")
                experts(nc, sems, sh, m, weights_T, sh.gates[:, 2 * layer + 1:2 * layer + 2], f"moe{layer}")

        with own_semaphores(nc):
            mixture(MOE0, 0)
        with own_semaphores(nc):
            rms_attention(nc, sems, sh, a["ctxT"], {x: a["rms_w" + x] for x in "qkv"}, sh.gates[:, 2:3])
        with own_semaphores(nc):
            mixture(MOE1, 1)
        with own_semaphores(nc):
            quantised_attention(nc, sems, sh, a, sh.gates[:, 4:5])
        with own_semaphores(nc):
            quantised_ffn(nc, sems, sh, a, sh.gates[:, 5:6])
        with own_semaphores(nc):
            causal_attention(nc, sems, sh, a, sh.gates[:, 6:7])
        with own_semaphores(nc):
            ternary_ffn(nc, sems, sh, a, sh.gates[:, 7:8])
        store(nc, sems, sh, out)


def stationary(w):
    return w.T.reshape(-1, P, w.shape[0]).transpose(1, 0, 2).reshape(P, -1)


def by_tile(gate, up, down):
    F = down.shape[0] // P
    cols = [w.reshape(KT, P, F, P).transpose(1, 2, 0, 3).reshape(P, F, KT * P) for w in (gate, up)]
    cols.append(down.reshape(F, P, D).transpose(1, 0, 2))
    return np.concatenate(cols, axis=2).reshape(P, F * TW)


def expert_layouts(n):
    gu = n["L0_ffn_gate_up_proj"]
    I = gu.shape[1] // 2
    none = np.zeros((P - I, D), gu.dtype)
    gate0 = np.concatenate([gu[:, :I].reshape(-1, D), n["L0_ffn_shared_gate_w"], none]).T
    up0 = np.concatenate([gu[:, I:].reshape(-1, D), n["L0_ffn_shared_up_w"], none]).T
    down0 = np.concatenate([n["L0_ffn_down_proj"].transpose(0, 2, 1).reshape(-1, D), n["L0_ffn_shared_down_w"].T, none])
    router0 = np.concatenate([n["L0_ffn_router_w"], n["L0_ffn_shared_expert_gate_w"]]).T
    w1 = n["L1_ffn_w1"]
    F = w1.shape[2] // 2
    gate1 = np.concatenate([w1[:, :, :F].transpose(1, 0, 2).reshape(D, -1), n["L1_ffn_w_gate"]], axis=1)
    up1 = np.concatenate([w1[:, :, F:].transpose(1, 0, 2).reshape(D, -1), n["L1_ffn_w_up"]], axis=1)
    down1 = np.concatenate([n["L1_ffn_w2"].reshape(-1, D), n["L1_ffn_w_down"]])
    return {
        "moe0_w": by_tile(gate0, up0, down0), "moe0_router": router0.reshape(KT, P, -1).transpose(1, 0, 2),
        "moe1_w": by_tile(gate1, up1, down1), "moe1_router": n["L1_ffn_router_w"].reshape(KT, P, -1).transpose(1, 0, 2),
    }


def kernel(**inputs):
    import concourse.bacc as bacc
    from concourse.bass_utils import run_bass_kernel_spmd

    n = {k: np.asarray(v) for k, v in inputs.items()}
    c = n["ctx_2048"]
    ssm = n["L0_xattn_ssm_kernel"]
    arrays = {
        "x": n["x"], "g_xattn": n["g_xattn"], "g_ffn": n["g_ffn"],
        "ctx_flip": c.reshape(NB, P, KT, P)[:, :, :, ::-1].reshape(NB, P, D),
        "ctxT_flip": c.reshape(NB, P, KT, P)[:, :, :, ::-1].transpose(3, 0, 2, 1),
        "ssm_pad": np.concatenate([np.zeros((16, P - 1), ssm.dtype), ssm], axis=1),
        "ssm_D": n["L0_xattn_D"],
    }
    arrays |= expert_layouts(n)
    kv = np.concatenate([n["L1_xattn_Wk"], n["L1_xattn_Wv"]])
    arrays |= {
        "ctxT": stationary(c.reshape(T, D)),
        "rms_wq": stationary(n["L1_xattn_Wq"]), "rms_wk": stationary(kv[0::2]), "rms_wv": stationary(kv[1::2]),
    }
    wkv, bkv = n["L2_xattn_Wkv"], n["L2_xattn_bkv"]
    arrays |= {
        "qa_wq": stationary(n["L2_xattn_Wq"].T), "qa_wk": stationary(wkv[:, :D].T), "qa_wv": stationary(wkv[:, D:].T),
        "qa_wp": stationary(n["L2_xattn_Wp"].T), "qa_bq": n["L2_xattn_bq"], "qa_bk": bkv[:D],
        "qa_bv": bkv[D:].reshape(KT, P).T, "qa_bp": n["L2_xattn_bp"],
    }
    arrays |= {
        "qf_w1": stationary(n["L2_ffn_W1"]), "qf_w2": stationary(n["L2_ffn_W2"]),
        "qf_b1": n["L2_ffn_b1"].reshape(-1, P).T, "qf_b2": n["L2_ffn_b2"], "qf_s1": n["L2_ffn_s_act1"], "qf_s2": n["L2_ffn_s_act2"],
        "ctx": c, "tf_w1": stationary(n["L3_ffn_w1"]), "tf_w2": stationary(n["L3_ffn_w2"]),
    }
    arrays = {f"in_{k}": np.ascontiguousarray(v) for k, v in arrays.items()}
    nc = bacc.Bacc("TRN2", target_bir_lowering=False, num_devices=1)
    args = {k[3:]: nc.dram_tensor(k, v.shape, mybir.dt.from_np(v.dtype), kind="ExternalInput").ap() for k, v in arrays.items()}
    out = nc.dram_tensor("out_0_dram", (NB, P, D), F32, kind="ExternalOutput").ap()
    program(nc, args, out)
    r = run_bass_kernel_spmd(nc, [arrays], core_ids=[0])
    return r.results[0]["out_0_dram"]
```

```python
from contextlib import ExitStack, contextmanager
import numpy as np
import concourse.bass as bass
from concourse import mybir


F32 = mybir.dt.float32
F16 = mybir.dt.float16
BF16 = mybir.dt.bfloat16
ALU = mybir.AluOpType
ACT = mybir.ActivationFunctionType
AXX = mybir.AxisListType.X

P = 128
NB = 16
D = 256
KT = D // P
T = NB * P
EPS = 1e-5


class Shared:
    pass


def make_shared(nc, ctx, x, g_xattn, g_ffn):
    sh = Shared()

    def sb(n, shape, dt=F32):
        return ctx.enter_context(nc.sbuf_tensor(n, shape, dt))

    sh.X = sb("X", [P, NB, D])
    sh.H = sb("H", [P, NB, D])
    sh.gates = sb("gates", [P, 8])
    graw = sb("graw", [P, 8])
    sh.eps = sb("eps", [P, 1])
    sh.ident = sb("ident", [P, P])
    sh.ident16 = sb("ident16", [P, P], BF16)
    sh.identh = sb("identh", [P, P], F16)
    s_load = sh.s_load = nc.alloc_semaphore(name="setup_load")
    s_ident = nc.alloc_semaphore(name="setup_ident")
    s_set = sh.s_set = nc.alloc_semaphore(name="setup_set")
    with nc.Block() as block:
        @block.sync
        def _(sp):
            sp.dma_start(sh.X[:, :, :], x.rearrange("b p d -> p b d")).then_inc(s_load, 16)
            sp.dma_start(graw[:, 0:4], g_xattn.partition_broadcast(P)).then_inc(s_load, 16)
            sp.dma_start(graw[:, 4:8], g_ffn.partition_broadcast(P)).then_inc(s_load, 16)

        @block.gpsimd
        def _(pool):
            nc.gpsimd.memset(sh.eps[:, :], EPS).then_inc(s_set, 1)
            nc.gpsimd.memset(sh.ident[:, :], 0.0).then_inc(s_set, 1)
            pool.wait_ge(s_set, 2)
            nc.gpsimd.affine_select(out=sh.ident[:, :], in_=sh.ident[:, :], compare_op=ALU.not_equal, fill=1.0,
                                    base=0, pattern=[[-1, P]], channel_multiplier=1).then_inc(s_ident, 1)

        @block.vector
        def _(dve):
            dve.wait_ge(s_ident, 1)
            nc.vector.tensor_copy(sh.ident16[:, :], sh.ident[:, :])
            nc.vector.tensor_copy(sh.identh[:, :], sh.ident[:, :])

    sh.graw = graw
    return sh


def make_gates(nc, sh, act):
    act.wait_ge(sh.s_load, 48)
    for i in range(2):
        nc.scalar.activation(sh.gates[:, i::2], sh.graw[:, 4 * i:4 * i + 4], ACT.Tanh).then_inc(sh.s_set, 1)


class Layernorm:

    def __init__(self, nc, ctx, sh, name):
        self.nc, self.sh = nc, sh
        self.s_stats, self.s_mv, self.s_std, self.s_rstd, self.s_norm = (
            nc.alloc_semaphore(name=f"{name}_{x}") for x in ("stats", "mv", "std", "rstd", "norm"))
        self.stats = ctx.enter_context(nc.sbuf_tensor(name + "_stats", [P, NB, 6], F32))
        self.mv = ctx.enter_context(nc.sbuf_tensor(name + "_mv", [P, NB, 2], F32))
        self.std = ctx.enter_context(nc.sbuf_tensor(name + "_std", [P, NB], F32))
        self.rstd = ctx.enter_context(nc.sbuf_tensor(name + "_rstd", [P, NB], F32))

    def statistics(self, dve):
        nc = self.nc
        with dve.Fori(0, NB // 4) as four:
            for i in range(4):
                t = bass.ds(four * 4 + i, 1)
                nc.vector.bn_stats(self.stats[:, t, :], self.sh.X[:, t, :]).then_inc(self.s_stats, 1)
        dve.wait_ge(self.s_stats, NB)
        for t in range(NB):
            nc.vector.bn_aggr(self.mv[:, t, :], self.stats[:, t, :]).then_inc(self.s_mv, 1)
        dve.wait_ge(self.s_std, 1)
        nc.vector.reciprocal(self.rstd[:, :], self.std[:, :]).then_inc(self.s_rstd, 1)
        dve.wait_ge(self.s_rstd, 1)

    def tile(self, t):
        self.nc.vector.tensor_scalar(self.sh.H[:, bass.ds(t, 1), :], self.sh.X[:, bass.ds(t, 1), :],
                                     self.mv[:, bass.ds(t, 1), 0], self.rstd[:, bass.ds(t, 1)],
                                     ALU.subtract, ALU.mult).then_inc(self.s_norm, 1)

    def pair(self, dve, p):
        for par in range(2):
            self.tile(p * 2 + par)

    def vector(self, dve):
        self.statistics(dve)
        with dve.Fori(0, NB // 4) as four:
            for i in range(4):
                self.tile(four * 4 + i)

    def scalar(self, act):
        act.wait_ge(self.s_mv, NB)
        self.nc.scalar.activation(self.std[:, :], self.mv[:, :, 1], ACT.Sqrt, bias=self.sh.eps[:, 0:1]).then_inc(self.s_std, 1)

    def whole(self, eng):
        eng.wait_ge(self.s_norm, NB)


def long_convolution(nc, sh, ctx_flip, ctxT_flip, ssm_pad, ssm_D):
    NH, HD = 16, 8
    W = D + P
    HG = 2
    NG = NH // HG
    CG = 32 // HD
    head = lambda g, i: (g * HG + i) % 4 * CG + (g * HG + i) // 4
    R = 3 * HD
    with ExitStack() as ctx:
        def sb(n, shape, dt=F32):
            return ctx.enter_context(nc.sbuf_tensor("conv_" + n, shape, dt))

        def sem(n):
            return nc.alloc_semaphore(name="conv_" + n)

        toep = sb("toep", [P, NH, W])
        anti = sb("anti", [P, P])
        dvals = sb("dvals", [P, NH])
        kf = sb("kf", [P, NB, D])
        vt = sb("vt", [P, NB, KT, P])
        parts = sb("parts", [P, 4, NB, D], F16)
        qst = sb("qst", [R, 2, NH, D], F16)
        kst = sb("kst", [R, 2, NH, D], F16)
        vpad = sb("vpad", [P, 2, KT, NH, P])
        A = sb("A", [P, 4, HG, W])
        rows = nc.dram_tensor("conv_rows", [4, NB, P, D], F16, kind="Internal").ap()
        s_rows = sem("rows")
        gate = sh.gates[:, 0:1]
        S = ctx.enter_context(nc.psum_tensor("conv_S", [P, 2, HG, 512], F32))
        Y = ctx.enter_context(nc.psum_tensor("conv_Y", [P, 2, 512], F32))
        s_kf, s_vt = sem("kf"), sem("vt")
        s_load, s_zero, s_anti, s_toep = sem("load"), sem("zero"), sem("anti"), sem("toep")
        s_hi, s_lo = sem("hi"), sem("lo")
        s_stack = [sem("stack0"), sem("stack1")]
        s_vpad = sem("vpad")
        s_S, s_A, s_Y, s_res = sem("S"), sem("A"), sem("Y"), sem("res")
        norm = Layernorm(nc, ctx, sh, "conv_ln")
        with nc.Block() as block:
            @block.sync
            def _(sp):
                sp.dma_start(kf[:, :, :], ctx_flip.rearrange("b p d -> p b d")).then_inc(s_kf, 16)
                for h in range(NH):
                    sp.dma_start(toep[:, h, 0:D], bass.AP(ssm_pad.tensor, h * (P - 1 + D), [[1, P], [1, D]])).then_inc(s_load, 16)
                sp.dma_start(dvals[:, :], ssm_D.partition_broadcast(P)).then_inc(s_load, 16)
                sp.dma_start(vt[:, :, :, :], ctxT_flip).then_inc(s_vt, 16)
                for part, s_part, n in ((2, s_hi, 1), (3, s_lo, 1), (0, s_hi, 2), (1, s_lo, 2)):
                    sp.wait_ge(s_part, n)
                    sp.dma_start(rows[part, :, :, :].rearrange("b p l -> p b l"), parts[:, part, :, :]).then_inc(s_rows, 16)
                sp.wait_ge(s_rows, 64)
                with sp.Fori(0, NB // 2) as pair:
                    for par in range(2):
                        b = pair * 2 + par
                        sp.wait_ge(s_S, b * NG + NG)
                        for stack, order in ((qst, (0, 0, 1)), (kst, (2, 3, 2))):
                            for r, part in enumerate(order):
                                sp.dma_start(stack[r * HD:(r + 1) * HD, par, :, :],
                                             rows[part, b, :, :].rearrange("(h i) l -> i h l", i=HD)).then_inc(s_stack[par], 16)

            @block.scalar
            def _(act):
                make_gates(nc, sh, act)
                norm.scalar(act)
                act.wait_ge(s_kf, 16)
                nc.scalar.activation(parts[:, 2, :, :], kf[:, :, :], ACT.Copy).then_inc(s_hi, 1)
                norm.whole(act)
                nc.scalar.activation(parts[:, 0, :, :], sh.H[:, :, :], ACT.Copy).then_inc(s_hi, 1)

            @block.gpsimd
            def _(pool):
                nc.gpsimd.memset(vpad[:, :, :, :, :], 0.0).then_inc(s_zero, 1)
                nc.gpsimd.memset(anti[:, :], 0.0).then_inc(s_zero, 1)
                pool.wait_ge(s_zero, 2)
                nc.gpsimd.affine_select(out=anti[:, :], in_=anti[:, :], compare_op=ALU.not_equal, fill=1.0,
                                        base=-(P - 1), pattern=[[1, P]], channel_multiplier=1).then_inc(s_anti, 1)
                pool.wait_ge(s_vt, 16)
                with pool.Fori(0, NB // 2) as pair:
                    for par in range(2):
                        b = pair * 2 + par
                        pool.wait_ge(s_Y, b * NG + NG)
                        for mt in range(KT):
                            flat = vpad[:, par, mt, :, :].rearrange("p h c -> p (h c)")
                            dst = bass.AP(flat.tensor, flat.offset, [flat.ap[0], [P + HD, NH], [1, HD]])
                            nc.gpsimd.tensor_copy(dst, vt[:, b, mt, :].rearrange("p (h j) -> p h j", j=HD)).then_inc(s_vpad, 1)

            @block.vector
            def _(dve):
                dve.sem_inc(s_A, 2)
                dve.sem_inc(s_res, 2)
                dve.wait_ge(sh.s_load, 48)
                norm.vector(dve)
                dve.wait_ge(s_hi, 1)
                nc.vector.tensor_tensor(parts[:, 3, :, :], kf[:, :, :], parts[:, 2, :, :], ALU.subtract).then_inc(s_lo, 1)
                dve.wait_ge(s_hi, 2)
                nc.vector.tensor_tensor(parts[:, 1, :, :], sh.H[:, :, :], parts[:, 0, :, :], ALU.subtract).then_inc(s_lo, 1)
                dve.wait_ge(sh.s_set, 4)
                dve.wait_ge(s_load, 16 * (NH + 1))
                dve.wait_ge(s_anti, 1)
                for h in range(NH):
                    nc.vector.scalar_tensor_tensor(out=toep[:, h, 0:P], in0=anti[:, :], scalar=dvals[:, h:h + 1],
                                                   in1=toep[:, h, 0:P], op0=ALU.mult, op1=ALU.add).then_inc(s_toep, 1)
                dve.wait_ge(s_toep, NH)
                nc.vector.tensor_copy(toep[:, :, D:W], toep[:, :, 0:P]).then_inc(s_toep, 1)
                dve.wait_ge(s_toep, NH + 1)

                def weigh(b, g):
                    k = b * NG + g
                    dve.wait_ge(s_S, k + 2 * NG + 1)
                    dve.wait_ge(s_Y, k + 2 * NG - 3)
                    nc.vector.tensor_tensor(A[:, g % 4, :, :], S[:, g % 2, :, 0:W],
                                            toep[:, head(g, 0):head(g, 1) + 1:CG, :], ALU.mult).then_inc(s_A, 1)

                def tile(b, par, last):
                    for g in range(2, NG):
                        weigh(b, g)
                    if not last:
                        weigh(b + 1, 0)
                        weigh(b + 1, 1)
                    dve.wait_ge(s_Y, b * NG + 3 * NG)
                    nc.vector.scalar_tensor_tensor(out=sh.X[:, b, :], in0=Y[:, par, 0:D], scalar=gate,
                                                   in1=sh.X[:, b, :], op0=ALU.mult, op1=ALU.add).then_inc(s_res, 1)

                weigh(0, 0)
                weigh(0, 1)
                with dve.Fori(0, NB // 2 - 1) as pair:
                    for par in range(2):
                        tile(pair * 2 + par, par, False)
                tile(NB - 2, 0, False)
                tile(NB - 1, 1, True)

            @block.tensor
            def _(pe):
                pe.sem_inc(s_S, 2 * NG)
                pe.sem_inc(s_Y, 2 * NG)

                def scores(b, par, g):
                    k = b * NG + g
                    pe.wait_ge(s_A, k + 1)
                    for i in range(HG):
                        h = head(g, i)
                        nc.tensor.matmul(S[:, g % 2, i, 0:D], kst[:, par, h, 0:P], qst[:, par, h, :], start=True, stop=True)
                        last = nc.tensor.matmul(S[:, g % 2, i, D:W], kst[:, par, h, P:D], qst[:, par, h, P:D], start=True, stop=True)
                    last.then_inc(s_S, 1)

                def values(b, par, g):
                    pe.wait_ge(s_A, b * NG + g + 3)
                    for i in range(HG):
                        h = head(g, i)
                        rows = slice(h // CG * 32, h // CG * 32 + 32)
                        nc.tensor.matmul(Y[rows, par, 0:D], vpad[:, par, 0, h, rows], A[:, g % 4, i, 0:D],
                                         start=h % CG == 0, stop=False, skip_group_check=True)
                        last = nc.tensor.matmul(Y[rows, par, P:D], vpad[:, par, 1, h, rows], A[:, g % 4, i, D:W],
                                                start=False, stop=h % CG == CG - 1, skip_group_check=True)
                    last.then_inc(s_Y, 1)

                def tile(b, par, pair_next, last):
                    pe.wait_ge(s_vpad, b * 2 + 2)
                    pe.wait_ge(s_res, b + 1)
                    for g in range(NG):
                        if g + 2 < NG:
                            scores(b, par, g + 2)
                        elif not last:
                            if g + 2 == NG:
                                pe.wait_ge(s_stack[1 - par], pair_next * 96 + 96)
                            scores(b + 1, 1 - par, g + 2 - NG)
                        values(b, par, g)

                pe.wait_ge(s_stack[0], 96)
                scores(0, 0, 0)
                scores(0, 0, 1)
                with pe.Fori(0, NB // 2 - 1) as pair:
                    tile(pair * 2, 0, pair, False)
                    tile(pair * 2 + 1, 1, pair + 1, False)
                tile(NB - 2, 0, NB // 2 - 1, False)
                tile(NB - 1, 1, None, True)


def copy_indexed(nc, out, in_):
    return nc.vector.tensor_scalar(out, in_, 1.0, None, ALU.mult)


class Transposed:
    PAIRS = NB // 2

    def __init__(self, nc, ctx, sh, name, norm=None):
        self.nc, self.sh, self.norm = nc, sh, norm
        self.s_hi, self.s_lo, self.s_T, self.s_even, self.s_odd = (
            nc.alloc_semaphore(name=f"{name}_{n}") for n in ("hi", "lo", "T", "even", "odd"))
        self.parts = ctx.enter_context(nc.sbuf_tensor(name + "_parts", [P, 2, 2, 2, D], F16))
        self.TP = ctx.enter_context(nc.psum_tensor(name + "_TP", [P, 2, 2, 8 * P], F16))

    def in_pairs(self, eng, ahead, behind):
        ahead(0, 0)
        with eng.Fori(0, self.PAIRS // 2 - 1) as q:
            for i in range(2):
                ahead(q * 2 + i + 1, (i + 1) % 2)
                behind(q * 2 + i, i)
        ahead(self.PAIRS - 1, 1)
        behind(self.PAIRS - 2, 0)
        behind(self.PAIRS - 1, 1)

    def target(self, p, par):
        return self.sh.hT[:, :, :, bass.ds((p * 2 + par) * P, P)]

    def transposes(self, slot, par):
        return self.TP[:, slot, par, 0:2 * KT * P].rearrange("p (a k c) -> p a k c", a=2, k=KT)

    def vector(self, dve):
        nc, sh = self.nc, self.sh
        if self.norm:
            self.norm.statistics(dve)
        dve.sem_inc(self.s_odd, 2)

        def ahead(p, slot):
            if self.norm:
                self.norm.pair(dve, p)
            for par in range(2):
                t = p * 2 + par
                dve.wait_ge(self.s_hi, t + 1)
                nc.vector.tensor_tensor(self.parts[:, slot, par, 1, :], sh.H[:, t, :], self.parts[:, slot, par, 0, :],
                                        ALU.subtract).then_inc(self.s_lo, 1)

        def behind(p, slot):
            dve.wait_ge(self.s_T, p * 2 + 2 + 4)
            copy_indexed(nc, self.target(p, 1), self.transposes(slot, 1)).then_inc(self.s_odd, 1)

        self.in_pairs(dve, ahead, behind)

    def scalar(self, act):
        nc, sh = self.nc, self.sh
        if self.norm:
            self.norm.scalar(act)
        act.sem_inc(self.s_even, 2)

        def ahead(p, slot):
            for par in range(2):
                t = p * 2 + par
                if self.norm:
                    act.wait_ge(self.norm.s_norm, t + 1)
                act.wait_ge(self.s_T, t + 1)
                nc.scalar.activation(self.parts[:, slot, par, 0, :], sh.H[:, t, :], ACT.Copy).then_inc(self.s_hi, 1)

        def behind(p, slot):
            act.wait_ge(self.s_T, p * 2 + 1 + 4)
            nc.scalar.activation(self.target(p, 0), self.transposes(slot, 0), ACT.Copy).then_inc(self.s_even, 1)

        self.in_pairs(act, ahead, behind)

    def tensor(self, pe):
        nc = self.nc
        pe.sem_inc(self.s_T, 4)
        with pe.Fori(0, self.PAIRS // 2) as q:
            for slot in range(2):
                p = q * 2 + slot
                for par in range(2):
                    pe.wait_ge(self.s_lo, p * 2 + par + 1)
                    pe.wait_ge((self.s_even, self.s_odd)[par], p + 1)
                    out = self.transposes(slot, par)
                    for part in range(2):
                        for k in range(KT):
                            last = nc.tensor.transpose(out[:, part, k, :], self.parts[:, slot, par, part, k * P:(k + 1) * P],
                                                       self.sh.identh[:, :])
                    last.then_inc(self.s_T, 1)

    def sync(self, sp):
        pass

    def whole(self, eng):
        eng.wait_ge(self.s_even, self.PAIRS + 2)
        eng.wait_ge(self.s_odd, self.PAIRS + 2)


def run(nc, *steps):
    with nc.Block() as block:
        @block.sync
        def _(sp):
            for step in steps:
                step.sync(sp)

        @block.scalar
        def _(act):
            for step in steps:
                step.scalar(act)

        @block.vector
        def _(dve):
            for step in steps:
                step.vector(dve)

        @block.tensor
        def _(pe):
            for step in steps:
                step.tensor(pe)


PRODUCTS = ((0, 0), (0, 1), (1, 0))


class MoE:

    def __init__(self, experts, top, tiles, rows, chunk):
        self.experts, self.top, self.tiles, self.rows, self.chunk = experts, top, tiles, rows, chunk


MOE0 = MoE(64, 8, 33, 66, 3)
MOE1 = MoE(8, 2, 40, 80, 2)
TW = 6 * P


class ExpertWeights:

    FIRST = 3

    def __init__(self, nc, ctx, sh, m, w, name):
        self.nc, self.sh, self.m, self.w = nc, sh, m, w
        self.n = m.tiles // m.chunk
        self.s_load = [nc.alloc_semaphore(name=f"{name}_load{i}") for i in range(self.n)]
        self.s_hi, self.s_lo = (nc.alloc_semaphore(name=f"{name}_{x}") for x in ("hi", "lo"))
        sh.W = ctx.enter_context(nc.sbuf_tensor(name, [P, m.tiles + 2 * m.chunk, 2, TW], F16))

    def source(self, i):
        C = self.m.chunk
        return self.sh.W[:, (i + 2) * C:(i + 3) * C, :, :].rearrange("p f a c -> p (f a c)").bitcast(F32)

    def parts(self, i, part):
        C = self.m.chunk
        return self.sh.W[:, i * C:(i + 1) * C, part, :]

    def sync(self, sp):
        C = self.m.chunk * TW
        for i in range(self.n):
            sp.dma_start(self.source(i), self.w[:, i * C:(i + 1) * C]).then_inc(self.s_load[i], 16)

    def landed(self, sp):
        for s_load in self.s_load:
            sp.wait_ge(s_load, 16)

    def scalar(self, act):
        for i in range(self.FIRST):
            act.wait_ge(self.s_load[i], 16)
            if i >= 2:
                act.wait_ge(self.s_lo, i - 1)
            self.nc.scalar.activation(self.parts(i, 0), self.source(i).rearrange("p (f c) -> p f c", c=TW), ACT.Copy).then_inc(self.s_hi, 1)

    def vector(self, dve):
        for i in range(self.FIRST):
            dve.wait_ge(self.s_hi, i + 1)
            self.nc.vector.tensor_tensor(self.parts(i, 1), self.source(i).rearrange("p (f c) -> p f c", c=TW), self.parts(i, 0),
                                         ALU.subtract).then_inc(self.s_lo, 1)

    def tile(self, f):
        return self.sh.W[:, f + 2 * self.m.chunk, :, :].rearrange("p a c -> p (a c)").bitcast(F32)


LOW = -1.0e30
TAKEN = -3.0e38


def route(nc, sh, m, hT, load, router, weights_T, name):
    NE = m.experts
    NR = 65 if m is MOE0 else NE
    NL = NE + 8
    with ExitStack() as ctx:
        def sb(n, shape, dt=F32):
            return ctx.enter_context(nc.sbuf_tensor(f"{name}_{n}", shape, dt))

        def sem(n):
            return nc.alloc_semaphore(name=f"{name}_{n}")

        rw = sb("rw", [P, KT, NR])
        rwp = sb("rwp", [P, 2, KT, NR], F16)
        L = sb("L", [P, NB, NL])
        rest = sb("rest", [P, NB, NL])
        top8 = sb("top8", [P, NB, 8])
        chosen = sb("chosen", [P, NB, 8])
        shifted = sb("shifted", [P, NB, NE])
        e = sb("e", [P, NB, NE])
        em = sb("em", [P, NB, NE])
        total = sb("total", [P, NB])
        inv = sb("inv", [P, NB])
        sig = sb("sig", [P, NB])
        sig1 = sb("sig1", [P, NB])
        comb = sb("comb", [P, NB, m.rows])
        combT = sb("combT", [m.rows, T])
        LP = ctx.enter_context(nc.psum_tensor(name + "_LP", [P, NB, P], F32))
        CP = LP
        s_load, s_hi, s_lo, s_L, s_d, s_e, s_comb, s_CT, s_ct, s_out, s_Lc = map(sem, (
            "load", "hi", "lo", "L", "chain", "exp", "comb", "CT", "ct", "out", "Lc"))
        with nc.Block() as block:
            @block.sync
            def _(sp):
                sp.dma_start(rw[:, :, :], router).then_inc(s_load, 16)
                load.sync(sp)
                load.landed(sp)
                sp.wait_ge(s_ct, 1)
                sp.dma_start(weights_T, combT[:, :]).then_inc(s_out, 16)
                sp.wait_ge(s_out, 16)

            @block.scalar
            def _(act):
                hT.scalar(act)
                act.wait_ge(s_load, 16)
                nc.scalar.activation(rwp[:, 0, :, :], rw[:, :, :], ACT.Copy).then_inc(s_hi, 1)
                load.scalar(act)
                act.wait_ge(s_Lc, 2)
                nc.scalar.activation(e[:, :, :], shifted[:, :, :], ACT.Exp).then_inc(s_e, 1)
                if m is MOE0:
                    nc.scalar.activation(sig[:, :], LP[:, :, NE], ACT.Exp, scale=-1.0).then_inc(s_e, 1)
                act.wait_ge(s_CT, 1)
                nc.scalar.activation(combT[:, :], CP[0:m.rows, :, :].rearrange("p t c -> p (t c)"), ACT.Copy).then_inc(s_ct, 1)

            @block.tensor
            def _(pe):
                hT.tensor(pe)
                hT.whole(pe)
                pe.wait_ge(s_lo, 1)
                with pe.Fori(0, NB // 4) as four:
                    for j in range(4):
                        t = four * 4 + j
                        i = 0
                        for a, b in PRODUCTS:
                            for k in range(KT):
                                last = nc.tensor.matmul(LP[:, bass.ds(t, 1), 0:NR], sh.hT[:, a, k, bass.ds(t * P, P)], rwp[:, b, k, :],
                                                        start=i == 0, stop=i == 5)
                                i += 1
                        last.then_inc(s_L, 1)
                pe.wait_ge(s_comb, 1)
                for t in range(NB):
                    last = nc.tensor.transpose(CP[0:m.rows, t, :], comb[:, t, :], sh.ident[:, :])
                last.then_inc(s_CT, 1)

            @block.vector
            def _(dve):
                done = [0]

                def chained(ins):
                    done[0] += 1
                    ins.then_inc(s_d, 1)
                    dve.wait_ge(s_d, done[0])

                hT.vector(dve)
                dve.wait_ge(s_hi, 1)
                nc.vector.tensor_tensor(rwp[:, 1, :, :], rw[:, :, :], rwp[:, 0, :, :], ALU.subtract).then_inc(s_lo, 1)
                nc.vector.memset(L[:, :, NE:NL], LOW)
                nc.vector.memset(chosen[:, :, :], LOW)
                nc.vector.memset(comb[:, :, :], 1.0 if m is MOE1 else 0.0)
                load.vector(dve)
                dve.wait_ge(s_L, NB)
                chained(nc.vector.tensor_copy(L[:, :, 0:NE], LP[:, :, 0:NE]))
                for t in range(NB):
                    last = nc.vector.max(top8[:, t, :], L[:, t, :])
                chained(last)
                nc.vector.tensor_copy(chosen[:, :, 0:m.top], top8[:, :, 0:m.top]).then_inc(s_Lc, 1)
                nc.vector.tensor_tensor(shifted[:, :, :], L[:, :, 0:NE], top8[:, :, 0:1].to_broadcast([P, NB, NE]),
                                        ALU.subtract).then_inc(s_Lc, 1)
                dve.wait_ge(s_Lc, 2)
                for t in range(NB):
                    last = nc.vector.match_replace(rest[:, t, :], chosen[:, t, :], L[:, t, :], TAKEN)
                chained(last)
                dve.wait_ge(s_e, 2 if m is MOE0 else 1)
                chained(nc.vector.scalar_tensor_tensor(out=em[:, :, :], in0=rest[:, :, 0:NE], scalar=-2.0e38, in1=e[:, :, :],
                                                       op0=ALU.is_le, op1=ALU.mult))
                chained(nc.vector.reduce_sum(total[:, :], em[:, :, :], axis=AXX))
                chained(nc.vector.reciprocal(inv[:, :], total[:, :]))
                rep = 64 // NE
                dst = comb[:, :, 0:64].rearrange("p t (e r) -> p t e r", r=rep)
                if rep == 1:
                    chained(nc.vector.tensor_tensor(comb[:, :, 0:64], em[:, :, :], inv[:, :].unsqueeze(2).to_broadcast([P, NB, NE]), ALU.mult))
                    chained(nc.vector.tensor_scalar_add(sig1[:, :], sig[:, :], 1.0))
                    nc.vector.reciprocal(comb[:, :, 64], sig1[:, :]).then_inc(s_comb, 1)
                else:
                    chained(nc.vector.tensor_tensor(shifted[:, :, :], em[:, :, :], inv[:, :].unsqueeze(2).to_broadcast([P, NB, NE]), ALU.mult))
                    nc.vector.tensor_copy(dst, shifted[:, :, :].unsqueeze(3).to_broadcast([P, NB, NE, rep])).then_inc(s_comb, 1)

def experts(nc, sh, m, load, weights_T, gate, name):
    CT = 512
    NC = T // CT
    NF = m.tiles
    uses = ((NF + 1) // 2, NF // 2)
    with ExitStack() as ctx:
        def sb(n, shape, dt=F32):
            return ctx.enter_context(nc.sbuf_tensor(f"{name}_{n}", shape, dt))

        def sems2(n):
            return [nc.alloc_semaphore(name=f"{name}_{n}{u}") for u in range(2)]

        wb = sb("wb", [P, 2, CT])
        sg = sb("sg", [P, 2, CT])
        t1 = sb("t1", [P, 2, CT])
        a = sb("a", [P, 2, CT])
        ap = sb("ap", [P, 2, 2, CT], F16)
        zero = sb("zero", [P, CT], F16)
        G = ctx.enter_context(nc.psum_tensor(name + "_G", [P, 2, CT], F32))
        U = ctx.enter_context(nc.psum_tensor(name + "_U", [P, 2, CT], F32))
        O = ctx.enter_context(nc.psum_tensor(name + "_O", [P, CT // P, D], F32))
        s_wb, s_G, s_U, s_sg, s_t1, s_a, s_hi, s_lo, s_O = map(sems2, ("wb", "G", "U", "sg", "t1", "a", "hi", "lo", "O"))
        s_res = nc.alloc_semaphore(name=name + "_res")
        s_zero = nc.alloc_semaphore(name=name + "_zero")

        READY = load.FIRST * m.chunk
        s_whi, s_wlo = (nc.alloc_semaphore(name=f"{name}_{x}") for x in ("whi", "wlo"))

        def first_steps(eng, split, step):
            both = (NF - READY) // 2
            with eng.Fori(0, both) as i:
                for u in range(2):
                    step(i * 2 + u, u, i, split)
            with eng.Fori(0, NF // 2 - both) as i:
                for u in range(2):
                    step((i + both) * 2 + u, u, i + both)
            if NF % 2:
                step(NF - 1, 0, NF // 2)

        def steps(eng, c, step):
            with eng.Fori(0, NF // 2) as i:
                for u in range(2):
                    step(i * 2 + u, u, c * uses[u] + i)
            if NF % 2:
                step(NF - 1, 0, c * uses[0] + NF // 2)

        with nc.Block() as block:
            @block.sync
            def _(sp):
                def step(c, f, u, n):
                    sp.wait_ge(s_t1[u], n + 1)
                    for half in range(2):
                        src = weights_T[bass.ds(f * 2 + half, 1), bass.ds(c * CT, CT)].to_broadcast([P // 2, CT])
                        sp.dma_start(wb[half * 64:half * 64 + 64, u, :], src).then_inc(s_wb[u], 16)

                with sp.Fori(0, NC) as c:
                    steps(sp, c, lambda f, u, n: step(c, f, u, n))

            @block.scalar
            def _(act):
                def step(f, u, n, split=None):
                    act.wait_ge(s_G[u], n + 1)
                    nc.scalar.activation(sg[:, u, :], G[:, u, :], ACT.Silu).then_inc(s_sg[u], 1)
                    if split:
                        split(f + READY)
                    act.wait_ge(s_a[u], n + 2)
                    act.wait_ge(s_O[u], n + 1)
                    nc.scalar.activation(ap[:, u, 0, :], a[:, u, :], ACT.Copy).then_inc(s_hi[u], 1)

                act.sem_inc(s_sg[0], 1)
                act.sem_inc(s_sg[1], 1)

                def split(f):
                    act.wait_ge(s_wlo, f - 2 * m.chunk + 1)
                    nc.scalar.activation(sh.W[:, f, 0, :], load.tile(f), ACT.Copy).then_inc(s_whi, 1)

                first_steps(act, split, step)
                with act.Fori(0, NC - 1) as c1:
                    steps(act, c1 + 1, step)

            @block.vector
            def _(dve):
                def step(f, u, n, split=None):
                    dve.wait_ge(s_wb[u], n * 32 + 32)
                    dve.wait_ge(s_sg[u], n + 2)
                    nc.vector.tensor_tensor(t1[:, u, :], sg[:, u, :], wb[:, u, :], ALU.mult).then_inc(s_t1[u], 1)
                    dve.wait_ge(s_t1[u], n + 2)
                    dve.wait_ge(s_U[u], n + 1)
                    nc.vector.tensor_tensor(a[:, u, :], U[:, u, :], t1[:, u, :], ALU.mult).then_inc(s_a[u], 1)
                    dve.wait_ge(s_hi[u], n + 1)
                    nc.vector.tensor_tensor(ap[:, u, 1, :], a[:, u, :], ap[:, u, 0, :], ALU.subtract).then_inc(s_lo[u], 1)
                    if split:
                        split(f + READY)

                nc.vector.memset(zero[:, :], 0.0).then_inc(s_zero, 1)
                for u in range(2):
                    dve.sem_inc(s_t1[u], 1)
                    dve.sem_inc(s_a[u], 1)
                dve.sem_inc(s_res, 1)
                dve.sem_inc(s_wlo, READY)

                def split(f):
                    dve.wait_ge(s_whi, f - READY + 1)
                    nc.vector.tensor_tensor(sh.W[:, f, 1, :], load.tile(f), sh.W[:, f, 0, :], ALU.subtract).then_inc(s_wlo, 1)

                def output(c):
                    u = (NF - 1) % 2
                    dve.wait_ge(s_O[u], (c + 1) * uses[u] + 1)
                    xs = sh.X[:, bass.ds(c * (CT // P), CT // P), :]
                    nc.vector.scalar_tensor_tensor(out=xs, in0=O[:, :, :], scalar=gate, in1=xs, op0=ALU.mult,
                                                   op1=ALU.add).then_inc(s_res, 1)

                first_steps(dve, split, step)
                output(0)
                with dve.Fori(0, NC - 1) as c1:
                    steps(dve, c1 + 1, step)
                    output(c1 + 1)

            @block.tensor
            def _(pe):
                def up(c, f, u, n):
                    for X_, s_free, s_done, base in ((G, s_sg, s_G, 0), (U, s_a, s_U, 2 * P)):
                        pe.wait_ge(s_free[u], n + 1)
                        i = 0
                        for wp, xp in PRODUCTS:
                            for k in range(KT):
                                last = nc.tensor.matmul(X_[:, u, :], sh.W[:, f, wp, base + k * P:base + (k + 1) * P],
                                                        sh.hT[:, xp, k, bass.ds(c * CT, CT)], start=i == 0, stop=i == 5)
                                i += 1
                        last.then_inc(s_done[u], 1)

                def down(f, u, n):
                    pe.wait_ge(s_lo[u], n + 1)
                    for t in range(CT // P):
                        for xp, wp in PRODUCTS:
                            last = nc.tensor.matmul(O[:, t, :], ap[:, u, xp, t * P:(t + 1) * P],
                                                    sh.W[:, f, wp, 4 * P:TW], start=False, stop=False,
                                                    skip_group_check=True)
                    last.then_inc(s_O[u], 1)

                pe.sem_inc(s_O[0], 1)
                pe.sem_inc(s_O[1], 1)
                pe.wait_ge(s_zero, 1)

                def chunk(c, weights):
                    up(c, 0, 0, c * uses[0])
                    pe.wait_ge(s_res, c + 1)
                    for bank in range(2):
                        nc.tensor.matmul(O[:, 2 * bank:2 * bank + 2, :], zero[:, 0:P], zero[:, :], start=True, stop=False,
                                         skip_group_check=True)
                    NI = (NF - 1) // 2
                    with pe.Fori(0, NI) as i:
                        weights(i * 2 + 3)
                        up(c, i * 2 + 1, 1, c * uses[1] + i)
                        down(i * 2, 0, c * uses[0] + i)
                        up(c, i * 2 + 2, 0, c * uses[0] + i + 1)
                        down(i * 2 + 1, 1, c * uses[1] + i)
                    weights(NF)
                    if NF % 2 == 0:
                        up(c, NF - 1, 1, c * uses[1] + NI)
                        down(NF - 2, 0, c * uses[0] + NI)
                        down(NF - 1, 1, c * uses[1] + NI)
                    else:
                        down(NF - 1, 0, c * uses[0] + NI)

                chunk(0, lambda n: pe.wait_ge(s_wlo, n))
                with pe.Fori(0, NC - 1) as c1:
                    chunk(c1 + 1, lambda n: None)


class LoadSplit:

    def __init__(self, nc, ctx, items, name):
        self.nc, self.items = nc, items
        self.s_load = [nc.alloc_semaphore(name=f"{name}_load{i}") for i in range(len(items))]
        self.s_hi = nc.alloc_semaphore(name=name + "_hi")
        self.stages = [ctx.enter_context(nc.sbuf_tensor(f"{name}_stage{i}", [P, src.shape[1]], F32)) for i, (_, src) in enumerate(items)]

    def sync(self, sp):
        for s_load, stage, (_, src) in zip(self.s_load, self.stages, self.items):
            sp.dma_start(stage[:, :], src).then_inc(s_load, 16)

    def scalar(self, act):
        for s_load, stage, (dst, _) in zip(self.s_load, self.stages, self.items):
            act.wait_ge(s_load, 16)
            self.nc.scalar.activation(dst[:, 0, :], stage[:, :], ACT.Copy).then_inc(self.s_hi, 1)

    def vector(self, dve):
        for i, (stage, (dst, _)) in enumerate(zip(self.stages, self.items)):
            dve.wait_ge(self.s_hi, i + 1)
            self.nc.vector.tensor_tensor(dst[:, 1, :], stage[:, :], dst[:, 0, :], ALU.subtract)

    def tensor(self, pe):
        pass


def rms_attention(nc, sh, ctxT, weights, gate):
    NH, HD = 32, 8
    SLOT = 32
    GH = P // SLOT
    NG = NH // GH
    HE = HD + 1
    with ExitStack() as ctx:
        def sb(n, shape, dt=F32):
            return ctx.enter_context(nc.sbuf_tensor("rms_" + n, shape, dt))

        def sem(n):
            return nc.alloc_semaphore(name="rms_" + n)

        qk = sb("qk", [P, NB, 2, NH, HD])
        vf = sb("vf", [P, NB, NH, HD])
        vx = sb("vx", [P, NB, NH, 2, HE], F16)
        ss = sb("ss", [P, NB, 2 * NH])
        rs = sb("rs", [P, NB, 2 * NH])
        with ExitStack() as inner:
            cT = inner.enter_context(nc.sbuf_tensor("rms_cT", [P, 2, KT * T], F16))
            wq, wk, wv = (inner.enter_context(nc.sbuf_tensor(f"rms_{x}", [P, 2, KT * D], F16)) for x in ("wq", "wk", "wv"))
            with ExitStack() as head:
                norm = Layernorm(nc, head, sh, "rms_ln")
                items = [(cT, ctxT), (wq, weights["q"]), (wk, weights["k"]), (wv, weights["v"])]
                run(nc, Transposed(nc, head, sh, "rms_hT", norm), LoadSplit(nc, head, items, "rms_load"))
            sq = inner.enter_context(nc.sbuf_tensor("rms_sq", [P, 2, 2 * D], F32))
            QK = inner.enter_context(nc.psum_tensor("rms_QK", [P, 2, 2, D], F32))
            V = inner.enter_context(nc.psum_tensor("rms_V", [P, 2, 512], F32))
            s_mm, s_sq, s_ev, s_v, s_qk = map(sem, ("mm", "sq", "red", "v", "qk"))
            with nc.Block() as block:
                @block.tensor
                def _(pe):
                    with pe.Fori(0, NB // 2) as pair:
                        for par in range(2):
                            t = pair * 2 + par
                            pe.wait_ge(s_v, t + 1)
                            pe.wait_ge(s_qk, t + 1)
                            for out, x, w in ((QK[:, par, 0, :], None, wq), (QK[:, par, 1, :], cT, wk), (V[:, par, 0:D], cT, wv)):
                                i = 0
                                for a, b in PRODUCTS:
                                    for k in range(KT):
                                        lhs = sh.hT[:, a, k, bass.ds(t * P, P)] if x is None else x[:, a, bass.ds(t * P + k * T, P)]
                                        last = nc.tensor.matmul(out, lhs, w[:, b, k * D:(k + 1) * D], start=i == 0, stop=i == 5)
                                        i += 1
                            last.then_inc(s_mm, 1)

                @block.scalar
                def _(act):
                    act.sem_inc(s_v, 2)
                    with act.Fori(0, NB // 2) as pair:
                        for par in range(2):
                            t = pair * 2 + par
                            act.wait_ge(s_qk, t + 3)
                            act.wait_ge(s_ev, t + 1)
                            nc.scalar.activation(sq[:, par, :], qk[:, t, :, :, :].rearrange("p s h d -> p (s h d)"), ACT.Square).then_inc(s_sq, 1)
                            act.wait_ge(s_mm, t + 1)
                            nc.scalar.activation(vf[:, t, :, :], V[:, par, 0:D].rearrange("p (h d) -> p h d", d=HD),
                                                 ACT.Copy).then_inc(s_v, 1)

                @block.vector
                def _(dve):
                    dve.sem_inc(s_ev, 2)
                    dve.sem_inc(s_qk, 2)
                    with dve.Fori(0, NB // 2) as pair:
                        for par in range(2):
                            t = pair * 2 + par
                            dve.wait_ge(s_mm, t + 1)
                            copy_indexed(nc, qk[:, t, :, :, :], QK[:, par, :, :]).then_inc(s_qk, 1)
                            dve.wait_ge(s_sq, t + 1)
                            nc.vector.reduce_sum(ss[:, t, :], sq[:, par, :].rearrange("p (g d) -> p g d", d=HD),
                                                 axis=AXX).then_inc(s_ev, 1)

        s_root, s_rs = sem("root"), sem("rs")
        eps6 = sb("eps6", [P, 1])
        s_eps, s_zero = sem("eps"), sem("zero")
        s_n = sem("n")
        qs = sb("qs", [P, 2, NH, SLOT], F16)
        ks = sb("ks", [P, 2, NH, SLOT], F16)
        qT = sb("qT", [P, 2, NG, P], F16)
        kT = sb("kT", [P, 2, NG, P], F16)
        E = sb("E", [P, 4, 2, NG // 2, P])
        Ep = sb("Ep", [P, 4, 2, 2, NG // 2, P], F16)
        lift = sb("lift", [P, 1])
        osum = sb("osum", [P, NH, HE])
        inv = sb("inv", [P, 2, NH])
        on = sb("on", [P, 2, NH, HD])
        NR = 4
        TQ = ctx.enter_context(nc.psum_tensor("rms_TQ", [P, NG, P], F16))
        TK = ctx.enter_context(nc.psum_tensor("rms_TK", [P, NG, P], F16))
        S = ctx.enter_context(nc.psum_tensor("rms_S", [P, 2, 2, NG // 2, P], F32))
        O = ctx.enter_context(nc.psum_tensor("rms_O", [P, 2, 512], F32))
        s_hi, s_lo, s_TQ, s_TK, s_qT, s_kT, s_S, s_E, s_El, s_vh, s_vl, s_O, s_osum, s_inv, s_on, s_res = map(sem, (
            "hi", "lo", "TQ", "TK", "qT", "kT", "S", "E", "El", "vh", "vl", "O", "osum", "inv", "on", "res"))

        def in_tiles(eng, tile):
            with eng.Fori(0, NB // 2 - 1) as pair:
                for par in range(2):
                    tile(pair * 2 + par, par, 2)
            tile(NB - 2, 0, 1)
            tile(NB - 1, 1, 0)

        with nc.Block() as block:
            @block.gpsimd
            def _(pool):
                nc.gpsimd.memset(lift[:, :], float(np.log(1024.0)))
                nc.gpsimd.memset(eps6[:, :], 1e-6).then_inc(s_eps, 1)
                nc.gpsimd.memset(qs[:, :, :, :], 0.0).then_inc(s_zero, 1)
                nc.gpsimd.memset(ks[:, :, :, :], 0.0).then_inc(s_zero, 1)
                nc.gpsimd.memset(vx[:, :, :, 0, HD:HE], 1.0)
                nc.gpsimd.memset(vx[:, :, :, 1, HD:HE], 0.0)
                pool.wait_ge(s_vh, 1)
                nc.gpsimd.tensor_tensor(vx[:, :, :, 1, 0:HD], vf[:, :, :, :], vx[:, :, :, 0, 0:HD], ALU.subtract).then_inc(s_vl, 1)

            @block.tensor
            def _(pe):
                pe.sem_inc(s_TK, 2)
                pe.sem_inc(s_S, 2 * NR)
                pe.sem_inc(s_O, NR)

                def transposes(t, par):
                    pe.wait_ge(s_lo, t + 1)
                    for side, st, out, read, done in ((0, qs, TQ, s_qT, s_TQ), (1, ks, TK, s_kT, s_TK)):
                        pe.wait_ge(read, t + 1)
                        for g in range(NG):
                            last = nc.tensor.transpose(out[:, g, :], st[:, par, g * GH:(g + 1) * GH, :].rearrange("p h s -> p (h s)"), sh.identh[:, :])
                        last.then_inc(done, 1)

                def scores(t, par, r):
                    if r == 0:
                        pe.wait_ge(s_qT, t + 2)
                        pe.wait_ge(s_kT, t + 2)
                    pe.wait_ge(s_E, t * NR + r + 1)
                    for i in range(NG // 2):
                        for jj in range(2):
                            g, j = r // 2 * (NG // 2) + i, r % 2 * 2 + jj
                            last = nc.tensor.matmul(S[:, r % 2, jj, i, :], kT[j * SLOT:(j + 1) * SLOT, par, g, :],
                                                    qT[j * SLOT:(j + 1) * SLOT, par, g, :], start=True, stop=True,
                                                    skip_group_check=True)
                    last.then_inc(s_S, 1)

                def values(t, par, r):
                    if r == 0:
                        pe.wait_ge(s_osum, t + 1)
                    pe.wait_ge(s_El, t * NR + r + 1)
                    for i in range(NG // 2):
                        for jj in range(2):
                            h = (r // 2 * (NG // 2) + i) * GH + r % 2 * 2 + jj
                            out = O[:, h // 16, h % 16 * 2 * HE:(h % 16 + 1) * 2 * HE]
                            nc.tensor.matmul(out, Ep[:, r, 0, jj, i, :], vx[:, t, h, :, :].rearrange("p a d -> p (a d)"),
                                             start=True, stop=False, skip_group_check=True)
                            last = nc.tensor.matmul(out[:, 0:HE], Ep[:, r, 1, jj, i, :], vx[:, t, h, 0, :],
                                                    start=False, stop=True, skip_group_check=True)
                    last.then_inc(s_O, 1)

                def tile(t, par, ahead):
                    for r in range(NR):
                        if r + 2 < NR:
                            scores(t, par, r + 2)
                        elif ahead >= 1:
                            scores(t + 1, 1 - par, r + 2 - NR)
                        if r == 1 and ahead >= 1:
                            transposes(t + 1, 1 - par)
                        values(t, par, r)

                transposes(0, 0)
                scores(0, 0, 0)
                scores(0, 0, 1)
                pe.wait_ge(s_vl, 1)
                in_tiles(pe, tile)

            @block.scalar
            def _(act):
                act.sem_inc(s_E, 2)
                act.sem_inc(s_qT, 1)
                act.wait_ge(s_eps, 1)
                nc.scalar.activation(rs[:, :, :], ss[:, :, :], ACT.Sqrt, bias=eps6[:, 0:1], scale=1.0 / HD).then_inc(s_root, 1)
                nc.scalar.activation(vx[:, :, :, 0, 0:HD], vf[:, :, :, :], ACT.Copy).then_inc(s_vh, 1)

                def queries(t, par):
                    act.wait_ge(s_TQ, t + 1)
                    act.wait_ge(s_S, t * NR + NR)
                    nc.scalar.activation(qT[:, par, :, :], TQ[:, :, :], ACT.Copy).then_inc(s_qT, 1)

                def exponentials(t, r):
                    act.wait_ge(s_S, t * NR + r + 1 + 2 * NR)
                    act.wait_ge(s_O, t * NR + r + 1)
                    for out in (E[:, r, :, :, :], Ep[:, r, 0, :, :, :]):
                        last = nc.scalar.activation(out, S[:, r % 2, :, :, :], ACT.Exp, bias=lift[:, 0:1], scale=float(HD) ** -0.5)
                    last.then_inc(s_E, 1)

                def tile(t, par, ahead):
                    for r in range(2, NR):
                        exponentials(t, r)
                    if ahead >= 1:
                        queries(t + 1, 1 - par)
                        exponentials(t + 1, 0)
                        exponentials(t + 1, 1)

                queries(0, 0)
                exponentials(0, 0)
                exponentials(0, 1)
                in_tiles(act, tile)

            @block.vector
            def _(dve):
                dve.sem_inc(s_kT, 1)
                dve.sem_inc(s_osum, 1)
                dve.wait_ge(s_root, 1)
                nc.vector.reciprocal(ss[:, 0:2, :], rs[:, 0:2, :]).then_inc(s_rs, 1)
                dve.wait_ge(s_rs, 1)
                dve.wait_ge(s_zero, 2)
                dve.sem_inc(s_n, 1)

                def stacks(t, par):
                    x = qk[:, t, :, :, :].rearrange("p s h d -> p (s h) d")
                    nc.vector.tensor_tensor(x, x, ss[:, t, :].unsqueeze(2).to_broadcast([P, 2 * NH, HD]), ALU.mult).then_inc(s_n, 1)
                    dve.wait_ge(s_n, t + 2)
                    dve.wait_ge(s_TK, t + 1)
                    for side, st, second in ((0, qs, 1), (1, ks, 2)):
                        for slot in (0, second):
                            last = copy_indexed(nc, st[:, par, :, slot * HD:(slot + 1) * HD], qk[:, t, side, :, :])
                    last.then_inc(s_hi, 1)
                    dve.wait_ge(s_hi, t + 1)
                    nc.vector.tensor_tensor(qs[:, par, :, 2 * HD:3 * HD], qk[:, t, 0, :, :], qs[:, par, :, 0:HD], ALU.subtract)
                    nc.vector.tensor_tensor(ks[:, par, :, HD:2 * HD], qk[:, t, 1, :, :], ks[:, par, :, 0:HD], ALU.subtract).then_inc(s_lo, 1)

                def output(t, par):
                    o = O[:, :, 0:16 * 2 * HE].rearrange("p b (h x) -> p b h x", x=2 * HE)
                    dve.wait_ge(s_O, t * NR + 2 * NR)
                    nc.vector.tensor_copy(osum[:, :, :].rearrange("p (b h) d -> p b h d", b=2), o[:, :, :, 0:HE]).then_inc(s_on, 1)
                    dve.wait_ge(s_on, 2 * t + 1)
                    nc.vector.tensor_tensor(osum[:, :, :].rearrange("p (b h) d -> p b h d", b=2), o[:, :, :, HE:2 * HE],
                                            osum[:, :, :].rearrange("p (b h) d -> p b h d", b=2), ALU.add).then_inc(s_osum, 1)
                    dve.wait_ge(s_osum, t + 2)
                    nc.vector.reciprocal(inv[:, par, :], osum[:, :, HD]).then_inc(s_inv, 1)
                    dve.wait_ge(s_inv, t + 1)
                    nc.vector.tensor_tensor(on[:, par, :, :], osum[:, :, 0:HD], inv[:, par, :].unsqueeze(2).to_broadcast([P, NH, HD]),
                                            ALU.mult).then_inc(s_on, 1)
                    dve.wait_ge(s_on, 2 * t + 2)
                    nc.vector.scalar_tensor_tensor(out=sh.X[:, t, :], in0=on[:, par, :, :].rearrange("p h d -> p (h d)"),
                                                   scalar=gate, in1=sh.X[:, t, :], op0=ALU.mult, op1=ALU.add).then_inc(s_res, 1)

                def keys(t, par):
                    dve.wait_ge(s_TK, t + 3)
                    dve.wait_ge(s_S, t * NR + NR)
                    nc.vector.tensor_copy(kT[:, par, :, :], TK[:, :, :]).then_inc(s_kT, 1)

                def low(t, r):
                    dve.wait_ge(s_E, t * NR + r + 3)
                    nc.vector.tensor_tensor(Ep[:, r, 1, :, :, :], E[:, r, :, :, :], Ep[:, r, 0, :, :, :],
                                            ALU.subtract).then_inc(s_El, 1)

                def tile(t, par, ahead):
                    low(t, 2)
                    if ahead >= 1:
                        keys(t + 1, 1 - par)
                    low(t, 3)
                    if ahead == 2:
                        stacks(t + 2, par)
                    if ahead >= 1:
                        low(t + 1, 0)
                    output(t, par)
                    if ahead >= 1:
                        low(t + 1, 1)

                stacks(0, 0)
                stacks(1, 1)
                nc.vector.reciprocal(ss[:, 2:NB, :], rs[:, 2:NB, :]).then_inc(s_rs, 1)
                dve.wait_ge(s_rs, 2)
                keys(0, 0)
                low(0, 0)
                low(0, 1)
                in_tiles(dve, tile)


MAGIC = 1.5 * 2.0 ** 23


class TokensTransposed:

    def __init__(self, nc, ctx, sh, name, ints, ready):
        self.nc, self.sh, self.ints, self.ready = nc, sh, ints, ready
        self.s_T, self.s_read = (nc.alloc_semaphore(name=f"{name}_{n}") for n in ("T", "read"))
        self.TP = ctx.enter_context(nc.psum_tensor(name + "_TP", [P, 2, 4, P], F32))

    def scalar(self, act):
        act.sem_inc(self.s_read, 2)
        with act.Fori(0, NB // 4) as four:
            for i in range(4):
                t = four * 4 + i
                act.wait_ge(self.s_T, t + 1)
                self.nc.scalar.activation(self.sh.hT[:, 0, :, bass.ds(t * P, P)], self.TP[:, i % 2, 0:KT, :], ACT.Copy).then_inc(self.s_read, 1)

    def tensor(self, pe):
        pe.wait_ge(self.ready, 1)
        with pe.Fori(0, NB // 4) as four:
            for i in range(4):
                t = four * 4 + i
                pe.wait_ge(self.s_read, t + 1)
                for k in range(KT):
                    last = self.nc.tensor.matmul(self.TP[:, i % 2, k, :], self.ints[:, t, k * P:(k + 1) * P], self.sh.identh[:, :],
                                                 start=True, stop=True)
                last.then_inc(self.s_T, 1)


def quantised_attention(nc, sh, a, gate):
    NH, HD = 16, 16
    SLOT = 2 * HD
    GH = P // SLOT
    NG = NH // GH
    HALF = T // 2
    KB = HALF // P
    LN255 = float(np.log(255.0))
    with ExitStack() as ctx:
        def sb(n, shape, dt=F32, where=ctx):
            return where.enter_context(nc.sbuf_tensor("qa_" + n, shape, dt))

        def sem(n):
            return nc.alloc_semaphore(name="qa_" + n)

        qT = sb("qT", [P, NG, T], F16)
        kT = sb("kT", [P, NG, T], F16)
        V = sb("V", [P, NB, D], BF16)
        neg_sq = sb("neg_sq", [P, NB, NH])
        sq = sb("sq", [P, NB, NH])
        svb = sb("svb", [P, D])
        bias = sb("bias", [P, 3, D])
        bv = sb("bv", [P, KT])
        wp = sb("wp", [P, 2, KT * D], F16)
        with ExitStack() as inner:
            cT = sb("cT", [P, 2, KT * T], F16, inner)
            wq, wk, wv = (sb(x, [P, 2, KT * D], F16, inner) for x in ("wq", "wk", "wv"))
            with ExitStack() as head:
                norm = Layernorm(nc, head, sh, "qa_ln")
                items = [(cT, a["ctxT"]), (wq, a["qa_wq"]), (wk, a["qa_wk"]), (wv, a["qa_wv"]), (wp, a["qa_wp"])]
                run(nc, Transposed(nc, head, sh, "qa_hT", norm), LoadSplit(nc, head, items, "qa_load"))
            Y = sb("Y", [P, NB, D], F32, inner)
            Z = sb("Z", [P, NB, D], F32, inner)
            stack = sb("stack", [P, NB, NH, SLOT], F16, inner)
            ints = sb("ints", [P, KT, T], BF16, inner)
            amax = sb("amax", [P, NB, NH], F32, inner)
            sv = sb("sv", [P, KT], F32, inner)
            rsv = sb("rsv", [P, KT], F32, inner)
            s_b, s_b4, s_mmk, s_mmq, s_mmv, s_evk, s_evq, s_evv, s_c, s_st, s_st1, s_st2, s_vi, s_Tk, s_Tq, s_Tv, s_tk, s_tq, s_tv, s_sv, s_out, s_in = map(sem, (
                "bias", "b4", "mmk", "mmq", "mmv", "evk", "evq", "evv", "chain", "st", "st1", "st2", "vi", "Tk", "Tq", "Tv", "tk", "tq", "tv", "sv", "svout", "svin"))
            vT = sh.H[:, :, :].rearrange("p t d -> p (t d)").rearrange("p (m n) -> p m n", m=KT)
            zT = Z[:, :, :].rearrange("p t d -> p (t d)").rearrange("p (m n) -> p m n", m=KT)
            sv_dram = nc.dram_tensor("qa_value_scales", [P, KT], F32, kind="Internal").ap()
            QP = inner.enter_context(nc.psum_tensor("qa_QP", [P, 2, 512], F32))
            VP = inner.enter_context(nc.psum_tensor("qa_VP", [P, 2, 512], F32))
            TR = inner.enter_context(nc.psum_tensor("qa_TR", [P, 2, 4, P], F32))
            head_group = lambda g, t: stack[:, t, g * GH:(g + 1) * GH, :].rearrange("p h s -> p (h s)")
            with nc.Block() as block:
                @block.sync
                def _(sp):
                    for i, x in enumerate(("bq", "bk", "bp")):
                        sp.dma_start(bias[:, i, :], a["qa_" + x].partition_broadcast(P)).then_inc(s_b, 16)
                    sp.dma_start(bv[:, :], a["qa_bv"]).then_inc(s_b, 16)
                    sp.wait_ge(s_sv, 1)
                    sp.dma_start(sv_dram, sv[:, :]).then_inc(s_out, 16)
                    sp.wait_ge(s_out, 16)
                    sp.dma_start(svb[:, :], sv_dram.rearrange("p m -> (p m)").partition_broadcast(P)).then_inc(s_in, 16)
                    sp.wait_ge(s_in, 16)

                @block.gpsimd
                def _(pool):
                    pool.wait_ge(s_b4, 2)
                    nc.gpsimd.tensor_tensor(sh.X[:, :, :], sh.X[:, :, :], bias[:, 2, :].unsqueeze(1).to_broadcast([P, NB, D]), ALU.add)

                @block.tensor
                def _(pe):
                    def project(parts, w, s_ev, s_mm):
                        with pe.Fori(0, NB // 4) as four:
                            for i4 in range(4):
                                t, par = four * 4 + i4, i4 % 2
                                pe.wait_ge(s_ev, t + 1)
                                i = 0
                                for wp_, xp in PRODUCTS:
                                    for k in range(KT):
                                        last = nc.tensor.matmul(QP[:, par, 0:D], parts(wp_, k, t), w[:, xp, k * D:(k + 1) * D],
                                                                start=i == 0, stop=i == 5)
                                        i += 1
                                last.then_inc(s_mm, 1)

                    def transposes(groups, source, ident, s_T, s_t):
                        with pe.Fori(0, NB // 4) as four:
                            for i4 in range(4):
                                t, par = four * 4 + i4, i4 % 2
                                pe.wait_ge(s_t, t + 1)
                                for g in range(groups):
                                    last = nc.tensor.matmul(TR[:, par, g, :], source(g, t), ident, start=True, stop=True)
                                last.then_inc(s_T, 1)

                    project(lambda part, k, t: cT[:, part, bass.ds(t * P + k * T, P)], wk, s_evk, s_mmk)
                    for m in range(KT):
                        for c in range(4):
                            n = m * 4 + c
                            if n >= 2:
                                pe.wait_ge(s_evv, n - 1)
                            i = 0
                            for wpart, xpart in PRODUCTS:
                                for k in range(KT):
                                    last = nc.tensor.matmul(VP[:, n % 2, :], wv[:, wpart, k * D + m * P:k * D + (m + 1) * P],
                                                            cT[:, xpart, k * T + c * 512:k * T + (c + 1) * 512],
                                                            start=i == 0, stop=i == 5)
                                    i += 1
                            last.then_inc(s_mmv, 1)
                    pe.wait_ge(s_evk, NB + 2)
                    project(lambda part, k, t: sh.hT[:, part, k, bass.ds(t * P, P)], wq, s_evq, s_mmq)
                    pe.wait_ge(s_st, 1)
                    transposes(NG, head_group, sh.identh[:, :], s_Tk, s_tk)
                    pe.wait_ge(s_vi, 1)
                    pe.wait_ge(s_tk, NB + 2)
                    transposes(KT, lambda m, t: ints[:, m, bass.ds(t * P, P)], sh.ident16[:, :], s_Tv, s_tv)
                    pe.wait_ge(s_st2, 1)
                    pe.wait_ge(s_tv, NB + 2)
                    transposes(NG, head_group, sh.identh[:, :], s_Tq, s_tq)

                @block.scalar
                def _(act):
                    def transposed(groups, target, s_T, s_t):
                        with act.Fori(0, NB // 4) as four:
                            for i4 in range(4):
                                t, par = four * 4 + i4, i4 % 2
                                act.wait_ge(s_T, t + 1)
                                nc.scalar.activation(target(t), TR[:, par, 0:groups, :], ACT.Copy).then_inc(s_t, 1)

                    for s_t in (s_tk, s_tv, s_tq):
                        act.sem_inc(s_t, 2)
                    act.wait_ge(s_b, 64)
                    for m in range(KT):
                        for c in range(4):
                            n = m * 4 + c
                            act.wait_ge(s_mmv, n + 1)
                            nc.scalar.activation(vT[:, m, c * 512:(c + 1) * 512], VP[:, n % 2, :], ACT.Identity,
                                                 bias=bv[:, m:m + 1]).then_inc(s_evv, 1)
                    transposed(NG, lambda t: kT[:, :, bass.ds(t * P, P)], s_Tk, s_tk)
                    transposed(KT, lambda t: V[:, t, :].rearrange("p (m c) -> p m c", m=KT), s_Tv, s_tv)
                    act.wait_ge(s_st1, 1)
                    nc.scalar.activation(stack[:, :, :, HD:SLOT].rearrange("p t h s -> p (t h) s"),
                                         stack[:, :, :, 0:HD].rearrange("p t h s -> p (t h) s"), ACT.Copy).then_inc(s_st2, 1)
                    transposed(NG, lambda t: qT[:, :, bass.ds(t * P, P)], s_Tq, s_tq)

                @block.vector
                def _(dve):
                    chained = chain_on(dve, s_c)
                    wide = [P, NB * NH, HD]
                    y = Y[:, :, :].rearrange("p t (h d) -> p (t h) d", d=HD)
                    z = Z[:, :, :].rearrange("p t (h d) -> p (t h) d", d=HD)
                    st = stack[:, :, :, :].rearrange("p t h s -> p (t h) s")
                    inv = neg_sq[:, :, :].rearrange("p t h -> p (t h)")

                    def evacuate(s_mm, s_ev, out):
                        with dve.Fori(0, NB // 4) as four:
                            for i4 in range(4):
                                t, par = four * 4 + i4, i4 % 2
                                dve.wait_ge(s_mm, t + 1)
                                out(t, QP[:, par, 0:D]).then_inc(s_ev, 1)
                        dve.wait_ge(s_ev, NB + 2)

                    def integers(scale):
                        flat = scale[:, :, :].rearrange("p t h -> p (t h)")
                        chained(nc.vector.tensor_reduce(out=flat, in_=y, axis=AXX, op=ALU.max, apply_absolute_value=True))
                        chained(nc.vector.tensor_scalar(flat, flat, 1.0 / 127.0, 1e-8, ALU.mult, ALU.max))
                        chained(nc.vector.reciprocal(inv, flat))
                        chained(nc.vector.tensor_tensor(z, y, inv.unsqueeze(2).to_broadcast(wide), ALU.mult))
                        chained(nc.vector.tensor_scalar(Z[:, :, :], Z[:, :, :], MAGIC, MAGIC, ALU.add, ALU.subtract))
                        return flat

                    dve.sem_inc(s_evk, 2)
                    dve.sem_inc(s_evq, 2)
                    dve.wait_ge(s_b, 64)
                    nc.vector.tensor_scalar_mul(bias[:, 0, :], bias[:, 0, :], float(HD) ** -0.5).then_inc(s_b4, 1)
                    nc.vector.tensor_scalar(bias[:, 2, :], bias[:, 2, :], gate, None, ALU.mult).then_inc(s_b4, 1)
                    dve.wait_ge(s_b4, 1)
                    evacuate(s_mmk, s_evk, lambda t, psum: nc.vector.tensor_tensor(Y[:, t, :], psum, bias[:, 1, :], ALU.add))
                    flat = integers(amax)
                    chained(nc.vector.tensor_scalar(Z[:, :, :], Z[:, :, :], 127.0, -127.0, ALU.min, ALU.max))
                    chained(nc.vector.tensor_tensor(y, z, flat.unsqueeze(2).to_broadcast(wide), ALU.mult))
                    chained(nc.vector.tensor_copy(st[:, :, 0:HD], y))
                    nc.vector.tensor_tensor(st[:, :, HD:SLOT], y, st[:, :, 0:HD], ALU.subtract).then_inc(s_st, 1)
                    dve.wait_ge(s_st, 1)
                    evacuate(s_mmq, s_evq, lambda t, psum: nc.vector.scalar_tensor_tensor(
                        out=Y[:, t, :], in0=psum, scalar=float(HD) ** -0.5, in1=bias[:, 0, :], op0=ALU.mult, op1=ALU.add))
                    dve.wait_ge(s_evv, 4 * KT)
                    chained(nc.vector.tensor_reduce(out=sv[:, :], in_=vT, axis=AXX, op=ALU.max, apply_absolute_value=True))
                    nc.vector.tensor_scalar(sv[:, :], sv[:, :], 1.0 / 127.0, 1e-8, ALU.mult, ALU.max).then_inc(s_sv, 1)
                    dve.wait_ge(s_sv, 1)
                    chained(nc.vector.reciprocal(rsv[:, :], sv[:, :]))
                    for m in range(KT):
                        last = nc.vector.tensor_scalar(zT[:, m, :], vT[:, m, :], rsv[:, m:m + 1], MAGIC, ALU.mult, ALU.add)
                    chained(last)
                    chained(nc.vector.tensor_scalar(zT, zT, MAGIC, 127.0, ALU.subtract, ALU.min))
                    nc.vector.tensor_scalar(ints[:, :, :], zT, -127.0, None, ALU.max).then_inc(s_vi, 1)
                    dve.wait_ge(s_vi, 1)
                    integers(sq)
                    dve.wait_ge(s_Tk, NB)
                    nc.vector.tensor_scalar(st[:, :, 0:HD], z, 127.0, -127.0, ALU.min, ALU.max).then_inc(s_st1, 1)
                    nc.vector.tensor_scalar_mul(neg_sq[:, :, :], sq[:, :, :], -1.0)

        qb = sb("qb", [P, 2, GH, NG // 2, P], F16)
        mx = sb("mx", [P, 2, 3])
        mm = sb("mm", [P, 2])
        nb = sb("nb", [P, 2])
        ln255 = sb("ln255", [P, 1])
        sums = sb("sums", [P, NB * NH, 2])
        e16 = sb("e16", [P, 2, 2, HALF], mybir.dt.uint16)
        pb = sb("pb", [P, 4, 2, KB, P], BF16)
        pT = sb("pT", [P, 2, 2, KB, P], BF16)
        s_qz, s_q, s_Sa, s_Sb, s_Ea, s_Eb, s_mx, s_mm2, s_nb, s_cast, s_Ta, s_Tb, s_eva, s_evb, s_V, s_o = map(sem, (
            "qz", "q", "Sa", "Sb", "Ea", "Eb", "mx", "mm2", "nb", "cast", "Ta", "Tb", "eva", "evb", "V", "o"))
        with ExitStack() as pctx:
            Sa = pctx.enter_context(nc.psum_tensor("qa_Sa", [P, 2, HALF], F32))
            Sb = pctx.enter_context(nc.psum_tensor("qa_Sb", [P, HALF], F32))
            TP = pctx.enter_context(nc.psum_tensor("qa_TP", [P, KB, P], BF16))
            O = pctx.enter_context(nc.psum_tensor("qa_O", [P, NH * HD], F32))
            LAG = 5

            def skewed(eng, step):
                units = NB * NH
                for i in range(LAG):
                    step(i, lambda lag, i=i: 0 if i >= lag else None)
                with eng.Fori(0, NB - 1) as t:
                    for i in range(LAG, LAG + NH):
                        step(i % NH, lambda lag, i=i, t=t: t + 1 if i - lag >= NH else t)
                for i in range(LAG + (NB - 1) * NH, units + LAG):
                    step(i % NH, lambda lag, i=i: (i - lag) // NH if i - lag < units else None)

            with nc.Block() as block:
                @block.gpsimd
                def _(pool):
                    nc.gpsimd.memset(ln255[:, :], LN255).then_inc(s_qz, 1)
                    nc.gpsimd.memset(qb[:, :, :, :, :], 0.0).then_inc(s_qz, 1)
                    pool.wait_ge(s_qz, 2)
                    with pool.Fori(0, NB) as t:
                        for half in range(2):
                            pool.wait_ge(s_Sb, 2 * t * NH + (half + 1) * NH)
                            for j in range(GH):
                                rows = slice(j * SLOT, (j + 1) * SLOT)
                                last = nc.gpsimd.tensor_copy(qb[rows, half, j, :, :], qT[rows, half * 2:half * 2 + 2, bass.ds(t * P, P)])
                            last.then_inc(s_q, 1)

                @block.tensor
                def _(pe):
                    pe.sem_inc(s_Sb, 2 * NH)

                    def scores(h, out, first, done):
                        g, j = h // GH, h % GH
                        for c in range(0, HALF, 512):
                            last = nc.tensor.matmul(out[:, c:c + 512], qb[:, g // 2, j, g % 2, :],
                                                    kT[:, g, first + c:first + c + 512], start=True, stop=True)
                            if first or c + 512 == HALF:
                                last.then_inc(done, 1)

                    def transposes(h, half):
                        for b in range(KB):
                            last = nc.tensor.transpose(TP[:, b, :], pb[:, h % 4, half, b, :], sh.ident16[:, :])
                        return last

                    def step(i, tile):
                        if (t := tile(1)) is not None:
                            h = (i - 1) % NH
                            pe.wait_ge(s_Eb, t * NH + h + 1)
                            scores(h, Sb, HALF, s_Sb)
                        if (t := tile(4)) is not None:
                            h = (i - 4) % NH
                            pe.wait_ge(s_cast, t * NH + h + 3)
                            pe.wait_ge(s_evb, t * NH + h + 1)
                            transposes(h, 0).then_inc(s_Ta, 1)
                        if (t := tile(0)) is not None:
                            h = i
                            if h % 8 == 0:
                                pe.wait_ge(s_q, 2 * t + 1 + h // 8)
                            pe.wait_ge(s_Ea, t * NH + h + 1)
                            scores(h, Sa[:, h % 2, :], 0, s_Sa)
                        if (t := tile(5)) is not None:
                            h = (i - 5) % NH
                            pe.wait_ge(s_eva, t * NH + h + 1)
                            pe.wait_ge(s_evb, t * NH + h + 2)
                            if h == 0:
                                pe.wait_ge(s_o, t + 1)
                            for b in range(2 * KB):
                                last = nc.tensor.matmul(O[:, h * HD:(h + 1) * HD], pT[:, h % 2, b // KB, b % KB, :],
                                                        V[:, b, h * HD:(h + 1) * HD], start=b == 0, stop=b == 2 * KB - 1)
                            last.then_inc(s_V, 1)
                        if (t := tile(4)) is not None:
                            h = (i - 4) % NH
                            pe.wait_ge(s_eva, t * NH + h + 1)
                            transposes(h, 1).then_inc(s_Tb, 1)

                    pe.sem_inc(s_V, 2)
                    pe.sem_inc(s_Tb, 4)
                    skewed(pe, step)

                @block.scalar
                def _(act):
                    act.sem_inc(s_Ea, 2)
                    act.sem_inc(s_Eb, 1)
                    act.wait_ge(s_qz, 2)

                    def exponential(t, h, half, scores):
                        return nc.scalar.activation(e16[:, h % 2, half, :], scores, ACT.Exp, bias=nb[:, h % 2:h % 2 + 1],
                                                    scale=sq[:, t, h:h + 1], accum_out=sums[:, t * NH + h, half:half + 1])

                    def step(i, tile):
                        if (t := tile(1)) is not None:
                            h = (i - 1) % NH
                            act.wait_ge(s_mm2, t * NH + h + 1)
                            nc.scalar.activation(nb[:, h % 2:h % 2 + 1], mm[:, h % 2:h % 2 + 1], ACT.Identity, bias=ln255[:, 0:1],
                                                 scale=neg_sq[:, t, h:h + 1]).then_inc(s_nb, 1)
                            act.wait_ge(s_nb, t * NH + h + 1)
                            act.wait_ge(s_cast, t * NH + h + 1)
                            exponential(t, h, 1, Sb[:, :]).then_inc(s_Eb, 1)
                            exponential(t, h, 0, Sa[:, h % 2, :]).then_inc(s_Ea, 1)
                        if (t := tile(3)) is not None:
                            h = (i - 3) % NH
                            act.wait_ge(s_Ta, t * NH + h + 1)
                            act.wait_ge(s_V, t * NH + h + 1)
                            nc.scalar.activation(pT[:, h % 2, 0, :, :], TP[:, :, :], ACT.Copy).then_inc(s_eva, 1)

                    skewed(act, step)

                @block.vector
                def _(dve):
                    dve.sem_inc(s_cast, 2)
                    dve.sem_inc(s_evb, 1)
                    dve.sem_inc(s_o, 1)

                    def step(i, tile):
                        if (t := tile(1)) is not None:
                            h = (i - 1) % NH
                            u = t * NH + h
                            for q in range(2):
                                dve.wait_ge(s_Sb, 2 * u + q + 1 + 2 * NH)
                                nc.vector.reduce_max(mx[:, h % 2, q + 1:q + 2], Sb[:, q * 512:(q + 1) * 512], axis=AXX).then_inc(s_mx, 1)
                            dve.wait_ge(s_mx, 3 * u + 3)
                            nc.vector.tensor_scalar(mm[:, h % 2:h % 2 + 1], mx[:, h % 2, 0:1], mx[:, h % 2, 1:2], mx[:, h % 2, 2:3],
                                                    ALU.max, ALU.max).then_inc(s_mm2, 1)
                        if (t := tile(0)) is not None:
                            h = i
                            dve.wait_ge(s_Sa, t * NH + h + 1)
                            nc.vector.reduce_max(mx[:, h % 2, 0:1], Sa[:, h % 2, :], axis=AXX).then_inc(s_mx, 1)
                        if (t := tile(4)) is not None:
                            h = (i - 4) % NH
                            dve.wait_ge(s_Tb, t * NH + h + 5)
                            dve.wait_ge(s_V, t * NH + h + 1)
                            nc.vector.tensor_copy(pT[:, h % 2, 1, :, :], TP[:, :, :]).then_inc(s_evb, 1)
                        if (t := tile(2)) is not None:
                            h = (i - 2) % NH
                            dve.wait_ge(s_Ea, t * NH + h + 3)
                            dve.wait_ge(s_Tb, t * NH + h + 1)
                            nc.vector.tensor_copy(pb[:, h % 4, :, :, :], e16[:, h % 2, :, :]).then_inc(s_cast, 1)
                        if (i - 5) % NH == NH - 1 and (t := tile(5)) is not None:
                            dve.wait_ge(s_V, t * NH + NH + 2)
                            copy_indexed(nc, sh.H[:, t, :], O[:, :]).then_inc(s_o, 1)

                    skewed(dve, step)

        with ExitStack() as tail:
            scaled = ScaledOutputs(nc, tail, sh, sums, svb, NH)
            transposed = Transposed(nc, tail, sh, "qa_oT", scaled)
            run(nc, transposed, OutProjection(nc, tail, sh, transposed, wp, gate))


class ScaledOutputs:

    def __init__(self, nc, ctx, sh, sums, value_scales, heads):
        self.nc, self.sh, self.sums, self.value_scales, self.heads = nc, sh, sums, value_scales, heads
        self.s_sum, self.s_inv, self.s_norm = (nc.alloc_semaphore(name=f"qa_scaled_{x}") for x in ("sum", "inv", "norm"))
        self.s_head = nc.alloc_semaphore(name="qa_scaled_head")
        self.inv = ctx.enter_context(nc.sbuf_tensor("qa_inv", [P, NB, heads], F32))
        self.tot = ctx.enter_context(nc.sbuf_tensor("qa_tot", [P, NB * heads], F32))

    def statistics(self, dve):
        nc = self.nc
        nc.vector.tensor_tensor(self.tot[:, :], self.sums[:, :, 0], self.sums[:, :, 1], ALU.add).then_inc(self.s_sum, 1)
        dve.wait_ge(self.s_sum, 1)
        nc.vector.reciprocal(self.inv[:, :, :].rearrange("p t h -> p (t h)"), self.tot[:, :]).then_inc(self.s_inv, 1)
        dve.wait_ge(self.s_inv, 1)

    def pair(self, dve, p):
        nc, sh = self.nc, self.sh
        for t in (p * 2, p * 2 + 1):
            h = sh.H[:, t, :].rearrange("p (h d) -> p h d", h=self.heads)
            nc.vector.tensor_tensor(h, h, self.inv[:, t, :].unsqueeze(2).to_broadcast([P, self.heads, D // self.heads]),
                                    ALU.mult).then_inc(self.s_head, 1)
        for i in range(2):
            t = p * 2 + i
            dve.wait_ge(self.s_head, t + 1)
            h = sh.H[:, t, :].rearrange("q (m p) -> q m p", m=KT)
            nc.vector.tensor_tensor(h, h, self.value_scales[:, :].rearrange("q (p m) -> q m p", m=KT), ALU.mult).then_inc(self.s_norm, 1)

    def scalar(self, act):
        pass


class OutProjection:

    def __init__(self, nc, ctx, sh, transposed, w, gate):
        self.nc, self.sh, self.transposed, self.w, self.gate = nc, sh, transposed, w, gate
        self.s_mm, self.s_ev = (nc.alloc_semaphore(name=f"qa_out_{x}") for x in ("mm", "ev"))
        self.Q = ctx.enter_context(nc.psum_tensor("qa_out", [P, 2, 512], F32))

    def sync(self, sp):
        pass

    def scalar(self, act):
        pass

    def vector(self, dve):
        nc, sh = self.nc, self.sh
        dve.sem_inc(self.s_ev, 2)
        with dve.Fori(0, NB // 4) as four:
            for i in range(4):
                t = four * 4 + i
                dve.wait_ge(self.s_mm, t + 1)
                nc.vector.scalar_tensor_tensor(out=sh.X[:, t, :], in0=self.Q[:, i % 2, 0:D], scalar=self.gate, in1=sh.X[:, t, :],
                                               op0=ALU.mult, op1=ALU.add).then_inc(self.s_ev, 1)

    def tensor(self, pe):
        nc = self.nc
        self.transposed.whole(pe)
        with pe.Fori(0, NB // 4) as four:
            for j in range(4):
                t = four * 4 + j
                pe.wait_ge(self.s_ev, t + 1)
                i = 0
                for a, b in PRODUCTS:
                    for k in range(KT):
                        last = nc.tensor.matmul(self.Q[:, j % 2, 0:D], self.sh.hT[:, a, k, bass.ds(t * P, P)],
                                                self.w[:, b, k * D:(k + 1) * D], start=i == 0, stop=i == 5)
                        i += 1
                last.then_inc(self.s_mm, 1)


def chain_on(eng, s, start=0):
    done = [start]

    def chained(ins):
        done[0] += 1
        ins.then_inc(s, 1)
        eng.wait_ge(s, done[0])
    return chained


def quantised_ffn(nc, sh, a, gate):
    F = 1024
    NF = F // P
    CT = 512
    with ExitStack() as ctx:
        def sb(n, shape, dt=F32, where=ctx):
            return where.enter_context(nc.sbuf_tensor("qf_" + n, shape, dt))

        def sem(n):
            return nc.alloc_semaphore(name="qf_" + n)

        w1 = sb("w1", [P, KT * F], F16)
        w2 = sb("w2", [P, NF * D], F16)
        b1 = sb("b1", [P, NF])
        b2 = sb("b2", [P, D])
        sa = sb("sa", [P, 2])
        rsa = sb("rsa", [P, 2])
        sw = sb("sw", [P, 2])
        rsw = sb("rsw", [P, 2])
        c = sb("c", [P, 8])
        ints = sb("ints", [P, NB, D], F16)
        with ExitStack() as inner:
            f1 = sb("f1", [P, KT * F], F32, inner)
            f2 = sb("f2", [P, NF * D], F32, inner)
            Z = sb("Z", [P, NB * D], F32, inner)
            am = sb("am", [P, 2], F32, inner)
            amx = sb("amx", [P, 2], F32, inner)
            s_load, s_am, s_amx, s_c, s_b2 = map(sem, ("load", "am", "amx", "chain", "b2"))
            norm = Layernorm(nc, inner, sh, "qf_ln")
            s_ints = sem("ints")
            turned = TokensTransposed(nc, inner, sh, "qf_T", ints, s_ints)
            with nc.Block() as block:
                @block.tensor
                def _(pe):
                    turned.tensor(pe)

                @block.sync
                def _(sp):
                    sp.dma_start(f1[:, :], a["qf_w1"]).then_inc(s_load, 16)
                    sp.dma_start(f2[:, :], a["qf_w2"]).then_inc(s_load, 16)
                    sp.dma_start(b1[:, :], a["qf_b1"]).then_inc(s_load, 16)
                    sp.dma_start(b2[:, :], a["qf_b2"].partition_broadcast(P)).then_inc(s_load, 16)
                    sp.dma_start(sa[:, 0:1], a["qf_s1"].partition_broadcast(P)).then_inc(s_load, 16)
                    sp.dma_start(sa[:, 1:2], a["qf_s2"].partition_broadcast(P)).then_inc(s_load, 16)

                @block.gpsimd
                def _(pool):
                    pool.wait_ge(s_am, 2)
                    nc.gpsimd.partition_all_reduce(amx[:, :], am[:, :], P, bass.bass_isa.ReduceOp.max).then_inc(s_amx, 1)
                    pool.wait_ge(s_b2, 1)
                    nc.gpsimd.tensor_tensor(sh.X[:, :, :], sh.X[:, :, :], b2[:, :].unsqueeze(1).to_broadcast([P, NB, D]), ALU.add)

                @block.scalar
                def _(act):
                    norm.scalar(act)
                    turned.scalar(act)

                @block.vector
                def _(dve):
                    chained = chain_on(dve, s_c)
                    norm.vector(dve)
                    norm.whole(dve)
                    dve.wait_ge(s_load, 96)
                    for i, f in enumerate((f1, f2)):
                        nc.vector.tensor_reduce(out=am[:, i:i + 1], in_=f[:, :], axis=AXX, op=ALU.max,
                                                apply_absolute_value=True).then_inc(s_am, 1)
                    chained(nc.vector.reciprocal(rsa[:, :], sa[:, :]))
                    hf = sh.H[:, :, :].rearrange("p t d -> p (t d)")
                    chained(nc.vector.tensor_scalar(Z[:, :], hf, rsa[:, 0:1], MAGIC, ALU.mult, ALU.add))
                    chained(nc.vector.tensor_scalar(Z[:, :], Z[:, :], MAGIC, 7.0, ALU.subtract, ALU.min))
                    nc.vector.tensor_scalar(ints[:, :, :].rearrange("p t d -> p (t d)"), Z[:, :], -8.0, None, ALU.max).then_inc(s_ints, 1)
                    dve.wait_ge(s_amx, 1)
                    chained(nc.vector.tensor_scalar(sw[:, :], amx[:, :], 1.0 / 7.0, None, ALU.mult))
                    chained(nc.vector.reciprocal(rsw[:, :], sw[:, :]))
                    chained(nc.vector.tensor_tensor(c[:, 0:2], sa[:, :], sw[:, :], ALU.mult))
                    chained(nc.vector.reciprocal(c[:, 2:4], c[:, 0:2]))
                    chained(nc.vector.tensor_tensor(c[:, 4:5], c[:, 0:1], rsa[:, 1:2], ALU.mult))
                    chained(nc.vector.tensor_tensor(c[:, 5:6], c[:, 1:2], gate, ALU.mult))
                    for i, b in enumerate((b1, b2)):
                        chained(nc.vector.tensor_scalar(b[:, :], b[:, :], c[:, 2 + i:3 + i], MAGIC, ALU.mult, ALU.add))
                        chained(nc.vector.tensor_scalar(b[:, :], b[:, :], MAGIC, 2.0 ** 31 - 1, ALU.subtract, ALU.min))
                        chained(nc.vector.tensor_scalar(b[:, :], b[:, :], -2.0 ** 31, c[:, i:i + 1], ALU.max, ALU.mult))
                    nc.vector.tensor_scalar(b1[:, :], b1[:, :], rsa[:, 1:2], None, ALU.mult)
                    nc.vector.tensor_scalar(b2[:, :], b2[:, :], gate, None, ALU.mult).then_inc(s_b2, 1)
                    for i, (f, w) in enumerate(((f1, w1), (f2, w2))):
                        chained(nc.vector.tensor_scalar(f[:, :], f[:, :], rsw[:, i:i + 1], MAGIC, ALU.mult, ALU.add))
                        chained(nc.vector.tensor_scalar(f[:, :], f[:, :], MAGIC, 7.0, ALU.subtract, ALU.min))
                        nc.vector.tensor_scalar(w[:, :], f[:, :], -8.0, None, ALU.max)

        r = sb("r", [P, 2, CT])
        z = sb("z", [P, 2, CT])
        hq = sb("hq", [P, 2, NF, CT], F16)
        NT = CT // P
        Hp = ctx.enter_context(nc.psum_tensor("qf_H", [P, 2, CT], F32))
        O = ctx.enter_context(nc.psum_tensor("qf_O", [P, 2, 2, D], F32))
        s_H, s_r, s_z, s_hq, s_O, s_res = map(sem, ("H", "r", "z", "hq", "O", "res"))
        with nc.Block() as block:
            @block.tensor
            def _(pe):
                def hidden(ch, f):
                    n = ch * NF + f
                    pe.wait_ge(s_r, n + 1)
                    for k in range(KT):
                        last = nc.tensor.matmul(Hp[:, f % 2, :], w1[:, k * F + f * P:k * F + (f + 1) * P],
                                                sh.hT[:, 0, k, bass.ds(ch * CT, CT)], start=k == 0, stop=k == KT - 1)
                    last.then_inc(s_H, 1)

                pe.sem_inc(s_O, 4)
                with pe.Fori(0, T // CT // 2) as pair:
                    for par in range(2):
                        ch = pair * 2 + par
                        for f in range(NF):
                            hidden(ch, f)
                        pe.wait_ge(s_hq, ch * NF + NF)
                        for bank in range(2):
                            pe.wait_ge(s_res, 2 * ch + bank + 1)
                            for i in range(2):
                                t = bank * 2 + i
                                for f in range(NF):
                                    last = nc.tensor.matmul(O[:, bank, i, :], hq[:, par, f, t * P:(t + 1) * P], w2[:, f * D:(f + 1) * D],
                                                            start=f == 0, stop=f == NF - 1)
                            last.then_inc(s_O, 1)

            @block.scalar
            def _(act):
                act.sem_inc(s_r, 2)
                with act.Fori(0, T // CT // 2) as pair:
                    for par in range(2):
                        ch = pair * 2 + par
                        for f in range(NF):
                            n = ch * NF + f
                            act.wait_ge(s_H, n + 1)
                            act.wait_ge(s_z, n + 1)
                            nc.scalar.activation(r[:, f % 2, :], Hp[:, f % 2, :], ACT.Relu, bias=b1[:, f:f + 1], scale=c[:, 4:5]).then_inc(s_r, 1)

            @block.vector
            def _(dve):
                dve.sem_inc(s_z, 2)
                dve.sem_inc(s_res, 2)

                def outputs(ch):
                    for bank in range(2):
                        dve.wait_ge(s_O, 2 * ch + bank + 5)
                        xs = sh.X[:, bass.ds(ch * NT + bank * 2, 2), :]
                        nc.vector.scalar_tensor_tensor(out=xs, in0=O[:, bank, :, :], scalar=c[:, 5:6], in1=xs, op0=ALU.mult,
                                                       op1=ALU.add).then_inc(s_res, 1)

                with dve.Fori(0, T // CT // 2) as pair:
                    for par in range(2):
                        ch = pair * 2 + par
                        dve.wait_ge(s_O, 2 * ch + 2)
                        for f in range(NF):
                            n = ch * NF + f
                            dve.wait_ge(s_r, n + 3)
                            nc.vector.tensor_scalar(z[:, f % 2, :], r[:, f % 2, :], 15.0, MAGIC, ALU.min, ALU.add).then_inc(s_z, 1)
                            dve.wait_ge(s_z, n + 3)
                            nc.vector.tensor_scalar(hq[:, par, f, :], z[:, f % 2, :], MAGIC, None, ALU.subtract).then_inc(s_hq, 1)
                        outputs(ch)


def causal_attention(nc, sh, a, gate):
    NH, HD = 16, 16
    SLOT = 64
    NG = NH // 2
    HE = HD + 1
    SCALE = float(HD) ** -0.5
    LIFT = float(np.log(4096.0))
    with ExitStack() as ctx:
        def sb(n, shape, dt=F32):
            return ctx.enter_context(nc.sbuf_tensor("ca_" + n, shape, dt))

        def sem(n):
            return nc.alloc_semaphore(name="ca_" + n)

        cx = sb("cx", [P, NB, D])
        vx = sb("vx", [P, 2, NB, NH, HE], F16)
        lift = sb("lift", [P, 1])
        mask = sb("mask", [P, 4, P], BF16)
        maskf = sb("maskf", [P, 4, P])
        qs = sb("qs", [P, 2, NH, SLOT], F16)
        ks = sb("ks", [P, 2, NH, SLOT], F16)
        qT = sb("qT", [P, 2, NG, P], F16)
        kT = sb("kT", [P, 2, NG, P], F16)
        kc = sb("kc", [P, 2, NH, HD])
        m = sb("m", [P, 2, 2, 4])
        d = sb("d", [P, 2, 2, 4, P])
        E = sb("E", [P, 2, 8, P])
        eT = sb("eT", [P, 2, 2, 8, P], F16)
        inv = sb("inv", [P, NH])
        on = sb("on", [P, NH, HD])
        S = ctx.enter_context(nc.psum_tensor("ca_S", [P, 2, 2, 4, P], F32))
        TQ = ctx.enter_context(nc.psum_tensor("ca_TQ", [P, NG, P], F16))
        ET = ctx.enter_context(nc.psum_tensor("ca_ET", [P, 8, P], F32))
        O = ctx.enter_context(nc.psum_tensor("ca_O", [P, 512], F32))
        s_load, s_set, s_set1, s_mask, s_vx, s_qlo, s_klo, s_hi, s_khi, s_T, s_tr, s_S, s_m, s_d, s_E, s_ET, s_eh, s_el, s_V, s_inv, s_on, s_res = map(sem, (
            "load", "set", "set1", "mask", "vx", "qlo", "klo", "hi", "khi", "T", "tr", "S", "m", "d", "E", "ET", "eh", "el", "V", "inv", "on", "res"))
        norm = Layernorm(nc, ctx, sh, "ca_ln")
        def in_tiles(eng, tile):
            with eng.Fori(0, NB // 2 - 1) as pair:
                for par in range(2):
                    tile(pair * 2 + par, par, 2)
            tile(NB - 2, 0, 1)
            tile(NB - 1, 1, 0)

        with nc.Block() as block:
            @block.sync
            def _(sp):
                sp.dma_start(cx[:, :, :], a["ctx"].rearrange("b p d -> p b d")).then_inc(s_load, 16)

            @block.gpsimd
            def _(pool):
                nc.gpsimd.memset(maskf[:, :, :], 0.0).then_inc(s_set, 1)
                nc.gpsimd.memset(ks[:, :, :, :], 0.0).then_inc(s_set, 1)
                nc.gpsimd.memset(qs[:, :, :, :], 0.0).then_inc(s_set, 1)
                pool.wait_ge(s_set, 3)
                nc.gpsimd.affine_select(out=maskf[:, :, :], in_=maskf[:, :, :], compare_op=ALU.is_ge, fill=LOW,
                                        base=0, pattern=[[0, 4], [-1, P]], channel_multiplier=1).then_inc(s_mask, 1)
                pool.wait_ge(s_load, 16)
                with pool.Fori(0, NB // 2) as pair:
                    for par in range(2):
                        t = pair * 2 + par
                        k = cx[:, t, :].rearrange("p (h d) -> p h d", d=HD)
                        pool.wait_ge(s_T, 2 * t + 2)
                        for slot in (0, 2):
                            last = nc.gpsimd.tensor_copy(ks[:, par, :, slot * HD:(slot + 1) * HD], k)
                        last.then_inc(s_khi, 1)
                        nc.gpsimd.tensor_copy(kc[:, par, :, :], k).then_inc(s_khi, 1)
                        pool.wait_ge(s_khi, 2 * t + 2)
                        nc.gpsimd.tensor_tensor(ks[:, par, :, HD:2 * HD], kc[:, par, :, :], ks[:, par, :, 0:HD], ALU.subtract).then_inc(s_klo, 1)

            @block.tensor
            def _(pe):
                pe.sem_inc(s_T, 4)
                pe.sem_inc(s_S, 4)
                pe.sem_inc(s_ET, 2)
                pe.sem_inc(s_V, 2)
                pe.wait_ge(s_vx, 2)
                pe.wait_ge(s_set1, 2)

                def scores(t, par, r):
                    n = t * 2 + r
                    pe.wait_ge(s_d, n + 1)
                    for j in range(2):
                        nc.tensor.matmul(S[:, r, j, :, :], sh.ident16[:, :], mask[:, :, :], start=True, stop=False, skip_group_check=True)
                    for i in range(4):
                        for j in range(2):
                            rows = slice(j * SLOT, (j + 1) * SLOT)
                            last = nc.tensor.matmul(S[:, r, j, i, :], qT[rows, par, r * 4 + i, :], kT[rows, par, r * 4 + i, :],
                                                    start=False, stop=True, skip_group_check=True)
                    last.then_inc(s_S, 1)

                def transposes(t, par, side):
                    stack, ready = ((qs, s_qlo), (ks, s_klo))[side]
                    pe.wait_ge(ready, t + 1)
                    pe.wait_ge(s_tr, 2 * t + side + 1)
                    for g in range(NG):
                        last = nc.tensor.transpose(TQ[:, g, :], stack[:, par, 2 * g:2 * g + 2, :].rearrange("p h s -> p (h s)"), sh.identh[:, :])
                    last.then_inc(s_T, 1)

                def exponentials(t, r):
                    n = t * 2 + r
                    pe.wait_ge(s_E, n + 3)
                    pe.wait_ge(s_el, n + 1)
                    for i in range(8):
                        last = nc.tensor.transpose(ET[:, i, :], E[:, r, i, :], sh.ident[:, :])
                    last.then_inc(s_ET, 1)

                def values(t, r):
                    pe.wait_ge(s_el, t * 2 + r + 2)
                    if r == 0:
                        pe.wait_ge(s_res, t + 1)
                    for i in range(8):
                        h = (r * 4 + i % 4) * 2 + i // 4
                        for n, (e, v) in enumerate(PRODUCTS):
                            last = nc.tensor.matmul(O[:, h * HE:(h + 1) * HE], eT[:, r, e, i, :], vx[:, v, t, h, :],
                                                    start=n == 0, stop=n == 2, skip_group_check=True)
                    last.then_inc(s_V, 1)

                def tile(t, par, ahead):
                    exponentials(t, 0)
                    if ahead >= 1:
                        pe.wait_ge(s_tr, 2 * t + 5)
                        scores(t + 1, 1 - par, 0)
                        scores(t + 1, 1 - par, 1)
                    exponentials(t, 1)
                    values(t, 0)
                    if ahead == 2:
                        transposes(t + 2, par, 0)
                    values(t, 1)
                    if ahead == 2:
                        transposes(t + 2, par, 1)

                for side in range(2):
                    transposes(0, 0, side)
                pe.wait_ge(s_tr, 3)
                for r in range(2):
                    scores(0, 0, r)
                for side in range(2):
                    transposes(1, 1, side)
                in_tiles(pe, tile)

            @block.scalar
            def _(act):
                norm.scalar(act)
                act.sem_inc(s_tr, 1)
                act.sem_inc(s_E, 2)
                act.wait_ge(s_load, 16)
                nc.scalar.activation(vx[:, 0, :, :, 0:HD].rearrange("p t h d -> p (t h) d"),
                                     cx[:, :, :].rearrange("p t (h d) -> p (t h) d", d=HD), ACT.Copy).then_inc(s_vx, 1)
                act.wait_ge(s_mask, 1)
                nc.scalar.activation(mask[:, :, :], maskf[:, :, :], ACT.Copy).then_inc(s_vx, 1)
                act.wait_ge(s_set1, 2)

                def transposed(t, par, side):
                    act.wait_ge(s_S, 2 * t + 2)
                    act.wait_ge(s_T, 2 * t + side + 5)
                    nc.scalar.activation((qT, kT)[side][:, par, :, :], TQ[:, :, :], ACT.Copy).then_inc(s_tr, 1)

                def exponentials(t, r):
                    n = t * 2 + r
                    act.wait_ge(s_d, n + 3)
                    act.wait_ge(s_ET, n + 1)
                    nc.scalar.activation(E[:, r, :, :], d[:, r, :, :, :].rearrange("p a b c -> p (a b) c"), ACT.Exp,
                                         bias=lift[:, 0:1], scale=SCALE).then_inc(s_E, 1)

                def tile(t, par, ahead):
                    for r in range(2):
                        n = t * 2 + r
                        act.wait_ge(s_ET, n + 3)
                        act.wait_ge(s_V, n + 1)
                        nc.scalar.activation(eT[:, r, 0, :, :], ET[:, :, :], ACT.Copy).then_inc(s_eh, 1)
                    for r in range(2):
                        if ahead >= 1:
                            exponentials(t + 1, r)
                        if ahead == 2:
                            transposed(t + 2, par, r)

                for side in range(2):
                    transposed(0, 0, side)
                for r in range(2):
                    exponentials(0, r)
                for side in range(2):
                    transposed(1, 1, side)
                in_tiles(act, tile)

            @block.vector
            def _(dve):
                norm.vector(dve)
                norm.whole(dve)
                dve.sem_inc(s_d, 2)
                dve.sem_inc(s_res, 1)
                dve.wait_ge(s_set, 3)
                nc.vector.memset(lift[:, :], LIFT)
                nc.vector.memset(vx[:, 0, :, :, HD:HE], 1.0)
                nc.vector.memset(vx[:, 1, :, :, HD:HE], 0.0).then_inc(s_set1, 1)
                dve.wait_ge(s_vx, 1)
                nc.vector.tensor_tensor(vx[:, 1, :, :, 0:HD].rearrange("p t h d -> p (t h) d"),
                                        cx[:, :, :].rearrange("p t (h d) -> p (t h) d", d=HD),
                                        vx[:, 0, :, :, 0:HD].rearrange("p t h d -> p (t h) d"), ALU.subtract).then_inc(s_set1, 1)
                dve.sem_inc(s_el, 1)

                def stack(t, par):
                    q = sh.H[:, t, :].rearrange("p (h d) -> p h d", d=HD)
                    dve.wait_ge(s_T, 2 * t + 1)
                    for slot in (0, 1):
                        last = copy_indexed(nc, qs[:, par, :, slot * HD:(slot + 1) * HD], q)
                    last.then_inc(s_hi, 1)
                    dve.wait_ge(s_hi, t + 1)
                    nc.vector.tensor_tensor(qs[:, par, :, 2 * HD:3 * HD], q, qs[:, par, :, 0:HD], ALU.subtract).then_inc(s_qlo, 1)

                def output(t):
                    o = O[:, 0:NH * HE].rearrange("p (h d) -> p h d", d=HE)
                    dve.wait_ge(s_V, 2 * t + 4)
                    nc.vector.reciprocal(inv[:, :], o[:, :, HD]).then_inc(s_inv, 1)
                    dve.wait_ge(s_inv, t + 1)
                    nc.vector.tensor_tensor(on[:, :, :], o[:, :, 0:HD], inv[:, :].unsqueeze(2).to_broadcast([P, NH, HD]),
                                            ALU.mult).then_inc(s_on, 1)
                    dve.wait_ge(s_on, t + 1)
                    nc.vector.scalar_tensor_tensor(out=sh.X[:, t, :], in0=on[:, :, :].rearrange("p h d -> p (h d)"), scalar=gate,
                                                   in1=sh.X[:, t, :], op0=ALU.mult, op1=ALU.add).then_inc(s_res, 1)

                def differences(t, r):
                    n = t * 2 + r
                    dve.wait_ge(s_S, n + 5)
                    nc.vector.reduce_max(m[:, r, :, :], S[:, r, :, :, :], axis=AXX).then_inc(s_m, 1)
                    dve.wait_ge(s_m, n + 1)
                    dve.wait_ge(s_E, n + 1)
                    nc.vector.tensor_tensor(d[:, r, :, :, :], S[:, r, :, :, :], m[:, r, :, :].unsqueeze(3).to_broadcast([P, 2, 4, P]),
                                            ALU.subtract).then_inc(s_d, 1)

                def tile(t, par, ahead):
                    if ahead == 2:
                        stack(t + 2, par)
                    for r in range(2):
                        dve.wait_ge(s_eh, t * 2 + r + 1)
                        nc.vector.tensor_tensor(eT[:, r, 1, :, :], ET[:, :, :], eT[:, r, 0, :, :], ALU.subtract).then_inc(s_el, 1)
                        if ahead >= 1:
                            differences(t + 1, r)
                    output(t)

                stack(0, 0)
                differences(0, 0)
                differences(0, 1)
                stack(1, 1)
                in_tiles(dve, tile)


def ternary_ffn(nc, sh, a, gate, out):
    F = 1024
    NF = F // P
    with ExitStack() as ctx:
        def sb(n, shape, dt=F32, where=ctx):
            return where.enter_context(nc.sbuf_tensor("tf_" + n, shape, dt))

        def sem(n):
            return nc.alloc_semaphore(name="tf_" + n)

        w1 = sb("w1", [P, KT, F], F16)
        w2 = sb("w2", [P, NF, D], F16)
        s1b = sb("s1b", [P, F])
        s2b = sb("s2b", [P, D])
        inv1 = sb("inv1", [P, NB])
        ints = sb("ints", [P, NB, D], F16)
        with ExitStack() as inner:
            f1 = sb("f1", [P, KT, F], F32, inner)
            f2 = sb("f2", [P, NF, D], F32, inner)
            Z = sb("Z", [P, NB, D], F32, inner)
            ab = sb("ab", [P, KT * F], F32, inner)
            ab2 = sb("ab2", [P, NF * D], F32, inner)
            r1 = sb("r1", [P, F], F32, inner)
            r2 = sb("r2", [P, D], F32, inner)
            am = sb("am", [P, NB], F32, inner)
            ra = sb("ra", [P, NB], F32, inner)
            ones = sb("ones", [P, P], F32, inner)
            M1 = inner.enter_context(nc.psum_tensor("tf_M1", [P, F], F32))
            M2 = inner.enter_context(nc.psum_tensor("tf_M2", [P, 512], F32))
            s_load, s_abs, s_ones, s_mean, s_c = map(sem, ("load", "abs", "ones", "mean", "chain"))
            norm = Layernorm(nc, inner, sh, "tf_ln")
            s_ints = sem("ints")
            turned = TokensTransposed(nc, inner, sh, "tf_T", ints, s_ints)
            with nc.Block() as block:
                @block.sync
                def _(sp):
                    sp.dma_start(f1[:, :, :].rearrange("p k n -> p (k n)"), a["tf_w1"]).then_inc(s_load, 16)
                    sp.dma_start(f2[:, :, :].rearrange("p k n -> p (k n)"), a["tf_w2"]).then_inc(s_load, 16)

                @block.scalar
                def _(act):
                    norm.scalar(act)
                    act.wait_ge(s_load, 32)
                    nc.scalar.activation(ab[:, :], f1[:, :, :].rearrange("p k n -> p (k n)"), ACT.Abs).then_inc(s_abs, 1)
                    nc.scalar.activation(ab2[:, :], f2[:, :, :].rearrange("p k n -> p (k n)"), ACT.Abs).then_inc(s_abs, 1)
                    turned.scalar(act)

                @block.tensor
                def _(pe):
                    pe.wait_ge(s_ones, 1)
                    pe.wait_ge(s_abs, 2)
                    for half in range(2):
                        for k in range(KT):
                            nc.tensor.matmul(M1[:, half * 512:(half + 1) * 512], ones[:, :],
                                             ab[:, k * F + half * 512:k * F + (half + 1) * 512], start=k == 0, stop=k == KT - 1)
                    for k in range(NF):
                        last = nc.tensor.matmul(M2[:, 0:D], ones[:, :], ab2[:, k * D:(k + 1) * D], start=k == 0, stop=k == NF - 1)
                    last.then_inc(s_mean, 1)
                    turned.tensor(pe)

                @block.vector
                def _(dve):
                    chained = chain_on(dve, s_c)
                    nc.vector.memset(ones[:, :], 1.0).then_inc(s_ones, 1)
                    norm.vector(dve)
                    norm.whole(dve)
                    chained(nc.vector.tensor_reduce(out=am[:, :], in_=sh.H[:, :, :], axis=AXX, op=ALU.max, apply_absolute_value=True))
                    chained(nc.vector.tensor_scalar(inv1[:, :], am[:, :], 1e-5, 1.0 / 127.0, ALU.max, ALU.mult))
                    chained(nc.vector.reciprocal(ra[:, :], inv1[:, :]))
                    chained(nc.vector.tensor_tensor(Z[:, :, :], sh.H[:, :, :], ra[:, :].unsqueeze(2).to_broadcast([P, NB, D]), ALU.mult))
                    chained(nc.vector.tensor_scalar(Z[:, :, :], Z[:, :, :], MAGIC, MAGIC, ALU.add, ALU.subtract))
                    nc.vector.tensor_scalar(ints[:, :, :], Z[:, :, :], 127.0, -128.0, ALU.min, ALU.max).then_inc(s_ints, 1)
                    dve.wait_ge(s_mean, 1)
                    for M, s, r, f, w, n in ((M1[:, :], s1b, r1, f1, w1, KT), (M2[:, 0:D], s2b, r2, f2, w2, NF)):
                        width = [P, n, s.shape[1]]
                        chained(nc.vector.tensor_scalar(s[:, :], M, 1.0 / (n * P), 1e-5, ALU.mult, ALU.max))
                        chained(nc.vector.reciprocal(r[:, :], s[:, :]))
                        chained(nc.vector.tensor_tensor(f[:, :, :], f[:, :, :], r[:, :].unsqueeze(1).to_broadcast(width), ALU.mult))
                        chained(nc.vector.tensor_scalar(f[:, :, :], f[:, :, :], MAGIC, MAGIC, ALU.add, ALU.subtract))
                        nc.vector.tensor_scalar(w[:, :, :], f[:, :, :], 1.0, -1.0, ALU.min, ALU.max)

        h = sb("h", [P, 2, F])
        g = sb("g", [P, 2, F])
        z = sb("z", [P, 2, F])
        gi = sb("gi", [P, 2, F], F16)
        gT = sb("gT", [P, 2, NF, P], F16)
        am2 = sb("am2", [P, 2])
        inv2 = sb("inv2", [P, 2])
        ra2 = sb("ra2", [P, 2])
        ga2 = sb("ga2", [P, 2])
        tmp = sb("tmp", [P, 2, D])
        Hp = ctx.enter_context(nc.psum_tensor("tf_H", [P, 2, F], F32))
        TP = ctx.enter_context(nc.psum_tensor("tf_TP", [P, 2, NF, P], F16))
        O = ctx.enter_context(nc.psum_tensor("tf_O", [P, 2, 512], F32))
        s_H, s_h, s_g, s_c, s_gi, s_T, s_gT, s_O, s_tmp, s_res = map(sem, ("H", "h", "g", "chain2", "gi", "T", "gT", "O", "tmp", "res"))

        def in_pairs(eng, hidden, rest):
            hidden(0)
            with eng.Fori(0, NB // 2 - 1) as p:
                rest(p, True)
            rest(NB // 2 - 1, False)

        s_out = sem("out")
        with nc.Block() as block:
            @block.sync
            def _(sp):
                with sp.Fori(0, NB // 4) as four:
                    sp.wait_ge(s_res, four * 4 + 4 + 2)
                    sp.dma_start(out[bass.ds(four * 4, 4), :, :].rearrange("b p d -> p b d"), sh.X[:, bass.ds(four * 4, 4), :]).then_inc(s_out, 16)
                sp.wait_ge(s_out, 16 * (NB // 4))

            @block.tensor
            def _(pe):
                pe.sem_inc(s_T, 2)
                pe.sem_inc(s_O, 2)

                def hidden(p):
                    for par in range(2):
                        t = p * 2 + par
                        pe.wait_ge(s_h, t + 1)
                        for half in range(2):
                            for k in range(KT):
                                last = nc.tensor.matmul(Hp[:, par, half * 512:(half + 1) * 512], sh.hT[:, 0, k, bass.ds(t * P, P)],
                                                        w1[:, k, half * 512:(half + 1) * 512], start=k == 0, stop=k == KT - 1)
                        last.then_inc(s_H, 1)

                def down(t, par):
                    pe.wait_ge(s_gi, t + 3)
                    pe.wait_ge(s_gT, t + 1)
                    for f in range(NF):
                        last = nc.tensor.transpose(TP[:, par, f, :], gi[:, par, f * P:(f + 1) * P], sh.identh[:, :])
                    last.then_inc(s_T, 1)
                    pe.wait_ge(s_gT, t + 3)
                    pe.wait_ge(s_res, t + 1)
                    for f in range(NF):
                        last = nc.tensor.matmul(O[:, par, 0:D], gT[:, par, f, :], w2[:, f, :], start=f == 0, stop=f == NF - 1)
                    last.then_inc(s_O, 1)

                def rest(p, ahead):
                    if ahead:
                        hidden(p + 1)
                    down(p * 2, 0)
                    down(p * 2 + 1, 1)

                in_pairs(pe, hidden, rest)

            @block.scalar
            def _(act):
                act.sem_inc(s_gT, 2)

                def hidden(p):
                    for par in range(2):
                        t = p * 2 + par
                        act.wait_ge(s_h, t + 3)
                        act.wait_ge(s_gi, t + 1)
                        nc.scalar.activation(g[:, par, :], h[:, par, :], ACT.Gelu_apprx_tanh).then_inc(s_g, 1)

                def rest(p, ahead):
                    for par in range(2):
                        t = p * 2 + par
                        act.wait_ge(s_T, t + 3)
                        act.wait_ge(s_O, t + 1)
                        nc.scalar.activation(gT[:, par, :, :], TP[:, par, :, :], ACT.Copy).then_inc(s_gT, 1)
                    if ahead:
                        hidden(p + 1)

                in_pairs(act, hidden, rest)

            @block.vector
            def _(dve):
                dve.sem_inc(s_h, 2)
                dve.sem_inc(s_gi, 2)
                dve.sem_inc(s_res, 2)

                def hidden(p):
                    for par in range(2):
                        t = p * 2 + par
                        dve.wait_ge(s_H, t + 1)
                        nc.vector.scalar_tensor_tensor(out=h[:, par, :], in0=Hp[:, par, :], scalar=inv1[:, bass.ds(t, 1)],
                                                       in1=s1b[:, :], op0=ALU.mult, op1=ALU.mult).then_inc(s_h, 1)

                def integers(t, par):
                    i = slice(par, par + 1)
                    steps = iter(range(1, 9))

                    def chained(ins):
                        ins.then_inc(s_c, 1)
                        dve.wait_ge(s_c, t * 5 + next(steps))

                    dve.wait_ge(s_g, t + 1)
                    chained(nc.vector.tensor_reduce(out=am2[:, i], in_=g[:, par, :], axis=AXX, op=ALU.max, apply_absolute_value=True))
                    chained(nc.vector.tensor_scalar(inv2[:, i], am2[:, i], 1e-5, 1.0 / 127.0, ALU.max, ALU.mult))
                    nc.vector.tensor_tensor(ga2[:, i], inv2[:, i], gate, ALU.mult)
                    chained(nc.vector.reciprocal(ra2[:, i], inv2[:, i]))
                    chained(nc.vector.tensor_scalar(z[:, par, :], g[:, par, :], ra2[:, i], MAGIC, ALU.mult, ALU.add))
                    chained(nc.vector.tensor_scalar(z[:, par, :], z[:, par, :], MAGIC, 127.0, ALU.subtract, ALU.min))
                    dve.wait_ge(s_T, t + 1)
                    nc.vector.tensor_scalar(gi[:, par, :], z[:, par, :], -128.0, None, ALU.max).then_inc(s_gi, 1)

                def rest(p, ahead):
                    for par in range(2):
                        integers(p * 2 + par, par)
                    if ahead:
                        hidden(p + 1)
                    for par in range(2):
                        t = p * 2 + par
                        dve.wait_ge(s_O, t + 3)
                        nc.vector.scalar_tensor_tensor(out=tmp[:, par, :], in0=O[:, par, 0:D], scalar=ga2[:, par:par + 1],
                                                       in1=s2b[:, :], op0=ALU.mult, op1=ALU.mult).then_inc(s_tmp, 1)
                        dve.wait_ge(s_tmp, t + 1)
                        nc.vector.tensor_tensor(sh.X[:, t, :], sh.X[:, t, :], tmp[:, par, :], ALU.add).then_inc(s_res, 1)

                in_pairs(dve, hidden, rest)


@contextmanager
def own_semaphores(nc):
    before = nc.snapshot_sems()
    yield
    nc.clear_and_free_semaphores(nc.allocated_since(before))
    nc.all_engine_barrier()


def program(nc, a, out):
    with ExitStack() as ctx:
        sh = make_shared(nc, ctx, a["x"], a["g_xattn"], a["g_ffn"])
        with own_semaphores(nc):
            long_convolution(nc, sh, a["ctx_flip"], a["ctxT_flip"], a["ssm_pad"], a["ssm_D"])
        sh.hT = ctx.enter_context(nc.sbuf_tensor("hT", [P, 2, KT, T], F16))
        weights_T = nc.dram_tensor("weights_T", [MOE1.rows, T], F32, kind="Internal").ap()

        def mixture(m, layer):
            with ExitStack() as wide:
                load = ExpertWeights(nc, wide, sh, m, a[f"moe{layer}_w"], f"moe{layer}_W")
                with ExitStack() as head:
                    norm = Layernorm(nc, head, sh, f"moe{layer}_ln")
                    hT = Transposed(nc, head, sh, f"moe{layer}_hT", norm)
                    route(nc, sh, m, hT, load, a[f"moe{layer}_router"], weights_T[0:m.rows, :], f"moe{layer}_route")
                experts(nc, sh, m, load, weights_T, sh.gates[:, 2 * layer + 1:2 * layer + 2], f"moe{layer}")

        with own_semaphores(nc):
            mixture(MOE0, 0)
        with own_semaphores(nc):
            rms_attention(nc, sh, a["ctxT"], {x: a["rms_w" + x] for x in "qkv"}, sh.gates[:, 2:3])
        with own_semaphores(nc):
            mixture(MOE1, 1)
        with own_semaphores(nc):
            quantised_attention(nc, sh, a, sh.gates[:, 4:5])
        with own_semaphores(nc):
            quantised_ffn(nc, sh, a, sh.gates[:, 5:6])
        with own_semaphores(nc):
            causal_attention(nc, sh, a, sh.gates[:, 6:7])
        with own_semaphores(nc):
            ternary_ffn(nc, sh, a, sh.gates[:, 7:8], out)


def stationary(w):
    return w.T.reshape(-1, P, w.shape[0]).transpose(1, 0, 2).reshape(P, -1)


def by_tile(gate, up, down):
    F = down.shape[0] // P
    cols = [w.reshape(KT, P, F, P).transpose(1, 2, 0, 3).reshape(P, F, KT * P) for w in (gate, up)]
    cols.append(down.reshape(F, P, D).transpose(1, 0, 2))
    return np.concatenate(cols, axis=2).reshape(P, F * TW)


def expert_layouts(n):
    gu = n["L0_ffn_gate_up_proj"]
    I = gu.shape[1] // 2
    none = np.zeros((P - I, D), gu.dtype)
    gate0 = np.concatenate([gu[:, :I].reshape(-1, D), n["L0_ffn_shared_gate_w"], none]).T
    up0 = np.concatenate([gu[:, I:].reshape(-1, D), n["L0_ffn_shared_up_w"], none]).T
    down0 = np.concatenate([n["L0_ffn_down_proj"].transpose(0, 2, 1).reshape(-1, D), n["L0_ffn_shared_down_w"].T, none])
    router0 = np.concatenate([n["L0_ffn_router_w"], n["L0_ffn_shared_expert_gate_w"]]).T
    w1 = n["L1_ffn_w1"]
    F = w1.shape[2] // 2
    gate1 = np.concatenate([w1[:, :, :F].transpose(1, 0, 2).reshape(D, -1), n["L1_ffn_w_gate"]], axis=1)
    up1 = np.concatenate([w1[:, :, F:].transpose(1, 0, 2).reshape(D, -1), n["L1_ffn_w_up"]], axis=1)
    down1 = np.concatenate([n["L1_ffn_w2"].reshape(-1, D), n["L1_ffn_w_down"]])
    return {
        "moe0_w": by_tile(gate0, up0, down0), "moe0_router": router0.reshape(KT, P, -1).transpose(1, 0, 2),
        "moe1_w": by_tile(gate1, up1, down1), "moe1_router": n["L1_ffn_router_w"].reshape(KT, P, -1).transpose(1, 0, 2),
    }


def kernel(**inputs):
    import concourse.bacc as bacc
    from concourse.bass_utils import run_bass_kernel_spmd

    n = {k: np.asarray(v) for k, v in inputs.items()}
    c = n["ctx_2048"]
    ssm = n["L0_xattn_ssm_kernel"]
    arrays = {
        "x": n["x"], "g_xattn": n["g_xattn"], "g_ffn": n["g_ffn"],
        "ctx_flip": c.reshape(NB, P, KT, P)[:, :, :, ::-1].reshape(NB, P, D),
        "ctxT_flip": c.reshape(NB, P, KT, P)[:, :, :, ::-1].transpose(3, 0, 2, 1),
        "ssm_pad": np.concatenate([np.zeros((16, P - 1), ssm.dtype), ssm], axis=1),
        "ssm_D": n["L0_xattn_D"],
    }
    arrays |= expert_layouts(n)
    kv = np.concatenate([n["L1_xattn_Wk"], n["L1_xattn_Wv"]])
    arrays |= {
        "ctxT": stationary(c.reshape(T, D)),
        "rms_wq": stationary(n["L1_xattn_Wq"]), "rms_wk": stationary(kv[0::2]), "rms_wv": stationary(kv[1::2]),
    }
    wkv, bkv = n["L2_xattn_Wkv"], n["L2_xattn_bkv"]
    arrays |= {
        "qa_wq": stationary(n["L2_xattn_Wq"].T), "qa_wk": stationary(wkv[:, :D].T), "qa_wv": stationary(wkv[:, D:].T),
        "qa_wp": stationary(n["L2_xattn_Wp"].T), "qa_bq": n["L2_xattn_bq"], "qa_bk": bkv[:D],
        "qa_bv": bkv[D:].reshape(KT, P).T, "qa_bp": n["L2_xattn_bp"],
    }
    arrays |= {
        "qf_w1": stationary(n["L2_ffn_W1"]), "qf_w2": stationary(n["L2_ffn_W2"]),
        "qf_b1": n["L2_ffn_b1"].reshape(-1, P).T, "qf_b2": n["L2_ffn_b2"], "qf_s1": n["L2_ffn_s_act1"], "qf_s2": n["L2_ffn_s_act2"],
        "ctx": c, "tf_w1": stationary(n["L3_ffn_w1"]), "tf_w2": stationary(n["L3_ffn_w2"]),
    }
    arrays = {f"in_{k}": np.ascontiguousarray(v) for k, v in arrays.items()}
    nc = bacc.Bacc("TRN2", target_bir_lowering=False, num_devices=1)
    args = {k[3:]: nc.dram_tensor(k, v.shape, mybir.dt.from_np(v.dtype), kind="ExternalInput").ap() for k, v in arrays.items()}
    out = nc.dram_tensor("out_0_dram", (NB, P, D), F32, kind="ExternalOutput").ap()
    program(nc, args, out)
    r = run_bass_kernel_spmd(nc, [arrays], core_ids=[0])
    return r.results[0]["out_0_dram"]
```
